# Optimizing a Trainium2 kernel written in Bass

```python
import numpy as np
import jax
import jax.numpy as jnp

def _softmax(x, axis=-1):
    return jax.nn.softmax(x, axis=axis)

def _gelu(x):
    return jax.nn.gelu(x, approximate=True)

def _silu(x):
    return jax.nn.silu(x)

def _sigmoid(x):
    return jax.nn.sigmoid(x)

def _layernorm(x, axis=-1, eps=1e-05):
    m = jnp.mean(x, axis=axis, keepdims=True)
    v = jnp.var(x, axis=axis, keepdims=True)
    return (x - m) / jnp.sqrt(v + eps)

def _scatter_add(tgt, idx, src, axis=0):
    return tgt.at[idx].add(src)

def _segment_sum(src, seg, n):
    return jax.ops.segment_sum(src, seg, n)
kernel_name = 'mk_gnn_ffn_d2_gnn_r32_d3ac1d'

def setup_inputs(seed: int=0):
    np.random.seed(seed)
    _w = jnp.asarray

    def _rec_inputs():
        import jax
        import jax.numpy as jnp
        _gk = jax.random.key(seed)
        x = -0.0003713 + 1 * jax.random.normal(jax.random.fold_in(_gk, 1), (3125, 256), jnp.float32)
        src = jax.random.randint(jax.random.fold_in(_gk, 2), (50000,), 0, 3125, jnp.int32)
        dst = jnp.minimum((3125 * jax.random.uniform(jax.random.fold_in(_gk, 3), (50000,)) ** 2.0).astype(jnp.int32), 99999)
        _o = jnp.argsort(dst, stable=True)
        src = src[_o]
        dst = dst[_o]
        return (x, src, dst)
    x, src, dst = _rec_inputs()

    def _L0_gnn_setup():
        import jax, jax.numpy as jnp
        import numpy as np
        N_NODES = 50000
        N_EDGES = 25000
        IN_FEATS = 256
        N_HIDDEN = 256

        def _degree_norms(src, dst, n_nodes):
            ones = jnp.ones(src.shape, jnp.float32)
            out_deg = jax.ops.segment_sum(ones, src, num_segments=n_nodes)
            in_deg = jax.ops.segment_sum(ones, dst, num_segments=n_nodes)
            norm_src = jax.lax.rsqrt(jnp.maximum(out_deg, 1.0))
            norm_dst = jax.lax.rsqrt(jnp.maximum(in_deg, 1.0))
            return (norm_src, norm_dst)

        def _graph_conv(h, W, b, src, dst, norm_src, norm_dst, activation):
            h = h * norm_src[:, None] @ W
            msg = h[src]
            agg = jax.ops.segment_sum(msg, dst, num_segments=h.shape[0])
            out = agg * norm_dst[:, None] + b
            if activation:
                out = jax.nn.relu(out)
            return out
        key = jax.random.key(seed)
        ks = jax.random.split(key, 8)
        scale_in = 1.0 / np.sqrt(IN_FEATS)
        scale_h = 1.0 / np.sqrt(N_HIDDEN)
        return {'features': jax.random.normal(ks[0], (N_NODES, IN_FEATS), jnp.float32), 'W0': jax.random.normal(ks[1], (IN_FEATS, N_HIDDEN), jnp.float32) * scale_in, 'b0': jnp.zeros((N_HIDDEN,), jnp.float32), 'W1': jax.random.normal(ks[2], (N_HIDDEN, N_HIDDEN), jnp.float32) * scale_h, 'b1': jnp.zeros((N_HIDDEN,), jnp.float32), 'W2': jax.random.normal(ks[3], (N_HIDDEN, N_HIDDEN), jnp.float32) * scale_h, 'b2': jnp.zeros((N_HIDDEN,), jnp.float32), 'src': jax.random.randint(ks[4], (N_EDGES,), 0, N_NODES, jnp.int32), 'dst': jax.random.randint(ks[5], (N_EDGES,), 0, N_NODES, jnp.int32)}
    _L0_gnn_all = _L0_gnn_setup()
    _L0_gnn_in = {k: v for k, v in _L0_gnn_all.items() if k in ('W0', 'b0', 'W1', 'b1', 'W2', 'b2')}
    del _L0_gnn_all

    def _L0_ffn_setup():
        import jax, jax.numpy as jnp
        import numpy as np
        B, S, H, F, E, K = (8, 128, 256, 512, 16, 2)
        EPS = 1e-05
        key = jax.random.key(seed)
        ks = jax.random.split(key, 9)
        sc = 0.02
        return {'x': jax.random.normal(ks[0], (B, S, H), dtype=jnp.float32), 'gate_w': jax.random.normal(ks[1], (H, E), dtype=jnp.float32) * sc, 'gate_b': jnp.zeros((E,), dtype=jnp.float32), 'w1': jax.random.normal(ks[2], (E, H, F), dtype=jnp.float32) * sc, 'b1': jnp.zeros((E, F), dtype=jnp.float32), 'w2': jax.random.normal(ks[3], (E, F, H), dtype=jnp.float32) * sc, 'b2': jnp.zeros((E, H), dtype=jnp.float32), 'gamma': jnp.ones((H,), dtype=jnp.float32), 'beta': jnp.zeros((H,), dtype=jnp.float32)}
    _L0_ffn_all = _L0_ffn_setup()
    _L0_ffn_in = {k: v for k, v in _L0_ffn_all.items() if k in ('gate_w', 'gate_b', 'w1', 'b1', 'w2', 'b2', 'gamma', 'beta')}
    del _L0_ffn_all

    def _L1_gnn_setup():
        import jax, jax.numpy as jnp
        import numpy as np
        N_NODES = 50000
        N_EDGES = 50000
        IN_DIM, OUT_DIM, N_HEADS = (256, 64, 4)
        EPS = 1e-12
        key = jax.random.key(seed)
        k1, k2, k3, k4, k5 = jax.random.split(key, 5)
        h = jax.random.normal(k1, (N_NODES, IN_DIM), dtype=jnp.float32)
        edge_index = jax.random.randint(k2, (2, N_EDGES), 0, N_NODES, dtype=jnp.int32)
        W = jax.random.normal(k3, (IN_DIM, OUT_DIM), dtype=jnp.float32) * 0.05
        Wl = jax.random.normal(k4, (N_HEADS, OUT_DIM), dtype=jnp.float32) * 0.05
        Wr = jax.random.normal(k5, (N_HEADS, OUT_DIM), dtype=jnp.float32) * 0.05
        b = jnp.zeros((OUT_DIM,), dtype=jnp.float32)
        return {'h': h, 'W': W, 'Wl': Wl, 'Wr': Wr, 'b': b, 'edge_index': edge_index}
    _L1_gnn_all = _L1_gnn_setup()
    _L1_gnn_in = {k: v for k, v in _L1_gnn_all.items() if k in ('W', 'Wl', 'Wr', 'b')}
    del _L1_gnn_all

    def _L1_ffn_setup():
        import jax, jax.numpy as jnp
        import numpy as np
        B, T, D, H, E = (16, 128, 256, 512, 8)
        key = jax.random.key(seed)
        ks = jax.random.split(key, 5)
        x = jax.random.normal(ks[0], (B, T, D), dtype=jnp.float32)
        gate_w = jax.random.normal(ks[1], (D, E), dtype=jnp.float32) * 0.02
        gate_b = jnp.zeros((E,), dtype=jnp.float32)
        W1 = jax.random.normal(ks[2], (E, D, H), dtype=jnp.float32) * 0.02
        b1 = jnp.zeros((E, H), dtype=jnp.float32)
        W2 = jax.random.normal(ks[3], (E, H, D), dtype=jnp.float32) * 0.02
        b2 = jnp.zeros((E, D), dtype=jnp.float32)
        return {'x': x, 'gate_w': gate_w, 'gate_b': gate_b, 'W1': W1, 'b1': b1, 'W2': W2, 'b2': b2}
    _L1_ffn_all = _L1_ffn_setup()
    _L1_ffn_in = {k: v for k, v in _L1_ffn_all.items() if k in ('gate_w', 'gate_b', 'W1', 'b1', 'W2', 'b2')}
    del _L1_ffn_all
    return {'x': x, 'src': src, 'dst': dst, 'L0_gnn_W0': _L0_gnn_in['W0'], 'L0_gnn_b0': _L0_gnn_in['b0'], 'L0_gnn_W1': _L0_gnn_in['W1'], 'L0_gnn_b1': _L0_gnn_in['b1'], 'L0_gnn_W2': _L0_gnn_in['W2'], 'L0_gnn_b2': _L0_gnn_in['b2'], 'L0_ffn_gate_w': _L0_ffn_in['gate_w'], 'L0_ffn_gate_b': _L0_ffn_in['gate_b'], 'L0_ffn_w1': _L0_ffn_in['w1'], 'L0_ffn_b1': _L0_ffn_in['b1'], 'L0_ffn_w2': _L0_ffn_in['w2'], 'L0_ffn_b2': _L0_ffn_in['b2'], 'L0_ffn_gamma': _L0_ffn_in['gamma'], 'L0_ffn_beta': _L0_ffn_in['beta'], 'L1_gnn_W': _L1_gnn_in['W'], 'L1_gnn_Wl': _L1_gnn_in['Wl'], 'L1_gnn_Wr': _L1_gnn_in['Wr'], 'L1_gnn_b': _L1_gnn_in['b'], 'L1_ffn_gate_w': _L1_ffn_in['gate_w'], 'L1_ffn_gate_b': _L1_ffn_in['gate_b'], 'L1_ffn_W1': _L1_ffn_in['W1'], 'L1_ffn_b1': _L1_ffn_in['b1'], 'L1_ffn_W2': _L1_ffn_in['W2'], 'L1_ffn_b2': _L1_ffn_in['b2']}

def reference(x, src, dst, L0_gnn_W0, L0_gnn_b0, L0_gnn_W1, L0_gnn_b1, L0_gnn_W2, L0_gnn_b2, L0_ffn_gate_w, L0_ffn_gate_b, L0_ffn_w1, L0_ffn_b1, L0_ffn_w2, L0_ffn_b2, L0_ffn_gamma, L0_ffn_beta, L1_gnn_W, L1_gnn_Wl, L1_gnn_Wr, L1_gnn_b, L1_ffn_gate_w, L1_ffn_gate_b, L1_ffn_W1, L1_ffn_b1, L1_ffn_W2, L1_ffn_b2):
    import jax
    import jax.numpy as jnp

    def _L0_gnn_ref(features, W0, b0, W1, b1, W2, b2, src, dst):
        import jax, jax.numpy as jnp
        import numpy as np
        N_NODES = 50000
        N_EDGES = 25000
        IN_FEATS = 256
        N_HIDDEN = 256

        def _degree_norms(src, dst, n_nodes):
            ones = jnp.ones(src.shape, jnp.float32)
            out_deg = jax.ops.segment_sum(ones, src, num_segments=n_nodes)
            in_deg = jax.ops.segment_sum(ones, dst, num_segments=n_nodes)
            norm_src = jax.lax.rsqrt(jnp.maximum(out_deg, 1.0))
            norm_dst = jax.lax.rsqrt(jnp.maximum(in_deg, 1.0))
            return (norm_src, norm_dst)

        def _graph_conv(h, W, b, src, dst, norm_src, norm_dst, activation):
            h = h * norm_src[:, None] @ W
            msg = h[src]
            agg = jax.ops.segment_sum(msg, dst, num_segments=h.shape[0])
            out = agg * norm_dst[:, None] + b
            if activation:
                out = jax.nn.relu(out)
            return out
        n = features.shape[0]
        norm_src, norm_dst = _degree_norms(src, dst, n)
        h = _graph_conv(features, W0, b0, src, dst, norm_src, norm_dst, True)
        h = _graph_conv(h, W1, b1, src, dst, norm_src, norm_dst, True)
        h = _graph_conv(h, W2, b2, src, dst, norm_src, norm_dst, False)
        return h

    def _L0_ffn_ref(x, gate_w, gate_b, w1, b1, w2, b2, gamma, beta):
        import jax, jax.numpy as jnp
        import numpy as np
        B, S, H, F, E, K = (8, 128, 256, 512, 16, 2)
        EPS = 1e-05
        gate_logits = x @ gate_w + gate_b
        topk_vals, topk_idx = jax.lax.top_k(gate_logits, K)
        topk_w = jax.nn.softmax(topk_vals, axis=-1)
        h = jax.nn.relu(jnp.einsum('bsh,ehf->bsef', x, w1) + b1)
        expert_out = jnp.einsum('bsef,efh->bseh', h, w2) + b2
        sel = jnp.take_along_axis(expert_out, topk_idx[:, :, :, None], axis=2)
        moe = jnp.sum(topk_w[..., None] * sel, axis=2)
        y = x + moe
        mu = jnp.mean(y, axis=-1, keepdims=True)
        var = jnp.var(y, axis=-1, keepdims=True)
        return (y - mu) / jnp.sqrt(var + EPS) * gamma + beta

    def _L1_gnn_ref(h, W, Wl, Wr, b, edge_index):
        import jax, jax.numpy as jnp
        import numpy as np
        N_NODES = 50000
        N_EDGES = 50000
        IN_DIM, OUT_DIM, N_HEADS = (256, 64, 4)
        EPS = 1e-12
        N = h.shape[0]
        H = Wl.shape[0]
        x = h @ W
        el = x @ Wl.T
        er = x @ Wr.T
        src, dst = (edge_index[0], edge_index[1])
        e = el[src] + er[dst]
        e = jnp.exp(jax.nn.leaky_relu(e, negative_slope=0.2))
        rowsum = jax.ops.segment_sum(e, src, num_segments=N)
        w = e / jnp.maximum(rowsum, EPS)[src]
        heads = [jax.ops.segment_sum(w[:, hd:hd + 1] * x[dst], src, num_segments=N) for hd in range(H)]
        out = jnp.stack(heads, axis=1)
        out = jax.nn.elu(out + b)
        return out.reshape(N, H * x.shape[1])

    def _L1_ffn_ref(x, gate_w, gate_b, W1, b1, W2, b2):
        import jax, jax.numpy as jnp
        import numpy as np
        B, T, D, H, E = (16, 128, 256, 512, 8)
        Bb, Tt, Dd = x.shape
        Ee = gate_w.shape[1]
        xf = x.reshape(-1, Dd)
        N = xf.shape[0]
        logits = xf @ gate_w + gate_b
        probs = jax.nn.softmax(logits, axis=-1)
        top2_vals, top2_idx = jax.lax.top_k(probs, 2)
        cw = jnp.zeros((N, Ee), dtype=xf.dtype).at[jnp.arange(N)[:, None], top2_idx].add(top2_vals)

        def step(acc, params):
            w1, bb1, w2, bb2, we = params
            h = jax.nn.gelu(xf @ w1 + bb1, approximate=False)
            y = h @ w2 + bb2
            return (acc + we[:, None] * y, None)
        out, _ = jax.lax.scan(step, jnp.zeros_like(xf), (W1, b1, W2, b2, cw.T))
        return out.reshape(Bb, Tt, Dd)
    edge_index = jnp.stack([src, dst])
    x = x + _L0_gnn_ref(_layernorm(x, axis=-1), L0_gnn_W0, L0_gnn_b0, L0_gnn_W1, L0_gnn_b1, L0_gnn_W2, L0_gnn_b2, src, dst)
    x = x + _L0_ffn_ref(_layernorm(x, axis=-1)[None], L0_ffn_gate_w, L0_ffn_gate_b, L0_ffn_w1, L0_ffn_b1, L0_ffn_w2, L0_ffn_b2, L0_ffn_gamma, L0_ffn_beta)[0]
    x = x + _L1_gnn_ref(_layernorm(x, axis=-1), L1_gnn_W, L1_gnn_Wl, L1_gnn_Wr, L1_gnn_b, edge_index)
    x = x + _L1_ffn_ref(_layernorm(x, axis=-1)[None], L1_ffn_gate_w, L1_ffn_gate_b, L1_ffn_W1, L1_ffn_b1, L1_ffn_W2, L1_ffn_b2)[0]
    return x

_drawn_inputs = setup_inputs


def setup_inputs(seed=0):
    import zlib

    import numpy as np

    out = dict(_drawn_inputs(seed))
    spreads = {'L0_gnn_b0': (0.0, 0.1),
     'L0_gnn_b1': (0.0, 0.1),
     'L0_gnn_b2': (0.0, 0.1),
     'L0_ffn_gate_b': (0.0, 0.1),
     'L0_ffn_b1': (0.0, 0.7),
     'L0_ffn_b2': (0.0, 0.1),
     'L0_ffn_gamma': (1.0, 0.2),
     'L0_ffn_beta': (0.0, 0.1),
     'L1_gnn_b': (0.0, 0.1),
     'L1_ffn_gate_b': (0.0, 0.8),
     'L1_ffn_b1': (0.0, 0.8),
     'L1_ffn_b2': (0.0, 0.647)}
    factors = {'L0_gnn_W0': 5.729,
     'L1_gnn_Wl': 7.346,
     'L1_ffn_gate_w': 4.067,
     'L1_ffn_W1': 5.893,
     'L1_ffn_W2': 5.5}
    for name, (base, spread) in spreads.items():
        noise = np.random.default_rng([zlib.crc32(name.encode()), seed]).standard_normal(out[name].shape)
        drawn = base * np.exp(spread * noise) if base else spread * noise
        out[name] = jnp.asarray(drawn.astype(out[name].dtype))
    for name, factor in factors.items():
        out[name] = (out[name] * factor).astype(out[name].dtype)
    return out
```

```python
from contextlib import ExitStack

import concourse.bass as bass
from concourse import mybir

F32 = mybir.dt.float32
F16 = mybir.dt.float16
I32 = mybir.dt.int32
U32 = mybir.dt.uint32
ALU = mybir.AluOpType
ACT = mybir.ActivationFunctionType
AX = mybir.AxisListType

P = 128
D = 256
NODES = 3125
TILES = -(-NODES // P)
LAST = NODES - (TILES - 1) * P
EDGES = 50000
EP = 125
EM = EDGES // EP
EC = (EDGES + TILES * (P - 1)) // P + 1
EC = -(-EC // 16) * 16
FF = 512
E0, E1 = 16, 8
HEADS, HD = 4, 64
PM = 2 * TILES
RING = 5
GB = 8
EPS_LN = 1e-5
ROWSUM_EPS = 1e-12
GW = HD + 2 * HEADS
assert EP * EM == EDGES and TILES % RING == 0 and EM % RING == 0 and PM % RING == 0


def expert_chunks(experts):
    n = (2 * NODES + experts * (P - 1)) // P
    return -(-n // 8) * 8


C0, C1 = expert_chunks(E0), expert_chunks(E1)


class Chain:

    def __init__(self, eng, sem):
        self.eng, self.sem, self.n, self.term = eng, sem, 0, None

    def __call__(self, ins):
        self.n += 1
        ins.then_inc(self.sem, 1)
        self.eng.wait_ge(self.sem, self.n if self.term is None else self.term + self.n)

    def loop(self, count, per):
        start = self.n
        with self.eng.Fori(0, count) as i:
            self.term = i * per
            yield i
            assert self.n == start + per
            self.term = None
        self.n = start + count * per


def bank_free(r):
    return RING if r == 0 else r + 2 if r == 4 else r + 1


class Kit:
    pass


def allocate(nc, ctx):
    k = Kit()
    k.nc = nc
    k.spent = []

    def sb(name, shape, dt=F32):
        return ctx.enter_context(nc.sbuf_tensor(name, shape, dt))

    k.sb = sb
    k.ident = sb("ident", [P, P])
    k.ones = sb("ones", [P, P])
    k.before = sb("before", [P, P])
    k.upto = sb("upto", [P, P])
    k.iota1 = sb("iota1", [P, P])
    k.iota_f = sb("iota_f", [P, EC])
    k.iota_h = sb("iota_h", [P, EC], F16)
    k.zero_h = sb("zero_h", [P, P], F16)
    k.x = sb("x_sb", [P, TILES, D])
    k.src_slot = sb("src_slot", [P, EC], I32)
    k.src_local = sb("src_local", [P, EC])
    k.dst_slot = sb("dst_slot", [P, EC], I32)
    k.dst_local = sb("dst_local", [P, EC])
    k.win_dst = sb("win_dst", [1, EC], I32)
    k.win_src = sb("win_src", [1, EC], I32)
    k.deg_in = sb("deg_in", [P, TILES])
    k.deg_out = sb("deg_out", [P, TILES])
    k.mean = sb("mean", [P, TILES])
    k.rstd = sb("rstd", [P, TILES])
    k.big = sb("big", [P, E0 * 2048])
    k.ps = ctx.enter_context(nc.psum_tensor("ps", [P, 8, 512], F32))
    return k


def phase(k, name):
    ctx = ExitStack()

    def sem(n):
        k.spent.append(k.nc.alloc_semaphore(f"{name}_{n}"))
        return k.spent[-1]

    sb = lambda n, s, d=F32: ctx.enter_context(k.nc.sbuf_tensor(f"{name}_{n}", s, d))
    return ctx, sem, sb


def recycle(k):
    k.nc.clear_and_free_semaphores(k.spent)
    k.nc.all_engine_barrier()
    k.spent = []


def setup(k, x, src, dst, edge_src, edge_dst):
    nc = k.nc
    ctx, sem, sb = phase(k, "setup")
    with ctx:
        loaded, made, cleared = sem("loaded"), sem("made"), sem("cleared")
        block = ctx.enter_context(nc.Block())

        @block.sync
        def _(sp):
            sp.dma_start(edge_src[:], src.rearrange("(p m) -> p m", p=EP)).then_inc(loaded, 16)
            sp.dma_start(edge_dst[:], dst.rearrange("(p m) -> p m", p=EP)).then_inc(loaded, 16)
            sp.dma_start(k.x[:, 0:TILES - 1, :],
                         x[0:(TILES - 1) * P, :].rearrange("(t p) d -> p t d", p=P)).then_inc(loaded, 16)
            sp.wait_ge(cleared, 1)
            sp.dma_start(k.x[0:LAST, TILES - 1, :], x[(TILES - 1) * P:NODES, :]).then_inc(loaded, 16)
            sp.wait_ge(loaded, 64)

        @block.vector
        def _(dve):
            dve.memset(k.x[:, TILES - 1, :], 0.0).then_inc(cleared, 1)
            dve.memset(k.zero_h[:], 0.0)

        @block.gpsimd
        def _(pool):
            link = Chain(pool, made)
            link(pool.memset(k.ones[:], 1.0))
            link(pool.affine_select(out=k.ident[:], in_=k.ones[:], compare_op=ALU.is_equal, fill=0.0,
                                    base=0, pattern=[[-1, P]], channel_multiplier=1))
            link(pool.affine_select(out=k.before[:], in_=k.ones[:], compare_op=ALU.is_gt, fill=0.0,
                                    base=0, pattern=[[1, P]], channel_multiplier=-1))
            link(pool.affine_select(out=k.upto[:], in_=k.ones[:], compare_op=ALU.is_ge, fill=0.0,
                                    base=0, pattern=[[1, P]], channel_multiplier=-1))
            link(pool.iota(k.iota1[:], pattern=[[1, P]], base=1, channel_multiplier=0,
                           allow_small_or_imprecise_dtypes=True))
            link(pool.iota(k.iota_f[:], pattern=[[1, EC]], base=0, channel_multiplier=0,
                           allow_small_or_imprecise_dtypes=True))
            link(pool.iota(k.iota_h[:], pattern=[[1, EC]], base=0, channel_multiplier=0,
                           allow_small_or_imprecise_dtypes=True))


def sort_scratch(sb, m, room):
    s = Kit()

    def wide(name, dt=F32):
        if room is None:
            return sb(name, [P, m], dt)[:]
        wide.at += m
        part = room[:, wide.at - m:wide.at]
        return part if dt == F32 else part.bitcast(dt)

    wide.at = 0
    s.bucket, s.local1, s.mask, s.count, s.hit, s.acc = (wide(n) for n in ("bucket", "local1", "mask", "count", "hit", "acc"))
    s.zero, s.part_a, s.part_b, s.chunk, s.lane = (wide(n) for n in ("zero", "part_a", "part_b", "chunk", "lane"))
    s.int_a, s.int_b = wide("int_a", I32), wide("int_b", I32)
    s.cnt, s.pad, s.inc, s.base = (sb(n, [P, 32]) for n in ("cnt", "pad", "inc", "base"))
    s.pad_i = sb("pad_i", [P, 32], I32)
    s.tot_i, s.tot_f, s.ends = sb("tot_i", [32, 1], I32), sb("tot_f", [32, 1]), sb("ends", [32, 1])
    s.past = sb("past", [32, EC])
    s.low = sb("low", [P, EC], I32)
    s.lanes = sb("lanes", [P, RING, 2, P], F16)
    s.chunks = sb("chunks", [P, RING, EC], F16)
    s.hist_l = sb("hist_l", [P, RING, P], F16)
    s.hist_w = sb("hist_w", [P, RING, 32], F16)
    return s


def sort(k, name, np_, m, buckets, c, key, node, slot, local, owner, pos=None, degree=None, valid=None, room=None):
    nc, ps = k.nc, k.ps
    ctx, sem, sb = phase(k, name)
    with ctx:
        s = sort_scratch(sb, m, room)
        chain, counted, totals, tot_ready, ends_ready, past_ready, map_ready = (
            sem(n) for n in ("chain", "counted", "totals", "tot_ready", "ends_ready", "past_ready", "map_ready"))
        hot, used, placed = sem("hot"), sem("used"), sem("placed")
        block = ctx.enter_context(nc.Block())
        slot_a, slot_b, hist = ps[:, 0, 0:c], ps[:, 1, 0:c], ps[:, 2, 0:buckets]
        pre, tot, tot_t = ps[0:np_, 3, 0:buckets], ps[0:np_, 3, 64:64 + buckets], ps[0:buckets, 3, 128:129]
        ends, owner_ps = ps[0:buckets, 4, 0:1], ps[0:1, 5, 0:c]

        @block.vector
        def _(dve):
            link = Chain(dve, chain)
            q = slice(0, np_)
            link(dve.tensor_scalar(s.int_a[q, :], key, 7, None, ALU.logical_shift_right))
            link(dve.tensor_copy(s.bucket[q, :], s.int_a[q, :]))
            link(dve.tensor_scalar(s.int_b[q, :], key, 127, None, ALU.bitwise_and))
            link(dve.tensor_scalar(s.local1[q, :], s.int_b[q, :], 1.0, None, ALU.add))
            if valid is not None:
                link(dve.scalar_tensor_tensor(s.bucket[q, :], s.bucket[q, :], 1.0, valid, ALU.add, ALU.mult))
                link(dve.tensor_scalar(s.bucket[q, :], s.bucket[q, :], -1.0, None, ALU.add))
            link(dve.tensor_scalar(s.int_a[q, :], node, 2, None, ALU.logical_shift_right))
            link(dve.tensor_copy(s.part_a[q, :], s.int_a[q, :]))
            link(dve.tensor_scalar(s.int_b[q, :], node, 3, 8, ALU.bitwise_and, ALU.logical_shift_left))
            link(dve.tensor_tensor(s.part_b[q, :], s.int_b[q, :], s.local1[q, :], ALU.add))
            link(dve.memset(s.zero[q, :], 0.0))
            link(dve.memset(s.acc[q, :], 0.0))
            for b in link.loop(buckets, 1):
                link(dve.tensor_scalar(s.mask[q, :], s.bucket[q, :], k.iota_f[q, bass.ds(b, 1)], 0.0,
                                       ALU.is_equal, ALU.add, accum_out=s.cnt[q, bass.ds(b, 1)]))
            dve.sem_inc(counted, 1)
            dve.wait_ge(totals, 1)
            link(dve.tensor_scalar(s.pad_i[q, 0:buckets], tot, 127.0, None, ALU.add))
            link(dve.tensor_scalar(s.pad_i[q, 0:buckets], s.pad_i[q, 0:buckets], 7, 7,
                                   ALU.logical_shift_right, ALU.logical_shift_left))
            link(dve.tensor_copy(s.pad[q, 0:buckets], s.pad_i[q, 0:buckets]))
            link(dve.tensor_tensor_scan(s.inc[q, 0:buckets], s.pad[q, 0:buckets], s.zero[q, 0:buckets], 0.0,
                                        ALU.add, ALU.add))
            link(dve.tensor_tensor(s.base[q, 0:buckets], s.inc[q, 0:buckets], s.pad[q, 0:buckets], ALU.subtract))
            link(dve.scalar_tensor_tensor(s.base[q, 0:buckets], pre, -1.0, s.base[q, 0:buckets], ALU.add, ALU.add))
            link(dve.tensor_scalar(s.tot_i[0:buckets, :], tot_t, 127.0, None, ALU.add))
            link(dve.tensor_scalar(s.tot_i[0:buckets, :], s.tot_i[0:buckets, :], 7, None, ALU.logical_shift_right))
            dve.tensor_copy(s.tot_f[0:buckets, :], s.tot_i[0:buckets, :]).then_inc(tot_ready, 1)
            dve.wait_ge(ends_ready, 1)
            link(dve.tensor_copy(s.ends[0:buckets, :], ends))
            dve.tensor_scalar(s.past[0:buckets, 0:c], k.iota_f[0:buckets, 0:c], s.ends[0:buckets, 0:1], None,
                              ALU.is_ge).then_inc(past_ready, 1)
            dve.wait_ge(map_ready, 1)
            link(dve.tensor_scalar(owner, owner_ps, float(buckets - 1), None, ALU.min))
            for b in link.loop(buckets, 4):
                link(dve.tensor_scalar(s.mask[q, :], s.bucket[q, :], k.iota_f[q, bass.ds(b, 1)], None, ALU.is_equal))
                link(dve.tensor_tensor_scan(s.count[q, :], s.mask[q, :], s.zero[q, :], s.base[q, bass.ds(b, 1)],
                                            ALU.add, ALU.add))
                link(dve.scalar_tensor_tensor(s.hit[q, :], s.bucket[q, :], k.iota_f[q, bass.ds(b, 1)], s.count[q, :],
                                              ALU.is_equal, ALU.mult))
                link(dve.tensor_tensor(s.acc[q, :], s.acc[q, :], s.hit[q, :], ALU.add))
            where = s.int_a[q, :] if pos is None else pos
            link(dve.tensor_copy(where, s.acc[q, :]))
            link(dve.tensor_scalar(s.int_b[q, :], where, 7, None, ALU.logical_shift_right))
            link(dve.tensor_copy(s.chunk[q, :], s.int_b[q, :]))
            link(dve.tensor_scalar(s.int_b[q, :], where, 127, None, ALU.bitwise_and))
            link(dve.tensor_copy(s.lane[q, :], s.int_b[q, :]))
            link(dve.tensor_scalar(s.local1[q, :], s.local1[q, :], -1.0, None, ALU.add))
            if valid is not None:
                link(dve.scalar_tensor_tensor(s.chunk[q, :], s.chunk[q, :], 1.0, valid, ALU.add, ALU.mult))
                link(dve.tensor_scalar(s.chunk[q, :], s.chunk[q, :], -1.0, None, ALU.add))
            with dve.Fori(0, m // RING) as i:
                for r in range(RING):
                    col = bass.ds(i * RING + r, 1)
                    dve.wait_ge(used, i * RING + (r + 1))
                    dve.tensor_scalar(s.lanes[q, r, 0, :], k.iota_h[q, 0:P], s.lane[q, col], s.part_a[q, col],
                                      ALU.is_equal, ALU.mult)
                    dve.tensor_scalar(s.lanes[q, r, 1, :], k.iota_h[q, 0:P], s.lane[q, col], s.part_b[q, col],
                                      ALU.is_equal, ALU.mult)
                    if degree is not None:
                        dve.tensor_scalar(s.hist_l[q, r, :], k.iota_h[q, 0:P], s.local1[q, col], None, ALU.is_equal)
                        dve.tensor_scalar(s.hist_w[q, r, 0:buckets], k.iota_h[q, 0:buckets], s.bucket[q, col], None,
                                          ALU.is_equal)
                    dve.tensor_scalar(s.chunks[q, r, 0:c], k.iota_h[q, 0:c], s.chunk[q, col], None,
                                      ALU.is_equal).then_inc(hot, 1)
            dve.wait_ge(placed, 1)
            if degree is not None:
                link(dve.tensor_copy(degree, hist))
            link(dve.tensor_copy(slot, slot_b))
            link(dve.tensor_scalar(s.low[:, 0:c], slot, 255, None, ALU.bitwise_and))
            link(dve.tensor_copy(local, s.low[:, 0:c]))
            link(dve.tensor_scalar(slot, slot, 8, None, ALU.logical_shift_right))
            link(dve.scalar_tensor_tensor(slot, slot_a, 4.0, slot, ALU.mult, ALU.add))

        @block.tensor
        def _(pe):
            pe.sem_inc(used, RING)
            pe.wait_ge(counted, 1)
            cnt = s.cnt[0:np_, 0:buckets]
            pe.matmul(pre, k.before[0:np_, 0:np_], cnt, start=True, stop=True)
            pe.matmul(tot, k.ones[0:np_, 0:np_], cnt, start=True, stop=True)
            pe.matmul(tot_t, cnt, k.ones[0:np_, 0:1], start=True, stop=True).then_inc(totals, 1)
            pe.wait_ge(tot_ready, 1)
            pe.matmul(ends, k.upto[0:buckets, 0:buckets], s.tot_f[0:buckets, :], start=True, stop=True).then_inc(ends_ready, 1)
            pe.wait_ge(past_ready, 1)
            pe.matmul(owner_ps, k.ones[0:buckets, 0:1], s.past[0:buckets, 0:c], start=True, stop=True).then_inc(map_ready, 1)
            outs = [slot_a, slot_b] + ([hist] if degree is not None else [])
            for out in outs:
                pe.matmul(out, k.zero_h[:, :], k.iota_h[:, 0:out.shape[1]], start=True, stop=False, skip_group_check=True)
            with pe.Fori(0, m // RING) as i:
                for r in range(RING):
                    pe.wait_ge(hot, i * RING + (r + 1))
                    if degree is not None:
                        pe.matmul(hist, s.hist_l[0:np_, r, :], s.hist_w[0:np_, r, 0:buckets], start=False, stop=False,
                                  skip_group_check=True)
                    pe.matmul(slot_a, s.lanes[0:np_, r, 0, :], s.chunks[0:np_, r, 0:c], start=False, stop=False,
                              skip_group_check=True)
                    pe.matmul(slot_b, s.lanes[0:np_, r, 1, :], s.chunks[0:np_, r, 0:c], start=False, stop=False,
                              skip_group_check=True).then_inc(used, 1)
            for n, out in enumerate(outs):
                last = pe.matmul(out, k.zero_h[:, :], k.iota_h[:, 0:out.shape[1]], start=False, stop=True, skip_group_check=True)
            last.then_inc(placed, 1)


def norms(k, name):
    nc = k.nc
    ctx, sem, sb = phase(k, name)
    with ctx:
        chain, rooted = sem("chain"), sem("rooted")
        block = ctx.enter_context(nc.Block())

        @block.vector
        def _(dve):
            link = Chain(dve, chain)
            link(dve.tensor_scalar(k.deg_in[:], k.deg_in[:], 1.0, None, ALU.max))
            link(dve.tensor_scalar(k.deg_out[:], k.deg_out[:], 1.0, None, ALU.max))
            dve.wait_ge(rooted, 2)
            link(dve.reciprocal(k.deg_in[:], k.deg_in[:]))
            link(dve.reciprocal(k.deg_out[:], k.deg_out[:]))

        @block.scalar
        def _(act):
            act.wait_ge(chain, 2)
            act.activation(k.deg_in[:], k.deg_in[:], ACT.Sqrt).then_inc(rooted, 1)
            act.activation(k.deg_out[:], k.deg_out[:], ACT.Sqrt).then_inc(rooted, 1)


def moments(k, name, src):
    nc = k.nc
    ctx, sem, sb = phase(k, name)
    with ctx:
        stats, mv, var = sb("stats", [P, TILES, 6]), sb("mv", [P, TILES, 2]), sb("var", [P, TILES])
        chain, rooted = sem("chain"), sem("rooted")
        block = ctx.enter_context(nc.Block())

        @block.vector
        def _(dve):
            link = Chain(dve, chain)
            with dve.Fori(0, TILES) as t:
                dve.bn_stats(stats[:, bass.ds(t, 1), :], src[:, bass.ds(t, 1), :]).then_inc(chain, 1)
            dve.wait_ge(chain, TILES)
            link.n = TILES
            for t in range(TILES):
                dve.bn_aggr(mv[:, t, :], stats[:, t, :]).then_inc(chain, 1)
            link.n += TILES
            dve.wait_ge(chain, link.n)
            link(dve.tensor_copy(k.mean[:], mv[:, :, 0]))
            link(dve.tensor_scalar(var[:], mv[:, :, 1], EPS_LN, None, ALU.add))
            dve.wait_ge(rooted, 1)
            link(dve.reciprocal(k.rstd[:], var[:]))

        @block.scalar
        def _(act):
            act.wait_ge(chain, 2 * TILES + 2)
            act.activation(var[:], var[:], ACT.Sqrt).then_inc(rooted, 1)


def conv_dense(k, n, table, weight, bias_prev):
    nc, ps = k.nc, k.ps
    ctx, sem, sb = phase(k, f"dense{n}")
    with ctx:
        w = sb("w", [P, 2, D])
        bias = sb("bias", [P, D])
        act_in, act_out, turned = sb("act_in", [P, RING, D]), sb("act_out", [P, RING, D]), sb("turned", [P, RING, D])
        loaded, stored = sem("loaded"), sem("stored")
        in_ready, scaled, flipped, turned_back, multiplied, row_ready, cleared = (
            sem(x) for x in ("in_ready", "scaled", "flipped", "turned_back", "multiplied", "row_ready", "cleared"))
        flips, prods = [ps[:, r % 4, 0:D] for r in range(RING)], [ps[:, 4 + r % 4, 0:D] for r in range(RING)]
        block = ctx.enter_context(nc.Block())

        @block.sync
        def _(sp):
            sp.dma_start(w[:], weight.rearrange("(k p) n -> p k n", p=P)).then_inc(loaded, 16)
            if n:
                sp.dma_start(bias[:], bias_prev.partition_broadcast(P)).then_inc(loaded, 16)
            with sp.Fori(0, TILES) as t:
                sp.wait_ge(row_ready, t + (1 + RING))
                sp.dma_start(table[bass.ds(t * P, P), :], k.rows[:, bass.ds(t, 1), :]).then_inc(stored, 16)
            sp.wait_ge(stored, 16 * TILES)

        @block.vector
        def _(dve):
            dve.sem_inc(turned_back, RING)
            if n:
                dve.wait_ge(loaded, 32)
            with dve.Fori(0, TILES // RING) as i:
                for r in range(RING):
                    t = bass.ds(i * RING + r, 1)
                    dve.wait_ge(scaled, i * RING + (r + 1))
                    if n == 0:
                        dve.tensor_scalar(act_in[:, r, :], k.x[:, t, :], k.mean[:, t], k.rstd[:, t],
                                          ALU.subtract, ALU.mult).then_inc(in_ready, 1)
                    else:
                        dve.scalar_tensor_tensor(act_in[:, r, :], k.h[:, t, :], k.deg_in[:, t], bias[:],
                                                 ALU.mult, ALU.add).then_inc(in_ready, 1)
                for r in range(RING):
                    dve.wait_ge(flipped, i * RING + (r + 1 + RING))
                    dve.wait_ge(multiplied, i * RING + (r + 1))
                    dve.tensor_copy(turned[:, r, :], flips[r]).then_inc(turned_back, 1)
            dve.wait_ge(in_ready, TILES)
            dve.memset(k.h[:], 0.0).then_inc(cleared, 1)

        @block.scalar
        def _(act):
            act.sem_inc(scaled, RING)
            act.sem_inc(row_ready, RING)
            with act.Fori(0, TILES // RING) as i:
                for r in range(RING):
                    t = bass.ds(i * RING + r, 1)
                    act.wait_ge(in_ready, i * RING + (r + 1))
                    act.wait_ge(flipped, i * RING + (r + 1))
                    act.activation(act_out[:, r, :], act_in[:, r, :], ACT.Relu if n else ACT.Copy,
                                   scale=k.deg_out[:, t]).then_inc(scaled, 1)
                for r in range(RING):
                    act.wait_ge(multiplied, i * RING + (r + 1 + RING))
                    act.copy(k.rows[:, bass.ds(i * RING + r, 1), :], prods[r]).then_inc(row_ready, 1)

        @block.tensor
        def _(pe):
            pe.sem_inc(flipped, RING)
            pe.sem_inc(multiplied, RING)
            pe.wait_ge(loaded, 32 if n else 16)
            with pe.Fori(0, TILES // RING) as i:
                for r in range(RING):
                    pe.wait_ge(scaled, i * RING + (r + 1 + RING))
                    pe.wait_ge(turned_back, i * RING + bank_free(r))
                    for half in range(2):
                        last = pe.transpose(flips[r][:, half * P:(half + 1) * P],
                                            act_out[:, r, half * P:(half + 1) * P], k.ident[:])
                    last.then_inc(flipped, 1)
                for r in range(RING):
                    pe.wait_ge(turned_back, i * RING + (r + 1 + RING))
                    pe.wait_ge(row_ready, i * RING + bank_free(r))
                    for half in range(2):
                        last = pe.matmul(prods[r], turned[:, r, half * P:(half + 1) * P], w[:, half, :],
                                         start=(half == 0), stop=(half == 1))
                    last.then_inc(multiplied, 1)


def conv_sum(k, n, table):
    nc, ps = k.nc, k.ps
    ctx, sem, sb = phase(k, f"sum{n}")
    with ctx:
        msg, hot = sb("msg", [P, GB, D]), sb("hot", [P, GB, P])
        idx = sb("idx", [P, GB], I32)
        idx_ready, hot_ready, summed, added, issued = (sem(x) for x in ("idx_ready", "hot_ready", "summed", "added", "issued"))
        gathered = [sem(f"gathered{r}") for r in range(GB)]
        sums = [ps[:, r, 0:D] for r in range(GB)]
        turns = EC // GB
        block = ctx.enter_context(nc.Block())

        @block.scalar
        def _(act):
            with act.Fori(0, turns) as i:
                for r in range(GB):
                    act.wait_ge(summed, i * GB + (r + 1))
                    act.copy(idx[:, r:r + 1], k.src_slot[:, bass.ds(i * GB + r, 1)]).then_inc(idx_ready, 1)

        @block.gpsimd
        def _(pool):
            with pool.Fori(0, turns) as i:
                for r in range(GB):
                    pool.wait_ge(idx_ready, i * GB + (r + 1))
                    pool.sem_inc(issued, 1)
                    pool.indirect_dma_start(out=msg[:, r, :], out_offset=None, in_=table[:, :],
                                            in_offset=bass.IndirectOffsetOnAxis(ap=idx[:, r:r + 1], axis=0)
                                            ).then_inc(gathered[r], 16)

        @block.vector
        def _(dve):
            dve.sem_inc(added, GB)
            with dve.Fori(0, turns) as i:
                for r in range(GB):
                    dve.wait_ge(summed, i * GB + (r + 1))
                    dve.tensor_scalar(hot[:, r, :], k.iota1[:], k.src_local[:, bass.ds(i * GB + r, 1)], None,
                                      ALU.is_equal).then_inc(hot_ready, 1)
                for r in range(GB):
                    window = dve.value_load(k.win_dst[0:1, bass.ds(i * GB + r, 1)], min_val=0, max_val=TILES - 1)
                    here = k.h[:, bass.ds(window, 1), :]
                    dve.wait_ge(summed, i * GB + (r + 1 + GB))
                    dve.wait_ge(added, i * GB + (r + GB))
                    dve.tensor_tensor(here, here, sums[r], ALU.add).then_inc(added, 1)

        @block.tensor
        def _(pe):
            pe.sem_inc(summed, GB)
            with pe.Fori(0, turns) as i:
                for r in range(GB):
                    pe.wait_ge(hot_ready, i * GB + (r + 1))
                    pe.wait_ge(added, i * GB + (r + 1))
                    pe.wait_ge(gathered[r], i * 16 + 16)
                    pe.matmul(sums[r], hot[:, r, :], msg[:, r, :], start=True, stop=True).then_inc(summed, 1)


def conv_finish(k, bias_last):
    nc = k.nc
    ctx, sem, sb = phase(k, "finish")
    with ctx:
        bias = sb("bias", [P, D])
        loaded, chain = sem("loaded"), sem("chain")
        block = ctx.enter_context(nc.Block())

        @block.sync
        def _(sp):
            sp.dma_start(bias[:], bias_last.partition_broadcast(P)).then_inc(loaded, 16)

        @block.vector
        def _(dve):
            dve.wait_ge(loaded, 16)
            bias_all = bias[:].unsqueeze(1).to_broadcast([P, TILES, D])
            link = Chain(dve, chain)
            link(dve.tensor_tensor(k.x[:], k.x[:], bias_all, ALU.add))
            with dve.Fori(0, TILES) as t:
                here = k.x[:, bass.ds(t, 1), :]
                dve.scalar_tensor_tensor(here, k.h[:, bass.ds(t, 1), :], k.deg_in[:, bass.ds(t, 1)], here,
                                         ALU.mult, ALU.add).then_inc(chain, 1)
            dve.wait_ge(chain, 1 + TILES)


def norm_dense(k, name, weight, width, result, table=None, xn_table=None, clear=None):
    nc, ps = k.nc, k.ps
    ctx, sem, sb = phase(k, name)
    with ctx:
        xn, turned = sb("xn", [P, RING, D]), sb("turned", [P, RING, D])
        xn_ready, kept, flipped, turned_back, multiplied, row_ready, stored, cleared = (
            sem(x) for x in ("xn_ready", "kept", "flipped", "turned_back", "multiplied", "row_ready", "stored", "cleared"))
        xn_stored = [sem(f"xn_stored{r}") for r in range(RING)]
        flips, prods = [ps[:, r % 4, 0:D] for r in range(RING)], [ps[:, 4 + r % 4, 0:width] for r in range(RING)]
        block = ctx.enter_context(nc.Block())

        if xn_table is not None:
            @block.sync
            def _(sp):
                sp.sem_inc(kept, RING)
                with sp.Fori(0, TILES // RING) as i:
                    for r in range(RING):
                        sp.wait_ge(xn_ready, i * RING + (r + 1))
                        sp.dma_start(xn_table[bass.ds((i * RING + r) * P, P), :], xn[:, r, :]).then_inc(xn_stored[r], 16)
                    for r in range(RING):
                        sp.wait_ge(xn_stored[r], i * 16 + 16)
                        sp.sem_inc(kept, 1)

        if table is not None:
            @block.sync
            def _(sp):
                with sp.Fori(0, TILES) as t:
                    sp.wait_ge(row_ready, t + (1 + RING))
                    sp.dma_start(table[bass.ds(t * P, P), :], result[:, bass.ds(t, 1), :]).then_inc(stored, 16)
                sp.wait_ge(stored, 16 * TILES)

        @block.vector
        def _(dve):
            dve.sem_inc(turned_back, RING)
            with dve.Fori(0, TILES // RING) as i:
                for r in range(RING):
                    t = bass.ds(i * RING + r, 1)
                    dve.wait_ge(flipped, i * RING + (r + 1))
                    if xn_table is not None:
                        dve.wait_ge(kept, i * RING + (r + 1))
                    dve.tensor_scalar(xn[:, r, :], k.x[:, t, :], k.mean[:, t], k.rstd[:, t],
                                      ALU.subtract, ALU.mult).then_inc(xn_ready, 1)
                for r in range(RING):
                    dve.wait_ge(flipped, i * RING + (r + 1 + RING))
                    dve.wait_ge(multiplied, i * RING + (r + 1))
                    dve.tensor_copy(turned[:, r, :], flips[r]).then_inc(turned_back, 1)
            if clear is not None:
                dve.memset(clear, 0.0).then_inc(cleared, 1)

        @block.scalar
        def _(act):
            act.sem_inc(row_ready, RING)
            with act.Fori(0, TILES // RING) as i:
                for r in range(RING):
                    act.wait_ge(multiplied, i * RING + (r + 1 + RING))
                    act.copy(result[:, bass.ds(i * RING + r, 1), :], prods[r]).then_inc(row_ready, 1)

        @block.tensor
        def _(pe):
            pe.sem_inc(flipped, RING)
            pe.sem_inc(multiplied, RING)
            with pe.Fori(0, TILES // RING) as i:
                for r in range(RING):
                    pe.wait_ge(xn_ready, i * RING + (r + 1))
                    pe.wait_ge(turned_back, i * RING + bank_free(r))
                    for half in range(2):
                        last = pe.transpose(flips[r][:, half * P:(half + 1) * P],
                                            xn[:, r, half * P:(half + 1) * P], k.ident[:])
                    last.then_inc(flipped, 1)
                for r in range(RING):
                    pe.wait_ge(turned_back, i * RING + (r + 1 + RING))
                    pe.wait_ge(row_ready, i * RING + bank_free(r))
                    for half in range(2):
                        last = pe.matmul(prods[r], turned[:, r, half * P:(half + 1) * P], weight[:, half, :],
                                         start=(half == 0), stop=(half == 1))
                    last.then_inc(multiplied, 1)


class Moe:

    def __init__(self, k, ctx, name, experts, chunks, gate_w, gate_b, w1, b1, w2, b2):
        sb = lambda n, s, d=F32: ctx.enter_context(k.nc.sbuf_tensor(f"{name}_{n}", s, d))
        self.name, self.e, self.c = name, experts, chunks
        self.gate_w, self.gate_b, self.w1, self.b1, self.w2, self.b2 = gate_w, gate_b, w1, b1, w2, b2
        self.gate = sb("gate", [P, 2, experts])
        self.gate_bias = sb("gate_bias", [P, experts])
        self.score = sb("score", [P, TILES, experts])
        self.b1_t = sb("b1_t", [P, experts, FF // P])
        self.b2_sb = sb("b2_sb", [experts, D])
        self.weight = sb("weight", [P, TILES, 2])
        self.combine = sb("combine", [P, TILES, experts])
        self.slot = sb("slot", [P, chunks + 8], I32)
        self.pos = sb("pos", [P, TILES, 2], I32)
        self.owner = sb("owner", [1, chunks], I32)
        self.small = ctx.enter_context(k.nc.semaphore(f"{name}_small"))
        self.big = ctx.enter_context(k.nc.semaphore(f"{name}_big"))


def load_experts(k, eng, moe, first, last):
    for_expert = k.big[:].rearrange("p (e w) -> p e w", w=2048)
    with eng.Fori(first, last) as e:
        eng.dma_start(for_expert[:, bass.ds(e, 1), 0:1024].rearrange("p o (k f) -> p (o k) f", f=FF),
                      moe.w1[bass.ds(e, 1), :, :].rearrange("o (k p) f -> p (o k) f", p=P)).then_inc(moe.big, 16)
        eng.dma_start(for_expert[:, bass.ds(e, 1), 1024:2048].rearrange("p o (k f) -> p (o k) f", f=D),
                      moe.w2[bass.ds(e, 1), :, :].rearrange("o (k p) f -> p (o k) f", p=P)).then_inc(moe.big, 16)


def load_small(k, eng, moe):
    with k.nc.allow_non_contiguous_dma(reason="the bias of a hidden unit goes to the unit's partition"):
        eng.dma_start(moe.gate[:], moe.gate_w.rearrange("(k p) e -> p k e", p=P)).then_inc(moe.small, 16)
        eng.dma_start(moe.gate_bias[:], moe.gate_b.partition_broadcast(P)).then_inc(moe.small, 16)
        eng.dma_start(moe.b1_t[:].rearrange("p e f -> p (e f)"),
                      moe.b1.rearrange("e (f p) -> p (e f)", p=P)).then_inc(moe.small, 16)
        eng.dma_start(moe.b2_sb[:], moe.b2[:, :]).then_inc(moe.small, 16)


SMALL_LOADS = 64


def prefetch(k, name, jobs):
    ctx, sem, sb = phase(k, name)
    with ctx:
        block = ctx.enter_context(k.nc.Block())

        @block.sync
        def _(sp):
            for job in jobs:
                job(sp)


def choose(k, moe, softmax_first, key, node, valid):
    nc = k.nc
    e = moe.e
    ctx, sem, sb = phase(k, moe.name + "_choose")
    with ctx:
        top, which = sb("top", [P, TILES, 8]), sb("which", [P, TILES, 8], U32)
        ids, tmp, peak, node_f = sb("ids", [P, TILES, 2]), sb("tmp", [P, TILES, e]), sb("peak", [P, TILES]), sb("node_f", [P, TILES, 2])
        chain, numbered, ready, powered = sem("chain"), sem("numbered"), sem("ready"), sem("powered")
        block = ctx.enter_context(nc.Block())
        wide = [P, TILES, e]

        @block.gpsimd
        def _(pool):
            pool.iota(node, pattern=[[P, TILES], [0, 2]], base=0, channel_multiplier=1).then_inc(numbered, 1)

        @block.scalar
        def _(act):
            act.wait_ge(ready, 1)
            if softmax_first:
                act.activation(moe.score[:], moe.score[:], ACT.Exp).then_inc(powered, 1)
            else:
                act.activation(moe.weight[:, :, 1], moe.weight[:, :, 1], ACT.Exp).then_inc(powered, 1)

        @block.vector
        def _(dve):
            link = Chain(dve, chain)
            score = moe.score[:]
            link(dve.memset(moe.slot[:, moe.c:], 0))
            dve.wait_ge(moe.small, SMALL_LOADS)
            link(dve.tensor_tensor(score, score, moe.gate_bias[:].unsqueeze(1).to_broadcast(wide), ALU.add))
            if softmax_first:
                link(dve.tensor_reduce(peak[:], score, AX.X, ALU.max))
                dve.tensor_tensor(score, score, peak[:].unsqueeze(2).to_broadcast(wide), ALU.subtract).then_inc(ready, 1)
                dve.wait_ge(powered, 1)
                link(dve.tensor_reduce(peak[:], score, AX.X, ALU.add))
                link(dve.reciprocal(peak[:], peak[:]))
                link(dve.tensor_tensor(score, score, peak[:].unsqueeze(2).to_broadcast(wide), ALU.mult))
            for t in range(TILES):
                dve.max(top[:, t, :], moe.score[:, t, :]).then_inc(chain, 1)
            link.n += TILES
            dve.wait_ge(chain, link.n)
            for t in range(TILES):
                dve.max_index(which[:, t, :], top[:, t, :], moe.score[:, t, :]).then_inc(chain, 1)
            link.n += TILES
            dve.wait_ge(chain, link.n)
            link(dve.tensor_copy(ids[:], which[:, :, 0:2]))
            if softmax_first:
                link(dve.tensor_copy(moe.weight[:], top[:, :, 0:2]))
            else:
                dve.tensor_tensor(moe.weight[:, :, 1], top[:, :, 1], top[:, :, 0], ALU.subtract).then_inc(ready, 1)
                dve.wait_ge(powered, 1)
                link(dve.tensor_scalar(peak[:], moe.weight[:, :, 1], 1.0, None, ALU.add))
                link(dve.reciprocal(moe.weight[:, :, 0], peak[:]))
                link(dve.tensor_tensor(moe.weight[:, :, 1], moe.weight[:, :, 1], moe.weight[:, :, 0], ALU.mult))
            number = k.iota_f[:, 0:e].unsqueeze(1).to_broadcast(wide)
            for j in range(2):
                out = moe.combine[:] if j == 0 else tmp[:]
                link(dve.tensor_tensor(out, number, ids[:, :, j:j + 1].to_broadcast(wide), ALU.is_equal))
                link(dve.tensor_tensor(out, out, moe.weight[:, :, j:j + 1].to_broadcast(wide), ALU.mult))
            link(dve.tensor_tensor(moe.combine[:], moe.combine[:], tmp[:], ALU.add))
            link(dve.tensor_scalar(key, ids[:], 128.0, None, ALU.mult))
            dve.wait_ge(numbered, 1)
            link(dve.tensor_copy(node_f[:], node))
            link(dve.tensor_scalar(valid, node_f[:], float(NODES), None, ALU.is_lt))


def experts(k, moe, xn_table, y_table, func):
    nc, ps = k.nc, k.ps
    ctx, sem, sb = phase(k, moe.name + "_experts")
    with ctx:
        U = 8
        KD, KF = D // P, FF // P
        rows, idx = sb("rows", [P, U, D]), sb("idx", [P, U], I32)
        x_t, hid, hid_t, y = sb("x_t", [P, 2, D]), sb("hid", [P, 2, FF]), sb("hid_t", [P, 2, FF]), sb("y", [P, U, D])
        idx_ready, issued, flip_x, x_back, up, hid_ready, flip_h, acted, down, y_ready, kept = (
            sem(n) for n in ("idx_ready", "issued", "flip_x", "x_back", "up", "hid_ready", "flip_h", "acted", "down",
                             "y_ready", "kept"))
        gathered, stored = [sem(f"gathered{r}") for r in range(U)], [sem(f"stored{r}") for r in range(U)]
        weights = k.big[:].rearrange("p (e w) -> p e w", w=2048)
        turns = moe.c // U
        assert moe.c % U == 0
        block = ctx.enter_context(nc.Block())

        def owner(eng, i, r):
            return eng.value_load(moe.owner[0:1, bass.ds(i * U + r, 1)], min_val=0, max_val=moe.e - 1)

        @block.sync
        def _(sp):
            sp.sem_inc(kept, U)
            with sp.Fori(0, turns) as i:
                for r in range(U):
                    sp.wait_ge(y_ready, i * U + (r + 1 + 2))
                    sp.dma_start(y_table[bass.ds((i * U + r) * P, P), :], y[:, r, :]).then_inc(stored[r], 16)
                    if r >= U // 2:
                        sp.wait_ge(stored[r - U // 2], i * 16 + 16)
                        sp.sem_inc(kept, 1)
                for r in range(U // 2, U):
                    sp.wait_ge(stored[r], i * 16 + 16)
                    sp.sem_inc(kept, 1)

        @block.gpsimd
        def _(pool):
            with pool.Fori(0, turns) as i:
                for r in range(U):
                    pool.wait_ge(idx_ready, i * U + (r + 1))
                    pool.sem_inc(issued, 1)
                    pool.indirect_dma_start(out=rows[:, r, :], out_offset=None, in_=xn_table[:, :],
                                            in_offset=bass.IndirectOffsetOnAxis(ap=idx[:, r:r + 1], axis=0)
                                            ).then_inc(gathered[r], 16)

        @block.scalar
        def _(act):
            act.sem_inc(acted, 2)
            act.wait_ge(moe.small, SMALL_LOADS)
            act.copy(idx[:], moe.slot[:, 0:U]).then_inc(idx_ready, U)
            with act.Fori(0, turns) as i:
                for r in range(U):
                    e = owner(act, i, r)
                    act.wait_ge(flip_h, i * U + (r + 1 + 2))
                    act.wait_ge(down, i * U + (r + 1))
                    for f in range(KF):
                        last = act.activation(hid_t[:, r % 2, f * P:(f + 1) * P], ps[:, 4 + r % 2, f * P:(f + 1) * P], func,
                                              bias=moe.b1_t[:, bass.ds(e, 1), f])
                    last.then_inc(acted, 1)
                    act.wait_ge(flip_x, i * U + (r + 1 + U))
                    act.copy(idx[:, r:r + 1], moe.slot[:, bass.ds(i * U + (r + U), 1)]).then_inc(idx_ready, 1)

        @block.vector
        def _(dve):
            dve.sem_inc(x_back, 2)
            dve.sem_inc(hid_ready, 2)
            dve.sem_inc(y_ready, 2)
            with dve.Fori(0, turns) as i:
                for pair in range(0, U, 2):
                    for r in (pair, pair + 1):
                        dve.wait_ge(flip_x, i * U + (r + 1 + U))
                        dve.wait_ge(up, i * U + (r + 1))
                        dve.tensor_copy(x_t[:, r % 2, :], ps[:, r % 2, 0:D]).then_inc(x_back, 1)
                    for r in (pair, pair + 1):
                        dve.wait_ge(up, i * U + (r + 1 + 2))
                        dve.wait_ge(flip_h, i * U + (r + 1))
                        dve.tensor_copy(hid[:, r % 2, :], ps[:, 2 + r % 2, :]).then_inc(hid_ready, 1)
                    for r in (pair, pair + 1):
                        dve.wait_ge(down, i * U + (r + 1 + 2))
                        dve.wait_ge(kept, i * U + (r + 1))
                        dve.tensor_copy(y[:, r, :], ps[:, 6 + r % 2, 0:D]).then_inc(y_ready, 1)

        @block.tensor
        def _(pe):
            pe.sem_inc(flip_x, U)
            pe.sem_inc(up, 2)
            pe.sem_inc(flip_h, 2)
            pe.sem_inc(down, 2)
            pe.wait_ge(moe.big, 32 * moe.e)
            with pe.Fori(0, turns) as i:
                for pair in range(0, U, 2):
                    for r in (pair, pair + 1):
                        pe.wait_ge(x_back, i * U + (r + 1))
                        pe.wait_ge(gathered[r], i * 16 + 16)
                        for h in range(KD):
                            last = pe.transpose(ps[:, r % 2, h * P:(h + 1) * P], rows[:, r, h * P:(h + 1) * P], k.ident[:])
                        last.then_inc(flip_x, 1)
                    mine = [owner(pe, i, pair), owner(pe, i, pair + 1)]
                    for r in (pair, pair + 1):
                        w = weights[:, bass.ds(mine[r % 2], 1), :]
                        pe.wait_ge(x_back, i * U + (r + 1 + 2))
                        pe.wait_ge(hid_ready, i * U + (r + 1))
                        for h in range(KD):
                            last = pe.matmul(ps[:, 2 + r % 2, :], x_t[:, r % 2, h * P:(h + 1) * P],
                                             w[:, :, h * FF:(h + 1) * FF], start=(h == 0), stop=(h == KD - 1))
                        last.then_inc(up, 1)
                    for r in (pair, pair + 1):
                        pe.wait_ge(hid_ready, i * U + (r + 1 + 2))
                        pe.wait_ge(acted, i * U + (r + 1))
                        for f in range(KF):
                            last = pe.transpose(ps[:, 4 + r % 2, f * P:(f + 1) * P], hid[:, r % 2, f * P:(f + 1) * P],
                                                k.ident[:])
                        last.then_inc(flip_h, 1)
                    for r in (pair, pair + 1):
                        w = weights[:, bass.ds(mine[r % 2], 1), :]
                        pe.wait_ge(acted, i * U + (r + 1 + 2))
                        pe.wait_ge(y_ready, i * U + (r + 1))
                        for f in range(KF):
                            last = pe.matmul(ps[:, 6 + r % 2, 0:D], hid_t[:, r % 2, f * P:(f + 1) * P],
                                             w[:, :, KD * FF + f * D:KD * FF + (f + 1) * D],
                                             start=(f == 0), stop=(f == KF - 1))
                        last.then_inc(down, 1)


def combine(k, moe, y_table, result, add_norm):
    nc, ps = k.nc, k.ps
    e = moe.e
    ctx, sem, sb = phase(k, moe.name + "_combine")
    with ctx:
        got, idx = sb("got", [P, RING, 2, D]), sb("idx", [P, RING, 2], I32)
        cw, cw_t, part = sb("cw", [P, RING, e]), sb("cw_t", [e, RING, P]), sb("part", [P, RING, D])
        idx_ready, issued, cw_ready, flipped, cw_back, biased, summed, chain = (
            sem(n) for n in ("idx_ready", "issued", "cw_ready", "flipped", "cw_back", "biased", "summed", "chain"))
        gathered = [sem(f"gathered{r}") for r in range(RING)]
        block = ctx.enter_context(nc.Block())
        pos, weight = moe.pos[:], moe.weight[:].rearrange("p t j -> p (t j)")

        @block.scalar
        def _(act):
            act.sem_inc(cw_back, RING)
            with act.Fori(0, TILES // RING) as i:
                for r in range(RING):
                    t = bass.ds(i * RING + r, 1)
                    act.wait_ge(summed, i * RING + (r + 1))
                    act.copy(idx[:, r, :], pos[:, t, :]).then_inc(idx_ready, 1)
                    act.wait_ge(flipped, i * RING + (r + 1))
                    act.copy(cw[:, r, :], moe.combine[:, t, :]).then_inc(cw_ready, 1)
                for r in range(RING):
                    act.wait_ge(flipped, i * RING + (r + 1 + RING))
                    act.wait_ge(biased, i * RING + (r + 1))
                    act.copy(cw_t[:, r, :], ps[0:e, r % 4, 0:P]).then_inc(cw_back, 1)

        @block.gpsimd
        def _(pool):
            with pool.Fori(0, TILES // RING) as i:
                for r in range(RING):
                    pool.wait_ge(idx_ready, i * RING + (r + 1))
                    pool.sem_inc(issued, 1)
                    for j in range(2):
                        pool.indirect_dma_start(out=got[:, r, j, :], out_offset=None, in_=y_table[:, :],
                                                in_offset=bass.IndirectOffsetOnAxis(ap=idx[:, r, j:j + 1], axis=0)
                                                ).then_inc(gathered[r], 16)

        @block.tensor
        def _(pe):
            pe.sem_inc(flipped, RING)
            pe.sem_inc(biased, RING)
            with pe.Fori(0, TILES // RING) as i:
                for r in range(RING):
                    pe.wait_ge(cw_ready, i * RING + (r + 1))
                    pe.wait_ge(cw_back, i * RING + bank_free(r))
                    pe.transpose(ps[0:e, r % 4, 0:P], cw[:, r, :], k.ident[:]).then_inc(flipped, 1)
                for r in range(RING):
                    pe.wait_ge(cw_back, i * RING + (r + 1 + RING))
                    pe.wait_ge(summed, i * RING + bank_free(r))
                    pe.matmul(ps[:, 4 + r % 4, 0:D], cw_t[:, r, :], moe.b2_sb[:], start=True, stop=True).then_inc(biased, 1)

        @block.vector
        def _(dve):
            dve.sem_inc(summed, RING)
            link = Chain(dve, chain)
            for i in link.loop(TILES // RING, RING * (3 if add_norm else 2)):
                for r in range(RING):
                    t = bass.ds(i * RING + r, 1)
                    base = k.x[:, t, :]
                    if add_norm:
                        link(dve.tensor_scalar(part[:, r, :], base, k.mean[:, t], k.rstd[:, t], ALU.subtract, ALU.mult))
                        base = part[:, r, :]
                    dve.wait_ge(biased, i * RING + (r + 1 + RING))
                    link(dve.tensor_tensor(part[:, r, :], base, ps[:, 4 + r % 4, 0:D], ALU.add))
                    dve.wait_ge(gathered[r], i * 32 + 32)
                    w = [weight[:, bass.ds((i * RING + r) * 2 + j, 1)] for j in range(2)]
                    link(dve.scalar_tensor_tensor(part[:, r, :], got[:, r, 0, :], w[0], part[:, r, :], ALU.mult, ALU.add))
                    dve.scalar_tensor_tensor(result[:, t, :], got[:, r, 1, :], w[1], part[:, r, :],
                                             ALU.mult, ALU.add).then_inc(summed, 1)


def add_scaled_norm(k, y, gamma, beta):
    nc = k.nc
    ctx, sem, sb = phase(k, "scaled_norm")
    with ctx:
        g, b = sb("gamma", [P, D]), sb("beta", [P, D])
        loaded, chain = sem("loaded"), sem("chain")
        block = ctx.enter_context(nc.Block())

        @block.sync
        def _(sp):
            sp.dma_start(g[:], gamma.partition_broadcast(P)).then_inc(loaded, 16)
            sp.dma_start(b[:], beta.partition_broadcast(P)).then_inc(loaded, 16)

        @block.vector
        def _(dve):
            wide = [P, TILES, D]
            link = Chain(dve, chain)
            with dve.Fori(0, TILES) as t:
                here, one = y[:, bass.ds(t, 1), :], bass.ds(t, 1)
                dve.tensor_scalar(here, here, k.mean[:, one], k.rstd[:, one], ALU.subtract, ALU.mult).then_inc(chain, 1)
            link.n = TILES
            dve.wait_ge(chain, TILES)
            dve.wait_ge(loaded, 32)
            link(dve.tensor_tensor(y, y, g[:].unsqueeze(1).to_broadcast(wide), ALU.mult))
            link(dve.tensor_tensor(y, y, b[:].unsqueeze(1).to_broadcast(wide), ALU.add))
            link(dve.tensor_tensor(k.x[:], k.x[:], y, ALU.add))


def gat_weights(k, weight, left, right, w_all):
    nc, ps = k.nc, k.ps
    ctx, sem, sb = phase(k, "gat_weights")
    with ctx:
        lr, lr_t, w_t = sb("lr", [2 * HEADS, HD]), sb("lr_t", [HD, 2 * HEADS]), sb("w_t", [HD, 2, P])
        loaded, flipped, back, multiplied, done = (sem(n) for n in ("loaded", "flipped", "back", "multiplied", "done"))
        block = ctx.enter_context(nc.Block())

        @block.sync
        def _(sp):
            sp.dma_start(w_all[:, :, 0:HD], weight.rearrange("(k p) n -> p k n", p=P)).then_inc(loaded, 16)
            sp.dma_start(lr[0:HEADS, :], right[:, :]).then_inc(loaded, 16)
            sp.dma_start(lr[HEADS:2 * HEADS, :], left[:, :]).then_inc(loaded, 16)

        @block.tensor
        def _(pe):
            pe.wait_ge(loaded, 48)
            pe.transpose(ps[0:HD, 0, 0:2 * HEADS], lr[:, :], k.ident[0:2 * HEADS, 0:2 * HEADS])
            for half in range(2):
                last = pe.transpose(ps[0:HD, 1, half * P:(half + 1) * P], w_all[:, half, 0:HD], k.ident[:])
            last.then_inc(flipped, 1)
            pe.wait_ge(back, 2)
            for half in range(2):
                last = pe.matmul(ps[:, 2, half * 8:half * 8 + 8], w_t[:, half, :], lr_t[:], start=True, stop=True)
            last.then_inc(multiplied, 1)

        @block.vector
        def _(dve):
            dve.wait_ge(flipped, 1)
            dve.tensor_copy(lr_t[:], ps[0:HD, 0, 0:2 * HEADS]).then_inc(back, 1)
            dve.tensor_copy(w_t[:].rearrange("p k n -> p (k n)"), ps[0:HD, 1, 0:2 * P]).then_inc(back, 1)
            dve.wait_ge(multiplied, 1)
            for half in range(2):
                dve.tensor_copy(w_all[:, half, HD:HD + 8], ps[:, 2, half * 8:half * 8 + 8]).then_inc(done, 1)


def gat_sum(k, table, rows, acc, room):
    nc, ps = k.nc, k.ps
    ctx, sem, sb = phase(k, "gat_sum")
    with ctx:
        G, W = 8, HEADS * HD + HEADS
        idx, msg = sb("idx", [P, 2, G], I32), sb("msg", [P, 2, G, GW])
        hot, hot_t = sb("hot", [P, 2, G, P]), sb("hot_t", [P, 2, G, P])
        logit, e = sb("logit", [P, 2, G, HEADS]), sb("e", [P, 2, G, HEADS])
        val = room[:, 0:2 * G * W].rearrange("p (h c n) -> p h c n", h=2, c=G)
        idx_ready, issued, hot_ready, flipped, hot_back, scored, z_ready, l_ready, e_ready, e_kept, val_ready, summed, added = (
            sem(n) for n in ("idx_ready", "issued", "hot_ready", "flipped", "hot_back", "scored", "z_ready", "l_ready",
                             "e_ready", "e_kept", "val_ready", "summed", "added"))
        gathered = [sem(f"gathered{h}") for h in range(2)]
        turns = EC // (2 * G)
        block = ctx.enter_context(nc.Block())
        left = ps[:, 2, 0:G * HEADS]
        sums = [ps[:, 3 + c % 4, 0:W] for c in range(G)]

        @block.scalar
        def _(act):
            act.sem_inc(hot_back, 2)
            with act.Fori(0, turns) as i:
                for h in range(2):
                    act.wait_ge(val_ready, i * 2 + (h + 1))
                    act.copy(idx[:, h, :], k.dst_slot[:, bass.ds((i * 2 + h) * G, G)]).then_inc(idx_ready, 1)
                    act.wait_ge(scored, i * 2 + (h + 1))
                    for b in range(2):
                        act.wait_ge(flipped, i * 4 + (h * 2 + b + 1))
                        act.copy(hot_t[:, h, b * 4:b * 4 + 4, :].rearrange("p c n -> p (c n)"), ps[:, b, :]).then_inc(hot_back, 1)
                    act.wait_ge(l_ready, i * 2 + (h + 1))
                    act.activation(e[:, h].rearrange("p c n -> p (c n)"), logit[:, h].rearrange("p c n -> p (c n)"),
                                   ACT.Exp).then_inc(e_ready, 1)

        @block.gpsimd
        def _(pool):
            with pool.Fori(0, turns) as i:
                for h in range(2):
                    pool.wait_ge(idx_ready, i * 2 + (h + 1))
                    pool.sem_inc(issued, 1)
                    for c in range(G):
                        pool.indirect_dma_start(out=msg[:, h, c, :], out_offset=None, in_=table[:, :],
                                                in_offset=bass.IndirectOffsetOnAxis(ap=idx[:, h, c:c + 1], axis=0)
                                                ).then_inc(gathered[h], 16)

        @block.tensor
        def _(pe):
            pe.sem_inc(scored, 2)
            pe.sem_inc(summed, 2 * G)
            with pe.Fori(0, turns) as i:
                for h in range(2):
                    pe.wait_ge(hot_ready, i * 2 + (h + 1))
                    for b in range(2):
                        pe.wait_ge(hot_back, i * 4 + (h * 2 + b + 1))
                        for c in range(4):
                            last = pe.transpose(ps[:, b, c * P:(c + 1) * P], hot[:, h, b * 4 + c, :], k.ident[:])
                        last.then_inc(flipped, 1)
                    pe.wait_ge(hot_back, i * 4 + (h * 2 + 2 + 2))
                    pe.wait_ge(z_ready, i * 2 + (h + 1))
                    for c in range(G):
                        window = pe.value_load(k.win_src[0:1, bass.ds((i * 2 + h) * G + c, 1)], min_val=0, max_val=TILES - 1)
                        last = pe.matmul(left[:, c * HEADS:(c + 1) * HEADS], hot_t[:, h, c, :],
                                         rows[:, bass.ds(window, 1), HD + HEADS:GW], start=True, stop=True)
                    last.then_inc(scored, 1)
                    pe.wait_ge(val_ready, i * 2 + (h + 1 + 2))
                    for c in range(G):
                        pe.wait_ge(added, (i * 2 + h) * G + (c + 1))
                        pe.matmul(sums[c], hot[:, h, c, :], val[:, h, c, :], start=True, stop=True).then_inc(summed, 1)

        @block.vector
        def _(dve):
            dve.sem_inc(z_ready, 1)
            dve.sem_inc(val_ready, 2)
            dve.sem_inc(added, 4)
            with dve.Fori(0, turns) as i:
                for h in range(2):
                    dve.wait_ge(summed, (i * 2 + h) * G + G)
                    for c in range(G):
                        last = dve.tensor_scalar(hot[:, h, c, :], k.iota1[:], k.dst_local[:, bass.ds((i * 2 + h) * G + c, 1)],
                                                 None, ALU.is_equal)
                    last.then_inc(hot_ready, 1)
                    dve.wait_ge(scored, i * 2 + (h + 1 + 2))
                    dve.wait_ge(gathered[h], i * (16 * G) + 16 * G)
                    dve.tensor_tensor(logit[:, h], left.rearrange("p (c n) -> p c n", n=HEADS),
                                      msg[:, h, :, HD:HD + HEADS], ALU.add).then_inc(z_ready, 1)
                    dve.wait_ge(z_ready, i * 2 + (h + 1 + 1))
                    dve.scalar_tensor_tensor(logit[:, h], logit[:, h], 0.2, logit[:, h], ALU.mult, ALU.max).then_inc(l_ready, 1)
                    dve.wait_ge(e_ready, i * 2 + (h + 1))
                    dve.tensor_copy(val[:, h, :, HEADS * HD:W], e[:, h]).then_inc(e_kept, 1)
                    wide = [P, G, HEADS, HD]
                    dve.tensor_tensor(val[:, h, :, 0:HEADS * HD].rearrange("p c (n d) -> p c n d", d=HD),
                                      msg[:, h, :, 0:HD].unsqueeze(2).to_broadcast(wide),
                                      e[:, h].unsqueeze(3).to_broadcast(wide), ALU.mult).then_inc(val_ready, 1)
                    for c in range(G):
                        window = dve.value_load(k.win_src[0:1, bass.ds((i * 2 + h) * G + c, 1)], min_val=0, max_val=TILES - 1)
                        here = acc[:, bass.ds(window, 1), :]
                        dve.wait_ge(summed, (i * 2 + h) * G + (c + 1 + 2 * G))
                        dve.wait_ge(added, (i * 2 + h) * G + (c + 4))
                        dve.tensor_tensor(here, here, sums[c], ALU.add).then_inc(added, 1)


def gat_finish(k, acc, tmp, bias):
    nc = k.nc
    ctx, sem, sb = phase(k, "gat_finish")
    with ctx:
        b, inv = sb("b", [P, HD]), sb("inv", [P, TILES, HEADS])
        loaded, chain, ready, powered = sem("loaded"), sem("chain"), sem("ready"), sem("powered")
        block = ctx.enter_context(nc.Block())
        wide = [P, TILES, HEADS, HD]

        @block.sync
        def _(sp):
            sp.dma_start(b[:], bias.partition_broadcast(P)).then_inc(loaded, 16)

        @block.scalar
        def _(act):
            act.wait_ge(ready, 1)
            act.activation(tmp, tmp, ACT.Exp).then_inc(powered, 1)

        @block.vector
        def _(dve):
            link = Chain(dve, chain)
            v3 = acc[:, :, 0:D]
            v4 = v3.rearrange("p t (n d) -> p t n d", d=HD)
            link(dve.tensor_scalar(inv[:], acc[:, :, D:D + HEADS], ROWSUM_EPS, None, ALU.max))
            link(dve.reciprocal(inv[:], inv[:]))
            link(dve.tensor_tensor(v4, v4, inv[:].unsqueeze(3).to_broadcast(wide), ALU.mult))
            dve.wait_ge(loaded, 16)
            link(dve.tensor_tensor(v4, v4, b[:].unsqueeze(1).unsqueeze(1).to_broadcast(wide), ALU.add))
            dve.tensor_scalar(tmp, v3, 0.0, None, ALU.min).then_inc(ready, 1)
            dve.wait_ge(ready, 1)
            dve.wait_ge(powered, 1)
            link(dve.scalar_tensor_tensor(v3, v3, 0.0, tmp, ALU.max, ALU.add))
            link(dve.scalar_tensor_tensor(k.x[:], v3, -1.0, k.x[:], ALU.add, ALU.add))


def write_out(k, out):
    nc = k.nc
    ctx, sem, sb = phase(k, "out")
    with ctx:
        stored = sem("stored")
        block = ctx.enter_context(nc.Block())

        @block.sync
        def _(sp):
            sp.dma_start(out[0:(TILES - 1) * P, :].rearrange("(t p) d -> p t d", p=P),
                         k.x[:, 0:TILES - 1, :]).then_inc(stored, 16)
            sp.dma_start(out[(TILES - 1) * P:NODES, :], k.x[0:LAST, TILES - 1, :]).then_inc(stored, 16)
            sp.wait_ge(stored, 32)


EARLY = (E0 * 2048 - 2 * TILES * D) // 2048


def mixture(k, moe, xn_table, y_table, func, softmax_first, result, add_norm):
    nc = k.nc
    moments(k, moe.name + "_ln", k.x)
    norm_dense(k, moe.name + "_gate", moe.gate, moe.e, moe.score[:], xn_table=xn_table)
    with ExitStack() as ctx:
        key = ctx.enter_context(nc.sbuf_tensor(moe.name + "_key", [P, TILES, 2], I32))
        node = ctx.enter_context(nc.sbuf_tensor(moe.name + "_node", [P, TILES, 2], I32))
        valid = ctx.enter_context(nc.sbuf_tensor(moe.name + "_valid", [P, TILES, 2], F32))
        local = ctx.enter_context(nc.sbuf_tensor(moe.name + "_local", [P, moe.c], F32))
        choose(k, moe, softmax_first, key[:], node[:], valid[:])
        flat = lambda a: a.rearrange("p t j -> p (t j)")
        sort(k, moe.name + "_sort", P, PM, moe.e, moe.c, flat(key[:]), flat(node[:]), moe.slot[:, 0:moe.c], local[:],
             moe.owner[:], pos=flat(moe.pos[:]), valid=flat(valid[:]))
    experts(k, moe, xn_table, y_table, func)
    combine(k, moe, y_table, result, add_norm)


def build(nc, t, out):
    with ExitStack() as ctx:
        k = allocate(nc, ctx)
        table = nc.dram_tensor("conv_table", (TILES * P, D), F32, kind="Internal").ap()
        k.h = k.big[:, E0 * 2048 - TILES * D:].rearrange("p (t d) -> p t d", d=D)
        k.rows = k.big[:, E0 * 2048 - 2 * TILES * D:E0 * 2048 - TILES * D].rearrange("p (t d) -> p t d", d=D)
        xn_table = nc.dram_tensor("xn_table", (TILES * P, D), F32, kind="Internal").ap()
        y_table = nc.dram_tensor("y_table", (C0 * P, D), F32, kind="Internal").ap()
        gat_table = nc.dram_tensor("gat_table", (TILES * P, GW), F32, kind="Internal").ap()
        moe0, moe1 = (Moe(k, ctx, f"moe{n}", e, c, *(t[f"L{n}_ffn_{w}"] for w in ("gate_w", "gate_b", *names)))
                      for n, e, c, names in ((0, E0, C0, ("w1", "b1", "w2", "b2")), (1, E1, C1, ("W1", "b1", "W2", "b2"))))
        at = E1 * 2048
        y_all = k.big[:, at:at + TILES * D].rearrange("p (t d) -> p t d", d=D)
        at += TILES * D
        acc = k.big[:, at:at + TILES * (D + HEADS)].rearrange("p (t d) -> p t d", d=D + HEADS)
        at += TILES * (D + HEADS)
        gat_rows = k.big[:, at:at + TILES * GW].rearrange("p (t d) -> p t d", d=GW)
        at += TILES * GW
        w_all = k.big[:, at:at + 2 * GW].rearrange("p (h d) -> p h d", d=GW)
        prefetch(k, "weights0", [lambda sp: load_small(k, sp, moe0), lambda sp: load_small(k, sp, moe1),
                                 lambda sp: load_experts(k, sp, moe0, 0, EARLY)])
        room = k.big[:, E0 * 2048 - 2 * TILES * D:]
        with nc.sbuf_tensor("edge_src", [EP, EM], I32) as edge_src, nc.sbuf_tensor("edge_dst", [EP, EM], I32) as edge_dst:
            setup(k, t["x"], t["src"], t["dst"], edge_src, edge_dst)
            sort(k, "sort_dst", EP, EM, TILES, EC, edge_dst[:], edge_src[:], k.src_slot[:], k.src_local[:],
                 k.win_dst[:], degree=k.deg_in[:], room=room)
            sort(k, "sort_src", EP, EM, TILES, EC, edge_src[:], edge_dst[:], k.dst_slot[:], k.dst_local[:],
                 k.win_src[:], degree=k.deg_out[:], room=room)
        norms(k, "norms")
        moments(k, "ln0", k.x)
        for n in range(3):
            conv_dense(k, n, table, t[f"L0_gnn_W{n}"], t[f"L0_gnn_b{n - 1}"] if n else None)
            conv_sum(k, n, table)
        conv_finish(k, t["L0_gnn_b2"])
        recycle(k)
        prefetch(k, "rest0", [lambda sp: load_experts(k, sp, moe0, EARLY, E0)])
        mixture(k, moe0, xn_table, y_table, ACT.Relu, False, y_all, True)
        recycle(k)
        moments(k, "ln_y", y_all)
        add_scaled_norm(k, y_all, t["L0_ffn_gamma"], t["L0_ffn_beta"])
        moments(k, "ln2", k.x)
        gat_weights(k, t["L1_gnn_W"], t["L1_gnn_Wl"], t["L1_gnn_Wr"], w_all)
        norm_dense(k, "gat_dense", w_all, GW, gat_rows, table=gat_table, clear=acc)
        gat_sum(k, gat_table, gat_rows, acc, k.big[:, E1 * 2048:E1 * 2048 + TILES * D])
        gat_finish(k, acc, y_all, t["L1_gnn_b"])
        recycle(k)
        prefetch(k, "rest1", [lambda sp: load_experts(k, sp, moe1, 0, E1)])
        mixture(k, moe1, xn_table, y_table, ACT.Gelu, True, k.x[:], False)
        write_out(k, out)


def kernel(**inputs):
    import numpy as np
    import concourse.bacc as bacc
    from concourse.bass_utils import run_bass_kernel_spmd

    nc = bacc.Bacc("TRN2", target_bir_lowering=False, num_devices=1)
    arrays, aps = {}, {}
    for name, a in inputs.items():
        a = np.ascontiguousarray(a)
        arrays[f"in_{name}"] = a
        aps[name] = nc.dram_tensor(f"in_{name}", a.shape, mybir.dt.from_np(a.dtype), kind="ExternalInput").ap()
    out = nc.dram_tensor("out_x", (NODES, D), F32, kind="ExternalOutput").ap()
    build(nc, aps, out)
    result = run_bass_kernel_spmd(nc, [arrays], core_ids=[0])
    return result.results[0]["out_x"]
```

```python
from contextlib import ExitStack

import concourse.bass as bass
from concourse import mybir

F32 = mybir.dt.float32
F16 = mybir.dt.float16
I32 = mybir.dt.int32
U32 = mybir.dt.uint32
ALU = mybir.AluOpType
ACT = mybir.ActivationFunctionType
AX = mybir.AxisListType

P = 128
D = 256
NODES = 3125
TILES = -(-NODES // P)
LAST = NODES - (TILES - 1) * P
EDGES = 50000
EP = 125
EM = EDGES // EP
EC = (EDGES + TILES * (P - 1)) // P + 1
EC = -(-EC // 16) * 16
FF = 512
E0, E1 = 16, 8
HEADS, HD = 4, 64
PM = 2 * TILES
RING = 5
EPS_LN = 1e-5
ROWSUM_EPS = 1e-12
GW = HD + 2 * HEADS
assert EP * EM == EDGES and TILES % RING == 0 and EM % RING == 0 and PM % RING == 0


def expert_chunks(experts):
    n = (2 * NODES + experts * (P - 1)) // P
    return -(-n // 8) * 8


C0, C1 = expert_chunks(E0), expert_chunks(E1)


class Chain:

    def __init__(self, eng, sem):
        self.eng, self.sem, self.n, self.term = eng, sem, 0, None

    def __call__(self, ins):
        self.n += 1
        ins.then_inc(self.sem, 1)
        self.eng.wait_ge(self.sem, self.n if self.term is None else self.term + self.n)

    def loose(self, ins):
        self.n += 1
        ins.then_inc(self.sem, 1)
        self.eng.wait_ge(self.sem, self.n - 1 if self.term is None else self.term + (self.n - 1))

    def settle(self):
        self.eng.wait_ge(self.sem, self.n if self.term is None else self.term + self.n)

    def loop(self, count, per):
        start = self.n
        with self.eng.Fori(0, count) as i:
            self.term = i * per
            yield i
            assert self.n - start == per
            self.term = None
        self.n = start + count * per


def bank_free(r, banks=4):
    if r >= banks:
        return RING + r - banks + 1
    return 1 + max(x for x in range(RING) if x % banks == r)


class Kit:
    pass


def allocate(nc, ctx):
    k = Kit()
    k.nc = nc
    k.spent = []

    def sb(name, shape, dt=F32):
        return ctx.enter_context(nc.sbuf_tensor(name, shape, dt))

    k.sb = sb
    k.ident = sb("ident", [P, P])
    k.ones = sb("ones", [P, P])
    k.before = sb("before", [P, P])
    k.upto = sb("upto", [P, P])
    k.iota1 = sb("iota1", [P, P])
    k.iota_f = sb("iota_f", [P, EC])
    k.iota_h = sb("iota_h", [P, EC], F16)
    k.zero_h = sb("zero_h", [P, P], F16)
    k.x = sb("x_sb", [P, TILES, D])
    k.src_slot = sb("src_slot", [P, EC], I32)
    k.src_local = sb("src_local", [P, EC + 8])
    k.dst_slot = sb("dst_slot", [P, EC], I32)
    k.dst_local = sb("dst_local", [P, EC + 8])
    k.win_dst = sb("win_dst", [1, EC], I32)
    k.win_src = sb("win_src", [1, EC], I32)
    k.slot_low = sb("slot_low", [P, EC], I32)
    k.deg_in = sb("deg_in", [P, TILES])
    k.deg_out = sb("deg_out", [P, TILES])
    k.mean = sb("mean", [P, TILES])
    k.rstd = sb("rstd", [P, TILES])
    k.big = sb("big", [P, E0 * 2048])
    k.ps = ctx.enter_context(nc.psum_tensor("ps", [P, 8, 512], F32))
    return k


def phase(k, name):
    ctx = ExitStack()

    def sem(n):
        k.spent.append(k.nc.alloc_semaphore(f"{name}_{n}"))
        return k.spent[-1]

    sb = lambda n, s, d=F32: ctx.enter_context(k.nc.sbuf_tensor(f"{name}_{n}", s, d))
    return ctx, sem, sb


def recycle(k):
    k.nc.clear_and_free_semaphores(k.spent)
    k.nc.all_engine_barrier()
    k.spent = []


def setup(k, x, src, dst, edge_src, edge_dst):
    nc = k.nc
    ctx, sem, sb = phase(k, "setup")
    with ctx:
        loaded, made, cleared = sem("loaded"), sem("made"), sem("cleared")
        block = ctx.enter_context(nc.Block())

        @block.sync
        def _(sp):
            sp.dma_start(edge_src[:], src.rearrange("(p m) -> p m", p=EP)).then_inc(loaded, 16)
            sp.dma_start(edge_dst[:], dst.rearrange("(p m) -> p m", p=EP)).then_inc(loaded, 16)
            sp.dma_start(k.x[:, 0:TILES - 1, :],
                         x[0:(TILES - 1) * P, :].rearrange("(t p) d -> p t d", p=P)).then_inc(loaded, 16)
            sp.wait_ge(cleared, 1)
            sp.dma_start(k.x[0:LAST, TILES - 1, :], x[(TILES - 1) * P:NODES, :]).then_inc(loaded, 16)
            sp.wait_ge(loaded, 64)

        @block.vector
        def _(dve):
            dve.memset(k.x[:, TILES - 1, :], 0.0).then_inc(cleared, 1)
            dve.memset(k.zero_h[:], 0.0)
            dve.memset(k.src_local[:, EC:], 0.0)
            dve.memset(k.dst_local[:, EC:], 0.0)

        @block.gpsimd
        def _(pool):
            link = Chain(pool, made)
            link(pool.memset(k.ones[:], 1.0))
            link(pool.affine_select(out=k.ident[:], in_=k.ones[:], compare_op=ALU.is_equal, fill=0.0,
                                    base=0, pattern=[[-1, P]], channel_multiplier=1))
            link(pool.affine_select(out=k.before[:], in_=k.ones[:], compare_op=ALU.is_gt, fill=0.0,
                                    base=0, pattern=[[1, P]], channel_multiplier=-1))
            link(pool.affine_select(out=k.upto[:], in_=k.ones[:], compare_op=ALU.is_ge, fill=0.0,
                                    base=0, pattern=[[1, P]], channel_multiplier=-1))
            link(pool.iota(k.iota1[:], pattern=[[1, P]], base=1, channel_multiplier=0,
                           allow_small_or_imprecise_dtypes=True))
            link(pool.iota(k.iota_f[:], pattern=[[1, EC]], base=0, channel_multiplier=0,
                           allow_small_or_imprecise_dtypes=True))
            link(pool.iota(k.iota_h[:], pattern=[[1, EC]], base=0, channel_multiplier=0,
                           allow_small_or_imprecise_dtypes=True))


class Sort:

    def __init__(self, k, ctx, name, np_, m, buckets, c, key, node, slot, local, owner, pos=None, valid=None,
                 room=None, width=None):
        self.k, self.name, self.np_, self.m, self.buckets, self.c = k, name, np_, m, buckets, c
        self.key, self.node, self.slot, self.local, self.owner, self.pos, self.valid = key, node, slot, local, owner, pos, valid
        width = m if width is None else width
        self.width = width
        self.step = 5 if buckets % 5 == 0 else 8
        assert buckets % self.step == 0

        def sb(n, shape, dt=F32):
            return ctx.enter_context(k.nc.sbuf_tensor(f"{name}_{n}", shape, dt))

        def wide(n, dt=F32):
            if room is None:
                return sb(n, [P, width], dt)[0:np_, :]
            wide.at += width
            part = room[0:np_, wide.at - width:wide.at]
            return part if dt == F32 else part.bitcast(dt)

        wide.at = 0
        self.bucket, self.local1, self.part_a, self.part_b, self.chunk, self.lane = (
            wide(n) for n in ("bucket", "local1", "part_a", "part_b", "chunk", "lane"))
        at_mask = wide.at
        self.mask, self.count, self.acc, self.zero = (wide(n) for n in ("mask", "count", "acc", "zero"))
        self.int_a, self.int_b = wide("int_a", I32), wide("int_b", I32)
        self.cnt, self.pad, self.inc, self.base = (sb(n, [P, 32]) for n in ("cnt", "pad", "inc", "base"))
        self.pad_i = sb("pad_i", [P, 32], I32)
        self.tot_i, self.tot_f, self.ends = sb("tot_i", [32, 1], I32), sb("tot_f", [32, 1]), sb("ends", [32, 1])
        ps = k.ps
        self.slot_a, self.slot_b = ps[:, 6, 0:c], ps[:, 7, 0:c]
        self.pre, self.tot, self.tot_t = ps[0:np_, 3, 0:buckets], ps[0:np_, 3, 64:64 + buckets], ps[0:buckets, 3, 128:129]
        self.ends_ps, self.owner_ps = ps[0:buckets, 4, 0:1], ps[0:1, 5, 0:c]
        self.past = sb("past", [32, c]) if room is None else room[0:32, at_mask:at_mask + c]

    def signals(self, sem):
        self.scanned, self.counted, self.totals, self.tot_ready, self.ends_ready, self.past_ready, self.map_ready = (
            sem(n) for n in ("scanned", "counted", "totals", "tot_ready", "ends_ready", "past_ready", "map_ready"))

    def dve_keys(self, dve, link):
        k, m, buckets, c = self.k, self.m, self.buckets, self.c
        cut = slice(0, m)
        bucket, local1 = self.bucket[:, cut], self.local1[:, cut]
        int_a, int_b = self.int_a[:, cut], self.int_b[:, cut]
        if self.width > m:
            rest = slice(m, self.width)
            link(dve.memset(self.chunk[:, rest], -1.0))
            for a in (self.lane, self.part_a, self.part_b):
                link(dve.memset(a[:, rest], 0.0))
        link(dve.tensor_scalar(int_a, self.key, 7, None, ALU.logical_shift_right))
        link(dve.tensor_copy(bucket, int_a))
        link(dve.tensor_scalar(int_b, self.key, 127, None, ALU.bitwise_and))
        link(dve.tensor_scalar(local1, int_b, 1.0, None, ALU.add))
        if self.valid is not None:
            link(dve.scalar_tensor_tensor(bucket, bucket, 1.0, self.valid, ALU.add, ALU.mult))
            link(dve.tensor_scalar(bucket, bucket, -1.0, None, ALU.add))
        link(dve.tensor_scalar(int_a, self.node, 2, None, ALU.logical_shift_right))
        link(dve.tensor_copy(self.part_a[:, cut], int_a))
        link(dve.tensor_scalar(int_b, self.node, 3, 8, ALU.bitwise_and, ALU.logical_shift_left))
        link(dve.tensor_tensor(self.part_b[:, cut], int_b, local1, ALU.add))
        link(dve.memset(self.zero[:, cut], 0.0))
        link(dve.memset(self.acc[:, cut], 0.0))
        link(dve.memset(self.base[:], 0.0))
        step = self.step
        for i in link.loop(buckets // step, step):
            for r in range(step):
                mask = (self.mask, self.count)[r % 2][:, cut]
                link.loose(dve.tensor_scalar(mask, bucket, k.iota_f[0:self.np_, bass.ds(i * step + r, 1)], 0.0,
                                             ALU.is_equal, ALU.add, accum_out=self.cnt[0:self.np_, bass.ds(i * step + r, 1)]))
            link.settle()
        dve.sem_inc(self.counted, 1)
        q = slice(0, self.np_)
        dve.wait_ge(self.totals, 1)
        link(dve.tensor_scalar(self.pad_i[q, 0:buckets], self.tot, 127.0, None, ALU.add))
        link(dve.tensor_scalar(self.pad_i[q, 0:buckets], self.pad_i[q, 0:buckets], 7, 7,
                               ALU.logical_shift_right, ALU.logical_shift_left))
        link(dve.tensor_copy(self.pad[q, 0:buckets], self.pad_i[q, 0:buckets]))
        link(dve.tensor_tensor_scan(self.inc[q, 0:buckets], self.pad[q, 0:buckets], self.zero[:, 0:buckets], 0.0,
                                    ALU.add, ALU.add))
        link(dve.tensor_tensor(self.base[q, 0:buckets], self.inc[q, 0:buckets], self.pad[q, 0:buckets], ALU.subtract))
        link(dve.scalar_tensor_tensor(self.base[q, 0:buckets], self.pre, -1.0, self.base[q, 0:buckets], ALU.add, ALU.add))
        n = slice(0, buckets)
        link(dve.tensor_scalar(self.tot_i[n, :], self.tot_t, 127.0, None, ALU.add))
        link(dve.tensor_scalar(self.tot_i[n, :], self.tot_i[n, :], 7, None, ALU.logical_shift_right))
        dve.tensor_copy(self.tot_f[n, :], self.tot_i[n, :]).then_inc(self.tot_ready, 1)
        dve.wait_ge(self.ends_ready, 1)
        link(dve.tensor_copy(self.ends[n, :], self.ends_ps))
        dve.tensor_scalar(self.past[n, 0:c], k.iota_f[n, 0:c], self.ends[n, 0:1], None,
                          ALU.is_ge).then_inc(self.past_ready, 1)
        dve.wait_ge(self.map_ready, 1)
        link(dve.tensor_scalar(self.owner, self.owner_ps, float(buckets - 1), None, ALU.min))

    def pe_keys(self, pe):
        k, buckets = self.k, self.buckets
        pe.wait_ge(self.counted, 1)
        cnt, np_ = self.cnt[0:self.np_, 0:buckets], self.np_
        pe.matmul(self.pre, k.before[0:np_, 0:np_], cnt, start=True, stop=True)
        pe.matmul(self.tot, k.ones[0:np_, 0:np_], cnt, start=True, stop=True)
        pe.matmul(self.tot_t, cnt, k.ones[0:np_, 0:1], start=True, stop=True).then_inc(self.totals, 1)
        pe.wait_ge(self.tot_ready, 1)
        pe.matmul(self.ends_ps, k.upto[0:buckets, 0:buckets], self.tot_f[0:buckets, :], start=True,
                  stop=True).then_inc(self.ends_ready, 1)
        pe.wait_ge(self.past_ready, 1)
        pe.matmul(self.owner_ps, k.ones[0:buckets, 0:1], self.past[0:buckets, 0:self.c], start=True,
                  stop=True).then_inc(self.map_ready, 1)

    RANK_LINKS = 3

    def dve_rank(self, dve, link, b):
        cut, q = slice(0, self.m), slice(0, self.np_)
        mask, count = self.mask[:, cut], self.count[:, cut]
        link(dve.tensor_scalar(mask, self.bucket[:, cut], self.k.iota_f[q, bass.ds(b, 1)], None, ALU.is_equal))
        link(dve.tensor_tensor_scan(count, mask, self.zero[:, cut], self.base[q, bass.ds(b, 1)], ALU.add, ALU.add))
        dve.sem_inc(self.scanned, 1)
        link(dve.copy_predicated(self.acc[:, cut], mask.bitcast(I32), count))

    def dve_ranks(self, dve, link):
        cut, q, step = slice(0, self.m), slice(0, self.np_), self.step
        masks = [self.mask[:, cut], self.int_a[:, cut].bitcast(F32)]
        counts = [self.count[:, cut], self.int_b[:, cut].bitcast(F32)]
        for i in link.loop(self.buckets // step, 3 * step):
            def make_mask(r):
                link.loose(dve.tensor_scalar(masks[r % 2], self.bucket[:, cut], self.k.iota_f[q, bass.ds(i * step + r, 1)],
                                             None, ALU.is_equal))

            make_mask(0)
            link.settle()
            for r in range(step):
                link.loose(dve.tensor_tensor_scan(counts[r % 2], masks[r % 2], self.zero[:, cut],
                                                  self.base[q, bass.ds(i * step + r, 1)], ALU.add, ALU.add))
                if r + 1 < step:
                    make_mask(r + 1)
                else:
                    link.settle()
                dve.sem_inc(self.scanned, 1)
                link.loose(dve.copy_predicated(self.acc[:, cut], masks[r % 2].bitcast(I32), counts[r % 2]))
            link.settle()

    def dve_places(self, dve, link):
        cut = slice(0, self.m)
        where = self.int_a[:, cut] if self.pos is None else self.pos
        link(dve.tensor_copy(where, self.acc[:, cut]))
        link(dve.tensor_scalar(self.int_b[:, cut], where, 7, None, ALU.logical_shift_right))
        link(dve.tensor_copy(self.chunk[:, cut], self.int_b[:, cut]))
        link(dve.tensor_scalar(self.int_b[:, cut], where, 127, None, ALU.bitwise_and))
        link(dve.tensor_copy(self.lane[:, cut], self.int_b[:, cut]))
        if self.valid is not None:
            link(dve.scalar_tensor_tensor(self.chunk[:, cut], self.chunk[:, cut], 1.0, self.valid, ALU.add, ALU.mult))
            link(dve.tensor_scalar(self.chunk[:, cut], self.chunk[:, cut], -1.0, None, ALU.add))

    def dve_slots(self, dve, link):
        low = self.k.slot_low[:, 0:self.c]
        link(dve.tensor_copy(self.slot, self.slot_b))
        link(dve.tensor_scalar(low, self.slot, 255, None, ALU.bitwise_and))
        link(dve.tensor_copy(self.local, low))
        link(dve.tensor_scalar(self.slot, self.slot, 8, None, ALU.logical_shift_right))
        link(dve.scalar_tensor_tensor(self.slot, self.slot_a, 4.0, self.slot, ALU.mult, ALU.add))


def owners(k, eng, table, first, count, top):
    _, values = k.nc.values_load_multi_w_load_instructions(table[0:1, bass.ds(first, count)], engines=(eng.engine,),
                                                           min_val=0, max_val=top, skip_runtime_bounds_check_because=
                                                           "counts of chunks' ends passed, clamped to the last bucket")
    return values


class Columns:

    def __init__(self, k, sort, sem, sb, ring):
        self.k, self.s, self.ring = k, sort, ring
        self.lane_hot = sb("lane_hot", [P, ring, P], F16)
        self.lanes = sb("lanes", [P, ring, 2, P], F16)
        self.chunks = sb("chunks", [P, ring, sort.c], F16)
        self.lane_ready, self.parts_ready, self.chunk_ready, self.used = (
            sem(n) for n in ("lane_ready", "parts_ready", "chunk_ready", "used"))

    def dve(self, dve, i, r, ahead=0):
        s, q, col = self.s, slice(0, self.s.np_), bass.ds(i * self.ring + (self.at + r + ahead), 1)
        dve.wait_ge(self.used, i * self.ring + (r + ahead + 1))
        dve.tensor_scalar(self.lane_hot[q, r, :], self.k.iota_h[q, 0:P], s.lane[:, col], None,
                          ALU.is_equal).then_inc(self.lane_ready, 1)
        dve.tensor_scalar(self.chunks[q, r, :], self.k.iota_h[q, 0:s.c], s.chunk[:, col], None,
                          ALU.is_equal).then_inc(self.chunk_ready, 1)

    def act(self, act, i, r):
        s, q, col = self.s, slice(0, self.s.np_), bass.ds(i * self.ring + (self.at + r), 1)
        act.wait_ge(self.lane_ready, i * self.ring + (r + 1))
        act.activation(self.lanes[q, r, 0, :], self.lane_hot[q, r, :], ACT.Copy, scale=s.part_a[:, col])
        act.activation(self.lanes[q, r, 1, :], self.lane_hot[q, r, :], ACT.Copy,
                       scale=s.part_b[:, col]).then_inc(self.parts_ready, 1)

    def pe(self, pe, i, r):
        s, q = self.s, slice(0, self.s.np_)
        pe.wait_ge(self.chunk_ready, i * self.ring + (r + 1))
        pe.wait_ge(self.parts_ready, i * self.ring + (r + 1))
        pe.matmul(s.slot_a, self.lanes[q, r, 0, :], self.chunks[q, r, :], start=False, stop=False, skip_group_check=True)
        pe.matmul(s.slot_b, self.lanes[q, r, 1, :], self.chunks[q, r, :], start=False, stop=False,
                  skip_group_check=True).then_inc(self.used, 1)

    at = 0

    def pe_clear(self, pe, outs=()):
        for out in (self.s.slot_a, self.s.slot_b, *outs):
            pe.matmul(out, self.k.zero_h[:, :], self.k.iota_h[:, 0:out.shape[1]], start=True, stop=False,
                      skip_group_check=True)

    def pe_close(self, pe, outs=()):
        for out in (self.s.slot_a, self.s.slot_b, *outs):
            last = pe.matmul(out, self.k.zero_h[:, :], self.k.iota_h[:, 0:out.shape[1]], start=False, stop=True,
                             skip_group_check=True)
        return last


def sort_whole(k, s, batch, other=None, degree=None, spare=None):
    nc = k.nc
    ctx, sem, sb = phase(k, s.name + "_sort")
    with ctx:
        s.signals(sem)
        chain, placed = sem("chain"), sem("placed")
        hot_ready, chunks_ready, a_ready, b_ready, used = (
            sem(n) for n in ("hot_ready", "chunks_ready", "a_ready", "b_ready", "used"))
        lane_hot, chunks = sb("lane_hot", [P, 2, batch, P], F16), sb("chunks", [P, 2, batch, s.c], F16)
        both = sb("both", [P, 2, 2, batch, P], F16) if spare is None else (
            spare.bitcast(F16)[:, 0:4 * batch * P].rearrange("p (j h b n) -> p j h b n", j=2, h=2, b=batch))
        lane_a, lane_b = both[:, 0], both[:, 1]
        outs = [s.slot_a, s.slot_b]
        if other is not None:
            other.signals(lambda n: sem("other_" + n))
            hist_l = sb("hist_l", [P, 2, batch, P], F16)
            hist_w = k.hist_w[0:s.np_, :].rearrange("p (m w) -> p m w", w=TILES)
            hist = k.ps[:, 2, 0:TILES]
            outs.append(hist)
        q = slice(0, s.np_)
        turns = s.m // (2 * batch)
        assert s.m % (2 * batch) == 0
        block = ctx.enter_context(nc.Block())

        @block.vector
        def _(dve):
            link = Chain(dve, chain)
            s.dve_keys(dve, link)
            if other is not None:
                other.dve_keys(dve, link)
                wide = [s.np_, s.m, TILES]
                link(dve.tensor_scalar(other.local1[:, 0:s.m], other.local1[:, 0:s.m], -1.0, None, ALU.add))
                link(dve.tensor_tensor(hist_w, k.iota_h[q, 0:TILES].unsqueeze(1).to_broadcast(wide),
                                       other.bucket[:, 0:s.m].unsqueeze(2).to_broadcast(wide), ALU.is_equal))
            s.dve_ranks(dve, link)
            s.dve_places(dve, link)
            wide = [s.np_, batch, P]
            number = k.iota_h[q, 0:P].unsqueeze(1).to_broadcast(wide)
            with dve.Fori(0, turns) as i:
                for h in range(2):
                    cols = bass.ds(i * (2 * batch) + h * batch, batch)
                    dve.wait_ge(used, i * 2 + (h + 1))
                    dve.tensor_tensor(lane_hot[q, h], number, s.lane[:, cols].unsqueeze(2).to_broadcast(wide),
                                      ALU.is_equal).then_inc(hot_ready, 1)
                    if other is not None:
                        dve.tensor_tensor(hist_l[q, h], number, other.local1[:, cols].unsqueeze(2).to_broadcast(wide),
                                          ALU.is_equal)
                    for r in range(batch):
                        dve.tensor_scalar(chunks[q, h, r, :], k.iota_h[q, 0:s.c],
                                          s.chunk[:, bass.ds(i * (2 * batch) + (h * batch + r), 1)], None,
                                          ALU.is_equal).then_inc(chunks_ready, 1)
            dve.wait_ge(placed, 1)
            if other is not None:
                link(dve.tensor_scalar(degree, hist, 1.0, None, ALU.max))
            s.dve_slots(dve, link)

        @block.gpsimd
        def _(pool):
            wide = [s.np_, batch, P]
            with pool.Fori(0, turns) as i:
                for h in range(2):
                    part = s.part_b[:, bass.ds(i * (2 * batch) + h * batch, batch)]
                    pool.wait_ge(hot_ready, i * 2 + (h + 1))
                    pool.tensor_tensor(lane_b[q, h], lane_hot[q, h], part.unsqueeze(2).to_broadcast(wide),
                                       ALU.mult).then_inc(b_ready, 1)

        @block.scalar
        def _(act):
            with act.Fori(0, turns) as i:
                for h in range(2):
                    act.wait_ge(hot_ready, i * 2 + (h + 1))
                    for r in range(batch):
                        act.activation(lane_a[q, h, r, :], lane_hot[q, h, r, :], ACT.Copy,
                                       scale=s.part_a[:, bass.ds(i * (2 * batch) + (h * batch + r), 1)]).then_inc(a_ready, 1)

        @block.tensor
        def _(pe):
            pe.sem_inc(used, 2)
            s.pe_keys(pe)
            if other is not None:
                other.pe_keys(pe)
            for out in outs:
                pe.matmul(out, k.zero_h[:, :], k.iota_h[:, 0:out.shape[1]], start=True, stop=False, skip_group_check=True)
            with pe.Fori(0, turns) as i:
                for h in range(2):
                    pe.wait_ge(b_ready, i * 2 + (h + 1))
                    for r in range(batch):
                        n = i * (2 * batch) + (h * batch + r)
                        pe.wait_ge(chunks_ready, n + 1)
                        if other is not None:
                            pe.matmul(hist, hist_l[q, h, r, :], hist_w[:, bass.ds(n, 1), :], start=False, stop=False,
                                      skip_group_check=True)
                        pe.matmul(s.slot_b, lane_b[q, h, r, :], chunks[q, h, r, :], start=False, stop=False, skip_group_check=True)
                        pe.wait_ge(a_ready, n + 1)
                        last = pe.matmul(s.slot_a, lane_a[q, h, r, :], chunks[q, h, r, :], start=False, stop=False,
                                         skip_group_check=True)
                    last.then_inc(used, 1)
            for out in outs:
                last = pe.matmul(out, k.zero_h[:, :], k.iota_h[:, 0:out.shape[1]], start=False, stop=True,
                                 skip_group_check=True)
            last.then_inc(placed, 1)


def finish_sort(k, s):
    ctx, sem, sb = phase(k, s.name + "_finish")
    with ctx:
        chain = sem("chain")
        block = ctx.enter_context(k.nc.Block())

        @block.vector
        def _(dve):
            s.dve_slots(dve, Chain(dve, chain))


def root_degree(k, name, degree, counts=None, places=None):
    nc = k.nc
    ctx, sem, sb = phase(k, name)
    with ctx:
        chain, rooted, ready = sem("chain"), sem("rooted"), sem("ready")
        block = ctx.enter_context(nc.Block())

        @block.vector
        def _(dve):
            link = Chain(dve, chain)
            if counts is not None:
                link(dve.tensor_scalar(degree, counts, 1.0, None, ALU.max))
            dve.sem_inc(ready, 1)
            if places is not None:
                places.dve_places(dve, link)
            dve.wait_ge(rooted, 1)
            link(dve.reciprocal(degree, degree))

        @block.scalar
        def _(act):
            act.wait_ge(ready, 1)
            act.activation(degree, degree, ACT.Sqrt).then_inc(rooted, 1)


def moments(k, name, src):
    nc = k.nc
    ctx, sem, sb = phase(k, name)
    with ctx:
        stats, mv, var = sb("stats", [P, TILES, 6]), sb("mv", [P, TILES, 2]), sb("var", [P, TILES])
        chain, rooted = sem("chain"), sem("rooted")
        block = ctx.enter_context(nc.Block())

        @block.vector
        def _(dve):
            link = Chain(dve, chain)
            for t in range(TILES):
                dve.bn_stats(stats[:, t, :], src[:, t, :]).then_inc(chain, 1)
            dve.wait_ge(chain, TILES)
            link.n = TILES
            for t in range(TILES):
                dve.bn_aggr(mv[:, t, :], stats[:, t, :]).then_inc(chain, 1)
            link.n += TILES
            dve.wait_ge(chain, link.n)
            link(dve.tensor_copy(k.mean[:], mv[:, :, 0]))
            link(dve.tensor_scalar(var[:], mv[:, :, 1], EPS_LN, None, ALU.add))
            dve.wait_ge(rooted, 1)
            link(dve.reciprocal(k.rstd[:], var[:]))

        @block.scalar
        def _(act):
            act.wait_ge(chain, 2 * TILES + 2)
            act.activation(var[:], var[:], ACT.Sqrt).then_inc(rooted, 1)


def conv_dense(k, n, table, weight, bias_prev):
    nc, ps = k.nc, k.ps
    ctx, sem, sb = phase(k, f"dense{n}")
    with ctx:
        w = sb("w", [P, 2, D])
        bias = sb("bias", [P, D])
        act_in, act_out, turned = sb("act_in", [P, RING, D]), sb("act_out", [P, RING, D]), sb("turned", [P, RING, D])
        loaded, stored = sem("loaded"), sem("stored")
        in_ready, scaled, flipped, turned_back, multiplied, row_ready, cleared = (
            sem(x) for x in ("in_ready", "scaled", "flipped", "turned_back", "multiplied", "row_ready", "cleared"))
        flips, prods = [ps[:, r % 4, 0:D] for r in range(RING)], [ps[:, 4 + r % 2, 0:D] for r in range(RING)]
        block = ctx.enter_context(nc.Block())

        @block.sync
        def _(sp):
            sp.dma_start(w[:], weight.rearrange("(k p) n -> p k n", p=P)).then_inc(loaded, 16)
            if n:
                sp.dma_start(bias[:], bias_prev.partition_broadcast(P)).then_inc(loaded, 16)
            with sp.Fori(0, TILES) as t:
                sp.wait_ge(row_ready, t + (1 + RING))
                sp.dma_start(table[bass.ds(t * P, P), :], k.rows[:, bass.ds(t, 1), :]).then_inc(stored, 16)
            sp.wait_ge(stored, 16 * TILES)

        @block.vector
        def _(dve):
            dve.sem_inc(turned_back, RING)
            if n:
                dve.wait_ge(loaded, 32)
            with dve.Fori(0, TILES // RING) as i:
                for r in range(RING):
                    t = bass.ds(i * RING + r, 1)
                    dve.wait_ge(scaled, i * RING + (r + 1))
                    if n == 0:
                        dve.tensor_scalar(act_in[:, r, :], k.x[:, t, :], k.mean[:, t], k.rstd[:, t],
                                          ALU.subtract, ALU.mult).then_inc(in_ready, 1)
                    else:
                        dve.scalar_tensor_tensor(act_in[:, r, :], k.h[:, t, 0:D], k.deg_in[:, t], bias[:],
                                                 ALU.mult, ALU.add).then_inc(in_ready, 1)
                for r in range(RING):
                    dve.wait_ge(flipped, i * RING + (r + 1 + RING))
                    dve.wait_ge(multiplied, i * RING + (r + 1))
                    dve.tensor_copy(turned[:, r, :], flips[r]).then_inc(turned_back, 1)
            dve.wait_ge(in_ready, TILES)
            dve.memset(k.h, 0.0).then_inc(cleared, 1)

        @block.scalar
        def _(act):
            act.sem_inc(scaled, RING)
            act.sem_inc(row_ready, RING)
            with act.Fori(0, TILES // RING) as i:
                for r in range(RING):
                    t = bass.ds(i * RING + r, 1)
                    act.wait_ge(in_ready, i * RING + (r + 1))
                    act.wait_ge(flipped, i * RING + (r + 1))
                    act.activation(act_out[:, r, :], act_in[:, r, :], ACT.Relu if n else ACT.Copy,
                                   scale=k.deg_out[:, t]).then_inc(scaled, 1)
                for r in range(RING):
                    act.wait_ge(multiplied, i * RING + (r + 1 + RING))
                    act.copy(k.rows[:, bass.ds(i * RING + r, 1), :], prods[r]).then_inc(row_ready, 1)

        @block.tensor
        def _(pe):
            pe.sem_inc(flipped, RING)
            pe.sem_inc(multiplied, RING)
            pe.wait_ge(loaded, 32 if n else 16)
            with pe.Fori(0, TILES // RING) as i:
                for r in range(RING):
                    pe.wait_ge(scaled, i * RING + (r + 1 + RING))
                    pe.wait_ge(turned_back, i * RING + bank_free(r))
                    for half in range(2):
                        last = pe.transpose(flips[r][:, half * P:(half + 1) * P],
                                            act_out[:, r, half * P:(half + 1) * P], k.ident[:])
                    last.then_inc(flipped, 1)
                for r in range(RING):
                    pe.wait_ge(turned_back, i * RING + (r + 1 + RING))
                    pe.wait_ge(row_ready, i * RING + bank_free(r, 2))
                    for half in range(2):
                        last = pe.matmul(prods[r], turned[:, r, half * P:(half + 1) * P], w[:, half, :],
                                         start=(half == 0), stop=(half == 1))
                    last.then_inc(multiplied, 1)


def conv_sum(k, n, table, side):
    nc, ps = k.nc, k.ps
    ctx, sem, sb = phase(k, f"sum{n}")
    with ctx:
        G, HALF, BANKS = 16, 8, 4
        W = D + 1
        msg = k.rows_room[:, 0:G * W].rearrange("p (g w) -> p g w", w=W)
        hot = k.rows_room[:, G * W:G * (W + P)].rearrange("p (g w) -> p g w", w=P)
        idx = sb("idx", [P, G], I32)
        idx_ready, hot_ready, summed, added, issued, ones_ready = (
            sem(x) for x in ("idx_ready", "hot_ready", "summed", "added", "issued", "ones_ready"))
        gathered = [sem(f"gathered{r}") for r in range(G)]
        sums = [ps[:, r % BANKS, 0:W] for r in range(G)]
        turns = EC // G
        assert side.width == HALF * 2 * turns + HALF // 2 and TILES <= turns
        columns = None
        if n:
            columns = Columns(k, side, sem, sb, HALF)
            columns.at = (n - 1) * HALF * turns
        chain = sem("chain")
        block = ctx.enter_context(nc.Block())

        @block.scalar
        def _(act):
            with act.Fori(0, turns) as i:
                for r in range(G):
                    act.wait_ge(summed, i * G + (r + 1))
                    act.copy(idx[:, r:r + 1], k.src_slot[:, bass.ds(i * G + r, 1)]).then_inc(idx_ready, 1)
                    if n and r % 2:
                        columns.act(act, i, r // 2)

        @block.gpsimd
        def _(pool):
            with pool.Fori(0, turns) as i:
                for r in range(G):
                    pool.wait_ge(idx_ready, i * G + (r + 1))
                    pool.sem_inc(issued, 1)
                    pool.indirect_dma_start(out=msg[:, r, 0:D], out_offset=None, in_=table[:, :],
                                            in_offset=bass.IndirectOffsetOnAxis(ap=idx[:, r:r + 1], axis=0)
                                            ).then_inc(gathered[r], 16)

        @block.vector
        def _(dve):
            def make_hot(i, r, more=0):
                dve.wait_ge(summed, i * G + (r + more + 1))
                dve.tensor_scalar(hot[:, r, :], k.iota1[:], k.src_local[:, bass.ds(i * G + (r + more), 1)], None,
                                  ALU.is_equal).then_inc(hot_ready, 1)

            def add(i, r, window):
                here = k.h[:, bass.ds(window, 1), :]
                dve.wait_ge(summed, i * G + (r + 1 + G))
                dve.wait_ge(added, i * G + (r + BANKS))
                dve.tensor_tensor(here, here, sums[r], ALU.add).then_inc(added, 1)

            dve.sem_inc(added, BANKS)
            dve.memset(msg[:, :, D:W], 1.0).then_inc(ones_ready, 1)
            link = Chain(dve, chain)
            for r in range(HALF):
                dve.wait_ge(summed, r + 1)
                dve.tensor_scalar(hot[:, r, :], k.iota1[:], k.src_local[:, r:r + 1], None, ALU.is_equal).then_inc(hot_ready, 1)
                if n and r % 2:
                    columns.dve(dve, 0, r // 2)
            for i in link.loop(turns, 0 if n else side.RANK_LINKS):
                windows = owners(k, dve, k.win_dst, i * G, G, TILES - 1)
                for r in range(HALF):
                    make_hot(i, r + HALF)
                    if n and r % 2:
                        columns.dve(dve, i, (HALF + r) // 2)
                    add(i, r, windows[r])
                if not n:
                    side.dve_rank(dve, link, i)
                for r in range(HALF):
                    make_hot(i, r, G)
                    if n and r % 2:
                        columns.dve(dve, i, r // 2, HALF)
                    add(i, r + HALF, windows[r + HALF])

        @block.tensor
        def _(pe):
            pe.sem_inc(summed, G)
            if n:
                pe.sem_inc(columns.used, HALF)
            if n == 1:
                columns.pe_clear(pe)
            pe.wait_ge(ones_ready, 1)
            with pe.Fori(0, turns) as i:
                for r in range(G):
                    pe.wait_ge(hot_ready, i * G + (r + 1))
                    pe.wait_ge(added, i * G + (r + 1))
                    pe.wait_ge(gathered[r], i * 16 + 16)
                    pe.matmul(sums[r], hot[:, r, :], msg[:, r, :], start=True, stop=True).then_inc(summed, 1)
                    if n and r % 2:
                        columns.pe(pe, i, r // 2)
            if n == 2:
                columns.pe_close(pe)


def conv_finish(k, bias_last):
    nc = k.nc
    ctx, sem, sb = phase(k, "finish")
    with ctx:
        bias = sb("bias", [P, D])
        loaded, chain = sem("loaded"), sem("chain")
        block = ctx.enter_context(nc.Block())

        @block.sync
        def _(sp):
            sp.dma_start(bias[:], bias_last.partition_broadcast(P)).then_inc(loaded, 16)

        @block.vector
        def _(dve):
            dve.wait_ge(loaded, 16)
            bias_all = bias[:].unsqueeze(1).to_broadcast([P, TILES, D])
            link = Chain(dve, chain)
            link(dve.tensor_tensor(k.x[:], k.x[:], bias_all, ALU.add))
            with dve.Fori(0, TILES) as t:
                here = k.x[:, bass.ds(t, 1), :]
                dve.scalar_tensor_tensor(here, k.h[:, bass.ds(t, 1), 0:D], k.deg_in[:, bass.ds(t, 1)], here,
                                         ALU.mult, ALU.add).then_inc(chain, 1)
            dve.wait_ge(chain, 1 + TILES)


def norm_dense(k, name, weight, width, result, table=None, xn_table=None, clear=None):
    nc, ps = k.nc, k.ps
    ctx, sem, sb = phase(k, name)
    with ctx:
        xn, turned = sb("xn", [P, RING, D]), sb("turned", [P, RING, D])
        xn_ready, kept, flipped, turned_back, multiplied, row_ready, stored, cleared = (
            sem(x) for x in ("xn_ready", "kept", "flipped", "turned_back", "multiplied", "row_ready", "stored", "cleared"))
        xn_stored = [sem(f"xn_stored{r}") for r in range(RING)]
        flips, prods = [ps[:, r % 4, 0:D] for r in range(RING)], [ps[:, 4 + r % 4, 0:width] for r in range(RING)]
        block = ctx.enter_context(nc.Block())

        if xn_table is not None:
            @block.sync
            def _(sp):
                sp.sem_inc(kept, RING)
                with sp.Fori(0, TILES // RING) as i:
                    for r in range(RING):
                        sp.wait_ge(xn_ready, i * RING + (r + 1))
                        sp.dma_start(xn_table[bass.ds((i * RING + r) * P, P), :], xn[:, r, :]).then_inc(xn_stored[r], 16)
                    for r in range(RING):
                        sp.wait_ge(xn_stored[r], i * 16 + 16)
                        sp.sem_inc(kept, 1)

        if table is not None:
            @block.sync
            def _(sp):
                with sp.Fori(0, TILES) as t:
                    sp.wait_ge(row_ready, t + (1 + RING))
                    sp.dma_start(table[bass.ds(t * P, P), :], result[:, bass.ds(t, 1), :]).then_inc(stored, 16)
                sp.wait_ge(stored, 16 * TILES)

        @block.vector
        def _(dve):
            dve.sem_inc(turned_back, RING)
            with dve.Fori(0, TILES // RING) as i:
                for r in range(RING):
                    t = bass.ds(i * RING + r, 1)
                    dve.wait_ge(flipped, i * RING + (r + 1))
                    if xn_table is not None:
                        dve.wait_ge(kept, i * RING + (r + 1))
                    dve.tensor_scalar(xn[:, r, :], k.x[:, t, :], k.mean[:, t], k.rstd[:, t],
                                      ALU.subtract, ALU.mult).then_inc(xn_ready, 1)
                for r in range(RING):
                    dve.wait_ge(flipped, i * RING + (r + 1 + RING))
                    dve.wait_ge(multiplied, i * RING + (r + 1))
                    dve.tensor_copy(turned[:, r, :], flips[r]).then_inc(turned_back, 1)
            if clear is not None:
                dve.memset(clear, 0.0).then_inc(cleared, 1)

        @block.scalar
        def _(act):
            act.sem_inc(row_ready, RING)
            with act.Fori(0, TILES // RING) as i:
                for r in range(RING):
                    act.wait_ge(multiplied, i * RING + (r + 1 + RING))
                    act.copy(result[:, bass.ds(i * RING + r, 1), :], prods[r]).then_inc(row_ready, 1)

        @block.tensor
        def _(pe):
            pe.sem_inc(flipped, RING)
            pe.sem_inc(multiplied, RING)
            with pe.Fori(0, TILES // RING) as i:
                for r in range(RING):
                    pe.wait_ge(xn_ready, i * RING + (r + 1))
                    pe.wait_ge(turned_back, i * RING + bank_free(r))
                    for half in range(2):
                        last = pe.transpose(flips[r][:, half * P:(half + 1) * P],
                                            xn[:, r, half * P:(half + 1) * P], k.ident[:])
                    last.then_inc(flipped, 1)
                for r in range(RING):
                    pe.wait_ge(turned_back, i * RING + (r + 1 + RING))
                    pe.wait_ge(row_ready, i * RING + bank_free(r))
                    for half in range(2):
                        last = pe.matmul(prods[r], turned[:, r, half * P:(half + 1) * P], weight[:, half, :],
                                         start=(half == 0), stop=(half == 1))
                    last.then_inc(multiplied, 1)


class Moe:

    def __init__(self, k, ctx, name, experts, chunks, gate_w, gate_b, w1, b1, w2, b2):
        sb = lambda n, s, d=F32: ctx.enter_context(k.nc.sbuf_tensor(f"{name}_{n}", s, d))
        self.name, self.e, self.c = name, experts, chunks
        self.gate_w, self.gate_b, self.w1, self.b1, self.w2, self.b2 = gate_w, gate_b, w1, b1, w2, b2
        self.gate = sb("gate", [P, 2, experts])
        self.gate_bias = sb("gate_bias", [P, experts])
        self.score = sb("score", [P, TILES, experts])
        self.b1_t = sb("b1_t", [P, experts, FF // P])
        self.b2_sb = sb("b2_sb", [experts, D])
        self.weight = sb("weight", [P, TILES, 2])
        self.combine = sb("combine", [P, TILES, experts])
        self.slot = sb("slot", [P, chunks + 8], I32)
        self.pos = sb("pos", [P, TILES, 2], I32)
        self.owner = sb("owner", [1, chunks + 8], I32)
        self.small = ctx.enter_context(k.nc.semaphore(f"{name}_small"))
        self.loads = 0
        self.big = ctx.enter_context(k.nc.semaphore(f"{name}_big"))


def load_experts(k, eng, moe, which, first, last):
    dram, n = ((moe.w1, FF), (moe.w2, D))[which]
    for e in range(first, last, 4):
        end = min(e + 4, last)
        here = k.big[:, (which * moe.e + e) * 1024:(which * moe.e + end) * 1024]
        eng.dma_start(here.rearrange("p (m n) -> p m n", n=n),
                      dram[e:end, :, :].rearrange("e (k p) n -> p (e k) n", p=P)).then_inc(moe.big, 16)
        moe.loads += 16


def load_small(k, eng, moe):
    with k.nc.allow_non_contiguous_dma(reason="the bias of a hidden unit goes to the unit's partition"):
        eng.dma_start(moe.gate[:], moe.gate_w.rearrange("(k p) e -> p k e", p=P)).then_inc(moe.small, 16)
        eng.dma_start(moe.gate_bias[:], moe.gate_b.partition_broadcast(P)).then_inc(moe.small, 16)
        eng.dma_start(moe.b1_t[:].rearrange("p e f -> p (e f)"),
                      moe.b1.rearrange("e (f p) -> p (e f)", p=P)).then_inc(moe.small, 16)
        eng.dma_start(moe.b2_sb[:], moe.b2[:, :]).then_inc(moe.small, 16)


SMALL_LOADS = 64


def prefetch(k, name, jobs):
    ctx, sem, sb = phase(k, name)
    with ctx:
        block = ctx.enter_context(k.nc.Block())

        @block.sync
        def _(sp):
            for job in jobs:
                job(sp)


def choose(k, moe, softmax_first, key, node, valid):
    nc = k.nc
    e = moe.e
    ctx, sem, sb = phase(k, moe.name + "_choose")
    with ctx:
        top, which = sb("top", [P, TILES, 8]), sb("which", [P, TILES, 8], U32)
        ids, tmp, peak, node_f = sb("ids", [P, TILES, 2]), sb("tmp", [P, TILES, e]), sb("peak", [P, TILES]), sb("node_f", [P, TILES, 2])
        chain, numbered, ready, powered = sem("chain"), sem("numbered"), sem("ready"), sem("powered")
        block = ctx.enter_context(nc.Block())
        wide = [P, TILES, e]

        @block.gpsimd
        def _(pool):
            pool.iota(node, pattern=[[P, TILES], [0, 2]], base=0, channel_multiplier=1).then_inc(numbered, 1)

        @block.scalar
        def _(act):
            act.wait_ge(ready, 1)
            if softmax_first:
                act.activation(moe.score[:], moe.score[:], ACT.Exp).then_inc(powered, 1)
            else:
                act.activation(moe.weight[:, :, 1], moe.weight[:, :, 1], ACT.Exp).then_inc(powered, 1)

        @block.vector
        def _(dve):
            link = Chain(dve, chain)
            score = moe.score[:]
            link(dve.memset(moe.slot[:, moe.c:], 0))
            link(dve.memset(moe.owner[:, moe.c:], 0))
            dve.wait_ge(moe.small, SMALL_LOADS)
            link(dve.tensor_tensor(score, score, moe.gate_bias[:].unsqueeze(1).to_broadcast(wide), ALU.add))
            if softmax_first:
                link(dve.tensor_reduce(peak[:], score, AX.X, ALU.max))
                dve.tensor_tensor(score, score, peak[:].unsqueeze(2).to_broadcast(wide), ALU.subtract).then_inc(ready, 1)
                dve.wait_ge(powered, 1)
                link(dve.tensor_reduce(peak[:], score, AX.X, ALU.add))
                link(dve.reciprocal(peak[:], peak[:]))
                link(dve.tensor_tensor(score, score, peak[:].unsqueeze(2).to_broadcast(wide), ALU.mult))
            for t in range(TILES):
                dve.max(top[:, t, :], moe.score[:, t, :]).then_inc(chain, 1)
            link.n += TILES
            dve.wait_ge(chain, link.n)
            for t in range(TILES):
                dve.max_index(which[:, t, :], top[:, t, :], moe.score[:, t, :]).then_inc(chain, 1)
            link.n += TILES
            dve.wait_ge(chain, link.n)
            link(dve.tensor_copy(ids[:], which[:, :, 0:2]))
            if softmax_first:
                link(dve.tensor_copy(moe.weight[:], top[:, :, 0:2]))
            else:
                dve.tensor_tensor(moe.weight[:, :, 1], top[:, :, 1], top[:, :, 0], ALU.subtract).then_inc(ready, 1)
                dve.wait_ge(powered, 1)
                link(dve.tensor_scalar(peak[:], moe.weight[:, :, 1], 1.0, None, ALU.add))
                link(dve.reciprocal(moe.weight[:, :, 0], peak[:]))
                link(dve.tensor_tensor(moe.weight[:, :, 1], moe.weight[:, :, 1], moe.weight[:, :, 0], ALU.mult))
            number = k.iota_f[:, 0:e].unsqueeze(1).to_broadcast(wide)
            for j in range(2):
                out = moe.combine[:] if j == 0 else tmp[:]
                link(dve.tensor_tensor(out, number, ids[:, :, j:j + 1].to_broadcast(wide), ALU.is_equal))
                link(dve.tensor_tensor(out, out, moe.weight[:, :, j:j + 1].to_broadcast(wide), ALU.mult))
            link(dve.tensor_tensor(moe.combine[:], moe.combine[:], tmp[:], ALU.add))
            link(dve.tensor_scalar(key, ids[:], 128.0, None, ALU.mult))
            dve.wait_ge(numbered, 1)
            link(dve.tensor_copy(node_f[:], node))
            link(dve.tensor_scalar(valid, node_f[:], float(NODES), None, ALU.is_lt))


def experts(k, moe, xn_table, y_table, func):
    nc, ps = k.nc, k.ps
    ctx, sem, sb = phase(k, moe.name + "_experts")
    with ctx:
        U, Y = 8, 4
        KD, KF = D // P, FF // P
        rows, idx = sb("rows", [P, U, D]), sb("idx", [P, U], I32)
        x_t, hid_t, y = sb("x_t", [P, 2, D]), sb("hid_t", [P, 2, FF]), sb("y", [P, Y, D])
        w1 = sb("w1", [P, 2, KD * FF])
        idx_ready, issued, flip_x, x_back, w1_ready, up, acted, down, y_ready, kept = (
            sem(n) for n in ("idx_ready", "issued", "flip_x", "x_back", "w1_ready", "up", "acted", "down", "y_ready", "kept"))
        gathered, stored = [sem(f"gathered{r}") for r in range(U)], [sem(f"stored{r}") for r in range(U)]
        all_w1, all_w2 = (k.big[:, j * moe.e * 1024:(j + 1) * moe.e * 1024].rearrange("p (e w) -> p e w", w=1024)
                          for j in range(2))
        turns = moe.c // U
        assert moe.c % U == 0
        block = ctx.enter_context(nc.Block())

        @block.sync
        def _(sp):
            sp.sem_inc(kept, Y)
            with sp.Fori(0, turns) as i:
                for r in range(U):
                    sp.wait_ge(y_ready, i * U + (r + 1 + 2))
                    sp.dma_start(y_table[bass.ds((i * U + r) * P, P), :], y[:, r % Y, :]).then_inc(stored[r], 16)
                    if r >= 2:
                        sp.wait_ge(stored[r - 2], i * 16 + 16)
                        sp.sem_inc(kept, 1)
                for r in range(U - 2, U):
                    sp.wait_ge(stored[r], i * 16 + 16)
                    sp.sem_inc(kept, 1)

        @block.gpsimd
        def _(pool):
            with pool.Fori(0, turns) as i:
                for r in range(U):
                    pool.wait_ge(idx_ready, i * U + (r + 1))
                    pool.sem_inc(issued, 1)
                    pool.indirect_dma_start(out=rows[:, r, :], out_offset=None, in_=xn_table[:, :],
                                            in_offset=bass.IndirectOffsetOnAxis(ap=idx[:, r:r + 1], axis=0)
                                            ).then_inc(gathered[r], 16)
            for r in range(2):
                pool.wait_ge(idx_ready, moe.c + (r + 1))
                pool.sem_inc(issued, 1)
                pool.indirect_dma_start(out=rows[:, r, :], out_offset=None, in_=xn_table[:, :],
                                        in_offset=bass.IndirectOffsetOnAxis(ap=idx[:, r:r + 1], axis=0)
                                        ).then_inc(gathered[r], 16)

        @block.scalar
        def _(act):
            act.sem_inc(acted, 2)
            act.wait_ge(moe.small, SMALL_LOADS)
            act.copy(idx[:], moe.slot[:, 0:U]).then_inc(idx_ready, U)
            with act.Fori(0, turns) as i:
                mine = owners(k, act, moe.owner, i * U, U, moe.e - 1)
                for r in range(U):
                    act.wait_ge(up, i * U + (r + 1 + 2))
                    act.wait_ge(down, i * U + (r + 1))
                    for f in range(KF):
                        last = act.activation(hid_t[:, r % 2, f * P:(f + 1) * P], ps[:, 4 + r % 2, f * P:(f + 1) * P], func,
                                              bias=moe.b1_t[:, bass.ds(mine[r], 1), f])
                    last.then_inc(acted, 1)
                    act.wait_ge(flip_x, i * U + (r + 1 + U))
                    act.copy(idx[:, r:r + 1], moe.slot[:, bass.ds(i * U + (r + U), 1)]).then_inc(idx_ready, 1)

        @block.vector
        def _(dve):
            dve.sem_inc(x_back, 2)
            dve.sem_inc(w1_ready, 2)
            dve.sem_inc(y_ready, 2)
            dve.wait_ge(moe.big, moe.loads)

            def keep_x(i, r):
                dve.wait_ge(flip_x, i * U + (r + 1 + U))
                dve.wait_ge(up, i * U + (r + 1))
                dve.tensor_copy(x_t[:, r % 2, :], ps[:, r % 2, 0:D]).then_inc(x_back, 1)

            def keep_w1(i, r, e):
                dve.wait_ge(up, i * U + (r + 1))
                dve.tensor_copy(w1[:, r % 2, :], all_w1[:, bass.ds(e, 1), :]).then_inc(w1_ready, 1)

            first = owners(k, dve, moe.owner, 0, 2, moe.e - 1)
            for r in range(2):
                keep_x(0, r)
                keep_w1(0, r, first[r])
            with dve.Fori(0, turns) as i:
                mine = owners(k, dve, moe.owner, i * U + 2, U, moe.e - 1)
                for pair in range(0, U, 2):
                    for r in (pair, pair + 1):
                        keep_w1(i, r + 2, mine[r])
                    for r in (pair, pair + 1):
                        keep_x(i, r + 2)
                    for r in (pair, pair + 1):
                        dve.wait_ge(down, i * U + (r + 1 + 2))
                        dve.wait_ge(kept, i * U + (r + 1))
                        dve.tensor_copy(y[:, r % Y, :], ps[:, 6 + r % 2, 0:D]).then_inc(y_ready, 1)

        @block.tensor
        def _(pe):
            pe.sem_inc(flip_x, U)
            pe.sem_inc(up, 2)
            pe.sem_inc(down, 2)

            def transpose_x(i, r):
                pe.wait_ge(x_back, i * U + (r + 1))
                pe.wait_ge(gathered[r % U], i * 16 + (16 + r // U * 16))
                for h in range(KD):
                    last = pe.transpose(ps[:, r % 2, h * P:(h + 1) * P], rows[:, r % U, h * P:(h + 1) * P], k.ident[:])
                last.then_inc(flip_x, 1)

            transpose_x(0, 0)
            transpose_x(0, 1)
            pe.wait_ge(moe.big, moe.loads)
            with pe.Fori(0, turns) as i:
                mine = owners(k, pe, moe.owner, i * U, U, moe.e - 1)
                for pair in range(0, U, 2):
                    for r in (pair, pair + 1):
                        pe.wait_ge(x_back, i * U + (r + 1 + 2))
                        pe.wait_ge(w1_ready, i * U + (r + 1 + 2))
                        pe.wait_ge(acted, i * U + (r + 1))
                        for f in range(KF):
                            for h in range(KD):
                                last = pe.matmul(ps[:, 4 + r % 2, f * P:(f + 1) * P],
                                                 w1[:, r % 2, h * FF + f * P:h * FF + (f + 1) * P],
                                                 x_t[:, r % 2, h * P:(h + 1) * P], start=(h == 0), stop=(h == KD - 1))
                        last.then_inc(up, 1)
                    for r in (pair, pair + 1):
                        transpose_x(i, r + 2)
                    for r in (pair, pair + 1):
                        w2 = all_w2[:, bass.ds(mine[r], 1), :]
                        pe.wait_ge(acted, i * U + (r + 1 + 2))
                        pe.wait_ge(y_ready, i * U + (r + 1))
                        for f in range(KF):
                            last = pe.matmul(ps[:, 6 + r % 2, 0:D], hid_t[:, r % 2, f * P:(f + 1) * P],
                                             w2[:, :, f * D:(f + 1) * D],
                                             start=(f == 0), stop=(f == KF - 1))
                        last.then_inc(down, 1)


def combine(k, moe, y_table, result, add_norm):
    nc, ps = k.nc, k.ps
    e = moe.e
    ctx, sem, sb = phase(k, moe.name + "_combine")
    with ctx:
        got, idx = sb("got", [P, RING, 2, D]), sb("idx", [P, RING, 2], I32)
        cw, cw_t, part = sb("cw", [P, RING, e]), sb("cw_t", [e, RING, P]), sb("part", [P, RING, D])
        idx_ready, issued, cw_ready, flipped, cw_back, biased, summed, chain = (
            sem(n) for n in ("idx_ready", "issued", "cw_ready", "flipped", "cw_back", "biased", "summed", "chain"))
        gathered = [sem(f"gathered{r}") for r in range(RING)]
        block = ctx.enter_context(nc.Block())
        pos, weight = moe.pos[:], moe.weight[:].rearrange("p t j -> p (t j)")

        @block.scalar
        def _(act):
            act.sem_inc(cw_back, RING)
            with act.Fori(0, TILES // RING) as i:
                for r in range(RING):
                    t = bass.ds(i * RING + r, 1)
                    act.wait_ge(summed, i * RING + (r + 1))
                    act.copy(idx[:, r, :], pos[:, t, :]).then_inc(idx_ready, 1)
                    act.wait_ge(flipped, i * RING + (r + 1))
                    act.copy(cw[:, r, :], moe.combine[:, t, :]).then_inc(cw_ready, 1)
                for r in range(RING):
                    act.wait_ge(flipped, i * RING + (r + 1 + RING))
                    act.wait_ge(biased, i * RING + (r + 1))
                    act.copy(cw_t[:, r, :], ps[0:e, r % 4, 0:P]).then_inc(cw_back, 1)

        @block.gpsimd
        def _(pool):
            with pool.Fori(0, TILES // RING) as i:
                for r in range(RING):
                    pool.wait_ge(idx_ready, i * RING + (r + 1))
                    pool.sem_inc(issued, 1)
                    for j in range(2):
                        pool.indirect_dma_start(out=got[:, r, j, :], out_offset=None, in_=y_table[:, :],
                                                in_offset=bass.IndirectOffsetOnAxis(ap=idx[:, r, j:j + 1], axis=0)
                                                ).then_inc(gathered[r], 16)

        @block.tensor
        def _(pe):
            pe.sem_inc(flipped, RING)
            pe.sem_inc(biased, RING)
            with pe.Fori(0, TILES // RING) as i:
                for r in range(RING):
                    pe.wait_ge(cw_ready, i * RING + (r + 1))
                    pe.wait_ge(cw_back, i * RING + bank_free(r))
                    pe.transpose(ps[0:e, r % 4, 0:P], cw[:, r, :], k.ident[:]).then_inc(flipped, 1)
                for r in range(RING):
                    pe.wait_ge(cw_back, i * RING + (r + 1 + RING))
                    pe.wait_ge(summed, i * RING + bank_free(r))
                    pe.matmul(ps[:, 4 + r % 4, 0:D], cw_t[:, r, :], moe.b2_sb[:], start=True, stop=True).then_inc(biased, 1)

        @block.vector
        def _(dve):
            dve.sem_inc(summed, RING)
            link = Chain(dve, chain)
            for i in link.loop(TILES // RING, RING * (3 if add_norm else 2)):
                for r in range(RING):
                    t = bass.ds(i * RING + r, 1)
                    base = k.x[:, t, :]
                    if add_norm:
                        link(dve.tensor_scalar(part[:, r, :], base, k.mean[:, t], k.rstd[:, t], ALU.subtract, ALU.mult))
                        base = part[:, r, :]
                    dve.wait_ge(biased, i * RING + (r + 1 + RING))
                    link(dve.tensor_tensor(part[:, r, :], base, ps[:, 4 + r % 4, 0:D], ALU.add))
                    dve.wait_ge(gathered[r], i * 32 + 32)
                    w = [weight[:, bass.ds((i * RING + r) * 2 + j, 1)] for j in range(2)]
                    link(dve.scalar_tensor_tensor(part[:, r, :], got[:, r, 0, :], w[0], part[:, r, :], ALU.mult, ALU.add))
                    dve.scalar_tensor_tensor(result[:, t, :], got[:, r, 1, :], w[1], part[:, r, :],
                                             ALU.mult, ALU.add).then_inc(summed, 1)


def add_scaled_norm(k, y, gamma, beta):
    nc = k.nc
    ctx, sem, sb = phase(k, "scaled_norm")
    with ctx:
        g, b = sb("gamma", [P, D]), sb("beta", [P, D])
        loaded, chain = sem("loaded"), sem("chain")
        block = ctx.enter_context(nc.Block())

        @block.sync
        def _(sp):
            sp.dma_start(g[:], gamma.partition_broadcast(P)).then_inc(loaded, 16)
            sp.dma_start(b[:], beta.partition_broadcast(P)).then_inc(loaded, 16)

        @block.vector
        def _(dve):
            wide = [P, TILES, D]
            link = Chain(dve, chain)
            with dve.Fori(0, TILES) as t:
                here, one = y[:, bass.ds(t, 1), :], bass.ds(t, 1)
                dve.tensor_scalar(here, here, k.mean[:, one], k.rstd[:, one], ALU.subtract, ALU.mult).then_inc(chain, 1)
            link.n = TILES
            dve.wait_ge(chain, TILES)
            dve.wait_ge(loaded, 32)
            link(dve.tensor_tensor(y, y, g[:].unsqueeze(1).to_broadcast(wide), ALU.mult))
            link(dve.tensor_tensor(y, y, b[:].unsqueeze(1).to_broadcast(wide), ALU.add))
            link(dve.tensor_tensor(k.x[:], k.x[:], y, ALU.add))


def gat_weights(k, weight, left, right, w_all):
    nc, ps = k.nc, k.ps
    ctx, sem, sb = phase(k, "gat_weights")
    with ctx:
        lr, lr_t, w_t = sb("lr", [2 * HEADS, HD]), sb("lr_t", [HD, 2 * HEADS]), sb("w_t", [HD, 2, P])
        loaded, flipped, back, multiplied, done = (sem(n) for n in ("loaded", "flipped", "back", "multiplied", "done"))
        block = ctx.enter_context(nc.Block())

        @block.sync
        def _(sp):
            sp.dma_start(w_all[:, :, 0:HD], weight.rearrange("(k p) n -> p k n", p=P)).then_inc(loaded, 16)
            sp.dma_start(lr[0:HEADS, :], right[:, :]).then_inc(loaded, 16)
            sp.dma_start(lr[HEADS:2 * HEADS, :], left[:, :]).then_inc(loaded, 16)

        @block.tensor
        def _(pe):
            pe.wait_ge(loaded, 48)
            pe.transpose(ps[0:HD, 0, 0:2 * HEADS], lr[:, :], k.ident[0:2 * HEADS, 0:2 * HEADS])
            for half in range(2):
                last = pe.transpose(ps[0:HD, 1, half * P:(half + 1) * P], w_all[:, half, 0:HD], k.ident[:])
            last.then_inc(flipped, 1)
            pe.wait_ge(back, 2)
            for half in range(2):
                last = pe.matmul(ps[:, 2, half * 8:half * 8 + 8], w_t[:, half, :], lr_t[:], start=True, stop=True)
            last.then_inc(multiplied, 1)

        @block.vector
        def _(dve):
            dve.wait_ge(flipped, 1)
            dve.tensor_copy(lr_t[:], ps[0:HD, 0, 0:2 * HEADS]).then_inc(back, 1)
            dve.tensor_copy(w_t[:].rearrange("p k n -> p (k n)"), ps[0:HD, 1, 0:2 * P]).then_inc(back, 1)
            dve.wait_ge(multiplied, 1)
            for half in range(2):
                dve.tensor_copy(w_all[:, half, HD:HD + 8], ps[:, 2, half * 8:half * 8 + 8]).then_inc(done, 1)


def gat_sum(k, table, rows, acc, room):
    nc, ps = k.nc, k.ps
    ctx, sem, sb = phase(k, "gat_sum")
    with ctx:
        G, Q, W = 8, 4, HEADS * HD + HEADS
        idx, msg = sb("idx", [P, Q, G], I32), sb("msg", [P, Q, G, GW])
        hot = sb("hot", [P, Q, G, P])
        logit = sb("logit", [P, 2, G, HEADS])
        val = room[:, 0:2 * G * W].rearrange("p (h c n) -> p h c n", h=2, c=G)
        e = val[:, :, :, HEADS * HD:W]
        hot_t = room[:, 2 * G * W:2 * G * (W + P)].rearrange("p (h c n) -> p h c n", h=2, c=G)
        idx_ready, issued, hot_ready, flipped, hot_back, scored, z_ready, l_ready, e_ready, val_ready, summed, added = (
            sem(n) for n in ("idx_ready", "issued", "hot_ready", "flipped", "hot_back", "scored", "z_ready", "l_ready",
                             "e_ready", "val_ready", "summed", "added"))
        gathered = [sem(f"gathered{h}") for h in range(Q)]
        turns = EC // (Q * G)
        assert EC % (Q * G) == 0
        block = ctx.enter_context(nc.Block())
        left = ps[:, 2, 0:G * HEADS]
        sums = [ps[:, 3 + c % 4, 0:W] for c in range(G)]

        def run(eng, body):
            with eng.Fori(0, turns - 1) as i:
                for g in range(Q):
                    body(i, g, 2 * Q)
            for g in range(Q):
                body(turns - 1, g, Q - g)

        @block.scalar
        def _(act):
            act.sem_inc(hot_back, 2)

            def keep_indices(i, g):
                act.wait_ge(val_ready, i * Q + (g + 1))
                act.copy(idx[:, g % Q, :], k.dst_slot[:, bass.ds((i * Q + g) * G, G)]).then_inc(idx_ready, 1)

            def keep_flipped(i, g):
                act.wait_ge(scored, i * Q + (g + 1))
                for b in range(2):
                    act.wait_ge(flipped, i * (2 * Q) + (g * 2 + b + 1))
                    act.copy(hot_t[:, g % 2, b * 4:b * 4 + 4, :].rearrange("p c n -> p (c n)"), ps[:, b, :]).then_inc(hot_back, 1)

            def exponent(i, g):
                act.wait_ge(l_ready, i * Q + (g + 1))
                act.activation(e[:, g % 2], logit[:, g % 2], ACT.Exp).then_inc(e_ready, 1)

            for g in range(Q):
                keep_indices(0, g)
            keep_flipped(0, 0)
            exponent(0, 0)
            keep_flipped(0, 1)

            def body(i, g, left_over):
                if left_over > Q:
                    keep_indices(i, g + Q)
                if left_over > 1:
                    exponent(i, g + 1)
                if left_over > 2:
                    keep_flipped(i, g + 2)

            run(act, body)

        @block.gpsimd
        def _(pool):
            with pool.Fori(0, turns) as i:
                for g in range(Q):
                    pool.wait_ge(idx_ready, i * Q + (g + 1))
                    pool.sem_inc(issued, 1)
                    for c in range(G):
                        pool.indirect_dma_start(out=msg[:, g, c, :], out_offset=None, in_=table[:, :],
                                                in_offset=bass.IndirectOffsetOnAxis(ap=idx[:, g, c:c + 1], axis=0)
                                                ).then_inc(gathered[g], 16)

        @block.tensor
        def _(pe):
            pe.sem_inc(scored, 2)
            pe.sem_inc(summed, 2 * G)

            def score(i, g):
                for b in range(2):
                    pe.wait_ge(hot_ready, i * (2 * Q) + (g * 2 + b + 1))
                    pe.wait_ge(hot_back, i * (2 * Q) + (g * 2 + b + 1))
                    for c in range(4):
                        last = pe.transpose(ps[:, b, c * P:(c + 1) * P], hot[:, g % Q, b * 4 + c, :], k.ident[:])
                    last.then_inc(flipped, 1)
                windows = owners(k, pe, k.win_src, (i * Q + g) * G, G, TILES - 1)
                pe.wait_ge(z_ready, i * Q + (g + 1))
                for c in range(G):
                    if c % 4 == 0:
                        pe.wait_ge(hot_back, i * (2 * Q) + (g * 2 + c // 4 + 1 + 2))
                    last = pe.matmul(left[:, c * HEADS:(c + 1) * HEADS], hot_t[:, g % 2, c, :],
                                     rows[:, bass.ds(windows[c], 1), HD + HEADS:GW], start=True, stop=True)
                last.then_inc(scored, 1)

            def body(i, g, left_over):
                pe.wait_ge(val_ready, i * Q + (g + 1 + Q))
                for c in range(G):
                    pe.wait_ge(added, (i * Q + g) * G + (c + 1))
                    pe.matmul(sums[c], hot[:, g, c, :], val[:, g % 2, c, :], start=True, stop=True).then_inc(summed, 1)
                if left_over > 2:
                    score(i, g + 2)

            score(0, 0)
            score(0, 1)
            run(pe, body)

        @block.vector
        def _(dve):
            dve.sem_inc(z_ready, 1)
            dve.sem_inc(val_ready, Q)
            dve.sem_inc(added, 4)

            def make_hot(i, g, c):
                made = dve.tensor_scalar(hot[:, g % Q, c, :], k.iota1[:], k.dst_local[:, bass.ds((i * Q + g) * G + c, 1)],
                                         None, ALU.is_equal)
                if c % 4 == 3:
                    made.then_inc(hot_ready, 1)

            def make_logit(i, g):
                h = g % 2
                dve.wait_ge(scored, i * Q + (g + 1 + 2))
                dve.wait_ge(gathered[g % Q], i * (16 * G) + 16 * G * (1 + g // Q))
                dve.tensor_tensor(logit[:, h], left.rearrange("p (c n) -> p c n", n=HEADS),
                                  msg[:, g % Q, :, HD:HD + HEADS], ALU.add).then_inc(z_ready, 1)
                dve.wait_ge(z_ready, i * Q + (g + 1 + 1))
                dve.scalar_tensor_tensor(logit[:, h], logit[:, h], 0.2, logit[:, h], ALU.mult, ALU.max).then_inc(l_ready, 1)

            def make_values(i, g):
                h, wide = g % 2, [P, G, HEADS, HD]
                dve.wait_ge(e_ready, i * Q + (g + 1))
                dve.tensor_tensor(val[:, h, :, 0:HEADS * HD].rearrange("p c (n d) -> p c n d", d=HD),
                                  msg[:, g % Q, :, 0:HD].unsqueeze(2).to_broadcast(wide),
                                  e[:, h].unsqueeze(3).to_broadcast(wide), ALU.mult).then_inc(val_ready, 1)

            def body(i, g, left_over):
                if left_over > 1:
                    make_logit(i, g + 1)
                windows = owners(k, dve, k.win_src, (i * Q + g) * G, G, TILES - 1)
                for c in range(G):
                    if left_over > 2:
                        make_hot(i, g + 2, c)
                    here = acc[:, bass.ds(windows[c], 1), :]
                    dve.wait_ge(summed, (i * Q + g) * G + (c + 1 + 2 * G))
                    dve.wait_ge(added, (i * Q + g) * G + (c + 4))
                    dve.tensor_tensor(here, here, sums[c], ALU.add).then_inc(added, 1)
                if left_over > 1:
                    make_values(i, g + 1)

            for g in range(2):
                for c in range(G):
                    make_hot(0, g, c)
            make_logit(0, 0)
            make_values(0, 0)
            run(dve, body)


def gat_finish(k, acc, tmp, bias):
    nc = k.nc
    ctx, sem, sb = phase(k, "gat_finish")
    with ctx:
        b, inv = sb("b", [P, HD]), sb("inv", [P, TILES, HEADS])
        loaded, chain, ready, powered = sem("loaded"), sem("chain"), sem("ready"), sem("powered")
        block = ctx.enter_context(nc.Block())
        wide = [P, TILES, HEADS, HD]

        @block.sync
        def _(sp):
            sp.dma_start(b[:], bias.partition_broadcast(P)).then_inc(loaded, 16)

        @block.scalar
        def _(act):
            act.wait_ge(ready, 1)
            act.activation(tmp, tmp, ACT.Exp).then_inc(powered, 1)

        @block.vector
        def _(dve):
            link = Chain(dve, chain)
            v3 = acc[:, :, 0:D]
            v4 = v3.rearrange("p t (n d) -> p t n d", d=HD)
            link(dve.tensor_scalar(inv[:], acc[:, :, D:D + HEADS], ROWSUM_EPS, None, ALU.max))
            link(dve.reciprocal(inv[:], inv[:]))
            link(dve.tensor_tensor(v4, v4, inv[:].unsqueeze(3).to_broadcast(wide), ALU.mult))
            dve.wait_ge(loaded, 16)
            link(dve.tensor_tensor(v4, v4, b[:].unsqueeze(1).unsqueeze(1).to_broadcast(wide), ALU.add))
            dve.tensor_scalar(tmp, v3, 0.0, None, ALU.min).then_inc(ready, 1)
            dve.wait_ge(ready, 1)
            dve.wait_ge(powered, 1)
            link(dve.scalar_tensor_tensor(v3, v3, 0.0, tmp, ALU.max, ALU.add))
            link(dve.scalar_tensor_tensor(k.x[:], v3, -1.0, k.x[:], ALU.add, ALU.add))


def write_out(k, out):
    nc = k.nc
    ctx, sem, sb = phase(k, "out")
    with ctx:
        stored = sem("stored")
        block = ctx.enter_context(nc.Block())

        @block.sync
        def _(sp):
            sp.dma_start(out[0:(TILES - 1) * P, :].rearrange("(t p) d -> p t d", p=P),
                         k.x[:, 0:TILES - 1, :]).then_inc(stored, 16)
            sp.dma_start(out[(TILES - 1) * P:NODES, :], k.x[0:LAST, TILES - 1, :]).then_inc(stored, 16)
            sp.wait_ge(stored, 32)


SORT_BUFFERS = 12
SIDE_WIDTH = EC + 4
H_SIZE, ROWS_SIZE, SIDE_SIZE = TILES * (D + 1), TILES * D, SORT_BUFFERS * SIDE_WIDTH
EARLY = min(E0, (E0 * 2048 - H_SIZE - ROWS_SIZE - SIDE_SIZE) // 1024)


def mixture(k, moe, xn_table, y_table, func, softmax_first, result, add_norm):
    nc = k.nc
    moments(k, moe.name + "_ln", k.x)
    norm_dense(k, moe.name + "_gate", moe.gate, moe.e, moe.score[:], xn_table=xn_table)
    with ExitStack() as ctx:
        key = ctx.enter_context(nc.sbuf_tensor(moe.name + "_key", [P, TILES, 2], I32))
        node = ctx.enter_context(nc.sbuf_tensor(moe.name + "_node", [P, TILES, 2], I32))
        valid = ctx.enter_context(nc.sbuf_tensor(moe.name + "_valid", [P, TILES, 2], F32))
        local = ctx.enter_context(nc.sbuf_tensor(moe.name + "_local", [P, moe.c], F32))
        choose(k, moe, softmax_first, key[:], node[:], valid[:])
        flat = lambda a: a.rearrange("p t j -> p (t j)")
        with ExitStack() as sort_ctx:
            s = Sort(k, sort_ctx, moe.name, P, PM, moe.e, moe.c, flat(key[:]), flat(node[:]), moe.slot[:, 0:moe.c],
                     local[:], moe.owner[:, 0:moe.c], pos=flat(moe.pos[:]), valid=flat(valid[:]))
            sort_whole(k, s, 5)
    experts(k, moe, xn_table, y_table, func)
    combine(k, moe, y_table, result, add_norm)


def build(nc, t, out):
    with ExitStack() as ctx:
        k = allocate(nc, ctx)
        table = nc.dram_tensor("conv_table", (TILES * P, D), F32, kind="Internal").ap()
        end = E0 * 2048
        k.h = k.big[:, end - H_SIZE:end].rearrange("p (t d) -> p t d", d=D + 1)
        k.rows_room = k.big[:, end - H_SIZE - ROWS_SIZE:end - H_SIZE]
        k.rows = k.rows_room.rearrange("p (t d) -> p t d", d=D)
        side_room = k.big[:, end - H_SIZE - ROWS_SIZE - SIDE_SIZE:end - H_SIZE - ROWS_SIZE]
        xn_table = nc.dram_tensor("xn_table", (TILES * P, D), F32, kind="Internal").ap()
        y_table = nc.dram_tensor("y_table", (C0 * P, D), F32, kind="Internal").ap()
        gat_table = nc.dram_tensor("gat_table", (TILES * P, GW), F32, kind="Internal").ap()
        moe0, moe1 = (Moe(k, ctx, f"moe{n}", e, c, *(t[f"L{n}_ffn_{w}"] for w in ("gate_w", "gate_b", *names)))
                      for n, e, c, names in ((0, E0, C0, ("w1", "b1", "w2", "b2")), (1, E1, C1, ("W1", "b1", "W2", "b2"))))
        at = E1 * 2048
        y_all = k.big[:, at:at + TILES * D].rearrange("p (t d) -> p t d", d=D)
        at += TILES * D
        acc = k.big[:, at:at + TILES * (D + HEADS)].rearrange("p (t d) -> p t d", d=D + HEADS)
        at += TILES * (D + HEADS)
        gat_rows = k.big[:, at:at + TILES * GW].rearrange("p (t d) -> p t d", d=GW)
        at += TILES * GW
        w_all = k.big[:, at:at + 2 * GW].rearrange("p (h d) -> p h d", d=GW)
        prefetch(k, "weights0", [lambda sp: load_small(k, sp, moe0), lambda sp: load_small(k, sp, moe1),
                                 lambda sp: load_experts(k, sp, moe0, 0, 0, EARLY)])
        with ExitStack() as side_ctx:
            k.edge_src, k.edge_dst = (side_ctx.enter_context(nc.sbuf_tensor(n, [EP, EM], I32)) for n in ("edge_src", "edge_dst"))
            side = Sort(k, side_ctx, "src", EP, EM, TILES, EC, k.edge_src[:], k.edge_dst[:], k.dst_slot[:, 0:EC], k.dst_local[:, 0:EC],
                        k.win_src[:], room=side_room, width=SIDE_WIDTH)
            with ExitStack() as main_ctx:
                room = k.big[:, end - H_SIZE - ROWS_SIZE:end]
                k.hist_w = room[:, SORT_BUFFERS * EM:].bitcast(F16)[:, 0:EM * TILES]
                main = Sort(k, main_ctx, "dst", EP, EM, TILES, EC, k.edge_dst[:], k.edge_src[:], k.src_slot[:],
                            k.src_local[:, 0:EC], k.win_dst[:], room=room)
                setup(k, t["x"], t["src"], t["dst"], k.edge_src, k.edge_dst)
                sort_whole(k, main, 8, other=side, degree=k.deg_out[:], spare=room[:, SORT_BUFFERS * EM + EM * TILES // 2:])
            root_degree(k, "root_out", k.deg_out[:])
            moments(k, "ln0", k.x)
            for n in range(3):
                conv_dense(k, n, table, t[f"L0_gnn_W{n}"], t[f"L0_gnn_b{n - 1}"] if n else None)
                conv_sum(k, n, table, side)
                if n == 0:
                    root_degree(k, "root_in", k.deg_in[:], counts=k.h[:, :, D], places=side)
            finish_sort(k, side)
        conv_finish(k, t["L0_gnn_b2"])
        recycle(k)
        prefetch(k, "rest0", [lambda sp: load_experts(k, sp, moe0, 0, EARLY, E0),
                              lambda sp: load_experts(k, sp, moe0, 1, 0, E0)])
        mixture(k, moe0, xn_table, y_table, ACT.Relu, False, y_all, True)
        recycle(k)
        moments(k, "ln_y", y_all)
        add_scaled_norm(k, y_all, t["L0_ffn_gamma"], t["L0_ffn_beta"])
        moments(k, "ln2", k.x)
        gat_weights(k, t["L1_gnn_W"], t["L1_gnn_Wl"], t["L1_gnn_Wr"], w_all)
        norm_dense(k, "gat_dense", w_all, GW, gat_rows, table=gat_table, clear=acc)
        gat_sum(k, gat_table, gat_rows, acc, k.big[:, E1 * 2048:E1 * 2048 + TILES * D])
        gat_finish(k, acc, y_all, t["L1_gnn_b"])
        recycle(k)
        prefetch(k, "rest1", [lambda sp, w=w: load_experts(k, sp, moe1, w, 0, E1) for w in range(2)])
        mixture(k, moe1, xn_table, y_table, ACT.Gelu, True, k.x[:], False)
        write_out(k, out)


def kernel(**inputs):
    import numpy as np
    import concourse.bacc as bacc
    from concourse.bass_utils import run_bass_kernel_spmd

    nc = bacc.Bacc("TRN2", target_bir_lowering=False, num_devices=1)
    arrays, aps = {}, {}
    for name, a in inputs.items():
        a = np.ascontiguousarray(a)
        arrays[f"in_{name}"] = a
        aps[name] = nc.dram_tensor(f"in_{name}", a.shape, mybir.dt.from_np(a.dtype), kind="ExternalInput").ap()
    out = nc.dram_tensor("out_x", (NODES, D), F32, kind="ExternalOutput").ap()
    build(nc, aps, out)
    result = run_bass_kernel_spmd(nc, [arrays], core_ids=[0])
    return result.results[0]["out_x"]
```

```python
from contextlib import ExitStack

import concourse.bass as bass
from concourse import mybir

F32 = mybir.dt.float32
F16 = mybir.dt.float16
I32 = mybir.dt.int32
U32 = mybir.dt.uint32
ALU = mybir.AluOpType
ACT = mybir.ActivationFunctionType
AX = mybir.AxisListType

P = 128
D = 256
NODES = 3125
TILES = -(-NODES // P)
LAST = NODES - (TILES - 1) * P
EDGES = 50000
EP = 125
EM = EDGES // EP
EC = (EDGES + TILES * (P - 1)) // P + 1
EC = -(-EC // 16) * 16
FF = 512
E0, E1 = 16, 8
HEADS, HD = 4, 64
PM = 2 * TILES
RING = 5
EPS_LN = 1e-5
ROWSUM_EPS = 1e-12
GW = HD + 2 * HEADS
assert EP * EM == EDGES and TILES % RING == 0 and EM % RING == 0 and PM % RING == 0


def expert_chunks(experts):
    n = (2 * NODES + experts * (P - 1)) // P
    return -(-n // 8) * 8


C0, C1 = expert_chunks(E0), expert_chunks(E1)


class Chain:

    def __init__(self, eng, sem):
        self.eng, self.sem, self.n, self.term = eng, sem, 0, None

    def __call__(self, ins):
        self.n += 1
        ins.then_inc(self.sem, 1)
        self.eng.wait_ge(self.sem, self.n if self.term is None else self.term + self.n)

    def loose(self, ins):
        self.n += 1
        ins.then_inc(self.sem, 1)
        self.eng.wait_ge(self.sem, self.n - 1 if self.term is None else self.term + (self.n - 1))

    def settle(self):
        self.eng.wait_ge(self.sem, self.n if self.term is None else self.term + self.n)

    def loop(self, count, per):
        start = self.n
        with self.eng.Fori(0, count) as i:
            self.term = i * per
            yield i
            assert self.n - start == per
            self.term = None
        self.n = start + count * per


def run(eng, turns, per, body):
    with eng.Fori(0, turns - 1) as i:
        for r in range(per):
            body(i, r, 2 * per)
    for r in range(per):
        body(turns - 1, r, per - r)


def bank(r):
    return r % RING % 3


def bank_free(r):
    apart = next(d for d in range(1, RING + 1) if bank(r - d) == bank(r))
    return RING + r - apart + 1


class Kit:
    pass


def allocate(nc, ctx):
    k = Kit()
    k.nc = nc
    k.spent = []

    def sb(name, shape, dt=F32):
        return ctx.enter_context(nc.sbuf_tensor(name, shape, dt))

    k.sb = sb
    k.ident = sb("ident", [P, P])
    k.ones = sb("ones", [P, P])
    k.before = sb("before", [P, P])
    k.upto = sb("upto", [P, P])
    k.iota1 = sb("iota1", [P, P])
    k.iota_f = sb("iota_f", [P, EC])
    k.iota_h = sb("iota_h", [P, EC], F16)
    k.zero_h = sb("zero_h", [P, P], F16)
    k.x = sb("x_sb", [P, TILES, D])
    k.src_slot = sb("src_slot", [P, EC], I32)
    k.src_local = sb("src_local", [P, EC + 8])
    k.dst_slot = sb("dst_slot", [P, EC], I32)
    k.dst_local = sb("dst_local", [P, EC + 8])
    k.win_dst = sb("win_dst", [1, EC], I32)
    k.win_src = sb("win_src", [1, EC], I32)
    k.slot_low = sb("slot_low", [P, EC], I32)
    k.deg_in = sb("deg_in", [P, TILES])
    k.deg_out = sb("deg_out", [P, TILES])
    k.mean = sb("mean", [P, TILES])
    k.rstd = sb("rstd", [P, TILES])
    k.big = sb("big", [P, E0 * 2048])
    k.ps = ctx.enter_context(nc.psum_tensor("ps", [P, 8, 512], F32))
    return k


def phase(k, name):
    ctx = ExitStack()

    def sem(n):
        k.spent.append(k.nc.alloc_semaphore(f"{name}_{n}"))
        return k.spent[-1]

    sb = lambda n, s, d=F32: ctx.enter_context(k.nc.sbuf_tensor(f"{name}_{n}", s, d))
    return ctx, sem, sb


def recycle(k):
    k.nc.clear_and_free_semaphores(k.spent)
    k.nc.all_engine_barrier()
    k.spent = []


def setup(k, x, src, dst, edge_src, edge_dst, jobs):
    nc = k.nc
    ctx, sem, sb = phase(k, "setup")
    with ctx:
        loaded, made, cleared = sem("loaded"), sem("made"), sem("cleared")
        block = ctx.enter_context(nc.Block())

        @block.sync
        def _(sp):
            sp.dma_start(edge_src[:], src.rearrange("(p m) -> p m", p=EP)).then_inc(loaded, 16)
            sp.dma_start(edge_dst[:], dst.rearrange("(p m) -> p m", p=EP)).then_inc(loaded, 16)
            sp.dma_start(k.x[:, 0:TILES - 1, :],
                         x[0:(TILES - 1) * P, :].rearrange("(t p) d -> p t d", p=P)).then_inc(k.x_loaded, 16)
            sp.wait_ge(cleared, 1)
            sp.dma_start(k.x[0:LAST, TILES - 1, :], x[(TILES - 1) * P:NODES, :]).then_inc(k.x_loaded, 16)
            for job in jobs:
                job(sp)
            sp.wait_ge(loaded, 32)

        @block.vector
        def _(dve):
            dve.memset(k.x[:, TILES - 1, :], 0.0).then_inc(cleared, 1)
            dve.memset(k.zero_h[:], 0.0)
            dve.memset(k.src_local[:, EC:], 0.0)
            dve.memset(k.dst_local[:, EC:], 0.0)

        @block.gpsimd
        def _(pool):
            link = Chain(pool, made)
            link(pool.memset(k.ones[:], 1.0))
            link(pool.affine_select(out=k.ident[:], in_=k.ones[:], compare_op=ALU.is_equal, fill=0.0,
                                    base=0, pattern=[[-1, P]], channel_multiplier=1))
            link(pool.affine_select(out=k.before[:], in_=k.ones[:], compare_op=ALU.is_gt, fill=0.0,
                                    base=0, pattern=[[1, P]], channel_multiplier=-1))
            link(pool.affine_select(out=k.upto[:], in_=k.ones[:], compare_op=ALU.is_ge, fill=0.0,
                                    base=0, pattern=[[1, P]], channel_multiplier=-1))
            link(pool.iota(k.iota1[:], pattern=[[1, P]], base=1, channel_multiplier=0,
                           allow_small_or_imprecise_dtypes=True))
            link(pool.iota(k.iota_f[:], pattern=[[1, EC]], base=0, channel_multiplier=0,
                           allow_small_or_imprecise_dtypes=True))
            link(pool.iota(k.iota_h[:], pattern=[[1, EC]], base=0, channel_multiplier=0,
                           allow_small_or_imprecise_dtypes=True))


class Sort:

    def __init__(self, k, ctx, name, np_, m, buckets, c, key, node, slot, local, owner, pos=None, valid=None,
                 room=None, width=None):
        self.k, self.name, self.np_, self.m, self.buckets, self.c = k, name, np_, m, buckets, c
        self.key, self.node, self.slot, self.local, self.owner, self.pos, self.valid = key, node, slot, local, owner, pos, valid
        width = m if width is None else width
        self.width = width
        self.step = 5 if buckets % 5 == 0 else 8
        assert buckets % self.step == 0

        def sb(n, shape, dt=F32):
            return ctx.enter_context(k.nc.sbuf_tensor(f"{name}_{n}", shape, dt))

        def wide(n, dt=F32):
            if room is None:
                return sb(n, [P, width], dt)[0:np_, :]
            wide.at += width
            part = room[0:np_, wide.at - width:wide.at]
            return part if dt == F32 else part.bitcast(dt)

        wide.at = 0
        self.bucket, self.local1, self.part_a, self.part_b, self.chunk, self.lane = (
            wide(n) for n in ("bucket", "local1", "part_a", "part_b", "chunk", "lane"))
        at_mask = wide.at
        self.mask, self.count, self.acc, self.zero = (wide(n) for n in ("mask", "count", "acc", "zero"))
        self.int_a, self.int_b = wide("int_a", I32), wide("int_b", I32)
        self.cnt, self.pad, self.inc, self.base = (sb(n, [P, 32]) for n in ("cnt", "pad", "inc", "base"))
        self.pad_i = sb("pad_i", [P, 32], I32)
        self.tot_i, self.tot_f, self.ends = sb("tot_i", [32, 1], I32), sb("tot_f", [32, 1]), sb("ends", [32, 1])
        ps = k.ps
        self.slot_a, self.slot_b = ps[:, 6, 0:c], ps[:, 7, 0:c]
        self.pre, self.tot, self.tot_t = ps[0:np_, 3, 0:buckets], ps[0:np_, 3, 64:64 + buckets], ps[0:buckets, 3, 128:129]
        self.ends_ps, self.owner_ps = ps[0:buckets, 4, 0:1], ps[0:1, 5, 0:c]
        self.past = sb("past", [32, c]) if room is None else room[0:32, at_mask:at_mask + c]

    def signals(self, sem):
        self.scanned, self.counted, self.totals, self.tot_ready, self.ends_ready, self.past_ready, self.map_ready = (
            sem(n) for n in ("scanned", "counted", "totals", "tot_ready", "ends_ready", "past_ready", "map_ready"))

    def dve_keys(self, dve, link):
        k, m, buckets, c = self.k, self.m, self.buckets, self.c
        cut = slice(0, m)
        bucket, local1 = self.bucket[:, cut], self.local1[:, cut]
        int_a, int_b = self.int_a[:, cut], self.int_b[:, cut]
        if self.width > m:
            rest = slice(m, self.width)
            link(dve.memset(self.chunk[:, rest], -1.0))
            for a in (self.lane, self.part_a, self.part_b):
                link(dve.memset(a[:, rest], 0.0))
        link(dve.tensor_scalar(int_a, self.key, 7, None, ALU.logical_shift_right))
        link(dve.tensor_copy(bucket, int_a))
        link(dve.tensor_scalar(int_b, self.key, 127, None, ALU.bitwise_and))
        link(dve.tensor_scalar(local1, int_b, 1.0, None, ALU.add))
        if self.valid is not None:
            link(dve.scalar_tensor_tensor(bucket, bucket, 1.0, self.valid, ALU.add, ALU.mult))
            link(dve.tensor_scalar(bucket, bucket, -1.0, None, ALU.add))
        link(dve.tensor_scalar(int_a, self.node, 2, None, ALU.logical_shift_right))
        link(dve.tensor_copy(self.part_a[:, cut], int_a))
        link(dve.tensor_scalar(int_b, self.node, 3, 8, ALU.bitwise_and, ALU.logical_shift_left))
        link(dve.tensor_tensor(self.part_b[:, cut], int_b, local1, ALU.add))
        link(dve.memset(self.zero[:, cut], 0.0))
        link(dve.memset(self.acc[:, cut], 0.0))
        link(dve.memset(self.base[:], 0.0))
        step = self.step
        for i in link.loop(buckets // step, step):
            for r in range(step):
                mask = (self.mask, self.count)[r % 2][:, cut]
                link.loose(dve.tensor_scalar(mask, bucket, k.iota_f[0:self.np_, bass.ds(i * step + r, 1)], 0.0,
                                             ALU.is_equal, ALU.add, accum_out=self.cnt[0:self.np_, bass.ds(i * step + r, 1)]))
            link.settle()
        dve.sem_inc(self.counted, 1)
        q = slice(0, self.np_)
        dve.wait_ge(self.totals, 1)
        link(dve.tensor_scalar(self.pad_i[q, 0:buckets], self.tot, 127.0, None, ALU.add))
        link(dve.tensor_scalar(self.pad_i[q, 0:buckets], self.pad_i[q, 0:buckets], 7, 7,
                               ALU.logical_shift_right, ALU.logical_shift_left))
        link(dve.tensor_copy(self.pad[q, 0:buckets], self.pad_i[q, 0:buckets]))
        link(dve.tensor_tensor_scan(self.inc[q, 0:buckets], self.pad[q, 0:buckets], self.zero[:, 0:buckets], 0.0,
                                    ALU.add, ALU.add))
        link(dve.tensor_tensor(self.base[q, 0:buckets], self.inc[q, 0:buckets], self.pad[q, 0:buckets], ALU.subtract))
        link(dve.scalar_tensor_tensor(self.base[q, 0:buckets], self.pre, -1.0, self.base[q, 0:buckets], ALU.add, ALU.add))
        n = slice(0, buckets)
        link(dve.tensor_scalar(self.tot_i[n, :], self.tot_t, 127.0, None, ALU.add))
        link(dve.tensor_scalar(self.tot_i[n, :], self.tot_i[n, :], 7, None, ALU.logical_shift_right))
        dve.tensor_copy(self.tot_f[n, :], self.tot_i[n, :]).then_inc(self.tot_ready, 1)
        dve.wait_ge(self.ends_ready, 1)
        link(dve.tensor_copy(self.ends[n, :], self.ends_ps))
        dve.tensor_scalar(self.past[n, 0:c], k.iota_f[n, 0:c], self.ends[n, 0:1], None,
                          ALU.is_ge).then_inc(self.past_ready, 1)
        dve.wait_ge(self.map_ready, 1)
        link(dve.tensor_scalar(self.owner, self.owner_ps, float(buckets - 1), None, ALU.min))

    def pe_keys(self, pe):
        k, buckets = self.k, self.buckets
        pe.wait_ge(self.counted, 1)
        cnt, np_ = self.cnt[0:self.np_, 0:buckets], self.np_
        pe.matmul(self.pre, k.before[0:np_, 0:np_], cnt, start=True, stop=True)
        pe.matmul(self.tot, k.ones[0:np_, 0:np_], cnt, start=True, stop=True)
        pe.matmul(self.tot_t, cnt, k.ones[0:np_, 0:1], start=True, stop=True).then_inc(self.totals, 1)
        pe.wait_ge(self.tot_ready, 1)
        pe.matmul(self.ends_ps, k.upto[0:buckets, 0:buckets], self.tot_f[0:buckets, :], start=True,
                  stop=True).then_inc(self.ends_ready, 1)
        pe.wait_ge(self.past_ready, 1)
        pe.matmul(self.owner_ps, k.ones[0:buckets, 0:1], self.past[0:buckets, 0:self.c], start=True,
                  stop=True).then_inc(self.map_ready, 1)

    RANK_LINKS = 3

    def dve_rank(self, dve, link, b):
        cut, q = slice(0, self.m), slice(0, self.np_)
        mask, count = self.mask[:, cut], self.count[:, cut]
        link(dve.tensor_scalar(mask, self.bucket[:, cut], self.k.iota_f[q, bass.ds(b, 1)], None, ALU.is_equal))
        link(dve.tensor_tensor_scan(count, mask, self.zero[:, cut], self.base[q, bass.ds(b, 1)], ALU.add, ALU.add))
        dve.sem_inc(self.scanned, 1)
        link(dve.copy_predicated(self.acc[:, cut], mask.bitcast(I32), count))

    def dve_ranks(self, dve, link):
        cut, q, step = slice(0, self.m), slice(0, self.np_), self.step
        masks = [self.mask[:, cut], self.int_a[:, cut].bitcast(F32)]
        counts = [self.count[:, cut], self.int_b[:, cut].bitcast(F32)]
        for i in link.loop(self.buckets // step, 3 * step):
            def make_mask(r):
                link.loose(dve.tensor_scalar(masks[r % 2], self.bucket[:, cut], self.k.iota_f[q, bass.ds(i * step + r, 1)],
                                             None, ALU.is_equal))

            make_mask(0)
            link.settle()
            for r in range(step):
                link.loose(dve.tensor_tensor_scan(counts[r % 2], masks[r % 2], self.zero[:, cut],
                                                  self.base[q, bass.ds(i * step + r, 1)], ALU.add, ALU.add))
                if r + 1 < step:
                    make_mask(r + 1)
                else:
                    link.settle()
                dve.sem_inc(self.scanned, 1)
                link.loose(dve.copy_predicated(self.acc[:, cut], masks[r % 2].bitcast(I32), counts[r % 2]))
            link.settle()

    def dve_places(self, dve, link):
        cut = slice(0, self.m)
        where = self.int_a[:, cut] if self.pos is None else self.pos
        link(dve.tensor_copy(where, self.acc[:, cut]))
        link(dve.tensor_scalar(self.int_b[:, cut], where, 7, None, ALU.logical_shift_right))
        link(dve.tensor_copy(self.chunk[:, cut], self.int_b[:, cut]))
        link(dve.tensor_scalar(self.int_b[:, cut], where, 127, None, ALU.bitwise_and))
        link(dve.tensor_copy(self.lane[:, cut], self.int_b[:, cut]))
        if self.valid is not None:
            link(dve.scalar_tensor_tensor(self.chunk[:, cut], self.chunk[:, cut], 1.0, self.valid, ALU.add, ALU.mult))
            link(dve.tensor_scalar(self.chunk[:, cut], self.chunk[:, cut], -1.0, None, ALU.add))

    def dve_slots(self, dve, link):
        low = self.k.slot_low[:, 0:self.c]
        link(dve.tensor_copy(self.slot, self.slot_b))
        link(dve.tensor_scalar(low, self.slot, 255, None, ALU.bitwise_and))
        link(dve.tensor_copy(self.local, low))
        link(dve.tensor_scalar(self.slot, self.slot, 8, None, ALU.logical_shift_right))
        link(dve.scalar_tensor_tensor(self.slot, self.slot_a, 4.0, self.slot, ALU.mult, ALU.add))


def owners(k, eng, table, first, count, top):
    _, values = k.nc.values_load_multi_w_load_instructions(table[0:1, bass.ds(first, count)], engines=(eng.engine,),
                                                           min_val=0, max_val=top, skip_runtime_bounds_check_because=
                                                           "counts of chunks' ends passed, clamped to the last bucket")
    return values


class Columns:

    def __init__(self, k, sort, sem, sb, ring):
        self.k, self.s, self.ring = k, sort, ring
        self.lane_hot = sb("lane_hot", [P, ring, P], F16)
        self.lanes = sb("lanes", [P, ring, 2, P], F16)
        self.chunks = sb("chunks", [P, ring, sort.c], F16)
        self.lane_ready, self.parts_ready, self.chunk_ready, self.used = (
            sem(n) for n in ("lane_ready", "parts_ready", "chunk_ready", "used"))

    def dve(self, dve, i, r, ahead=0):
        s, q, col = self.s, slice(0, self.s.np_), bass.ds(i * self.ring + (self.at + r + ahead), 1)
        dve.wait_ge(self.used, i * self.ring + (r + ahead + 1))
        dve.tensor_scalar(self.lane_hot[q, r, :], self.k.iota_h[q, 0:P], s.lane[:, col], None,
                          ALU.is_equal).then_inc(self.lane_ready, 1)
        dve.tensor_scalar(self.chunks[q, r, :], self.k.iota_h[q, 0:s.c], s.chunk[:, col], None,
                          ALU.is_equal).then_inc(self.chunk_ready, 1)

    def act(self, act, i, r):
        s, q, col = self.s, slice(0, self.s.np_), bass.ds(i * self.ring + (self.at + r), 1)
        act.wait_ge(self.lane_ready, i * self.ring + (r + 1))
        act.activation(self.lanes[q, r, 0, :], self.lane_hot[q, r, :], ACT.Copy, scale=s.part_a[:, col])
        act.activation(self.lanes[q, r, 1, :], self.lane_hot[q, r, :], ACT.Copy,
                       scale=s.part_b[:, col]).then_inc(self.parts_ready, 1)

    def pe(self, pe, i, r):
        s, q = self.s, slice(0, self.s.np_)
        pe.wait_ge(self.chunk_ready, i * self.ring + (r + 1))
        pe.wait_ge(self.parts_ready, i * self.ring + (r + 1))
        pe.matmul(s.slot_a, self.lanes[q, r, 0, :], self.chunks[q, r, :], start=False, stop=False, skip_group_check=True)
        pe.matmul(s.slot_b, self.lanes[q, r, 1, :], self.chunks[q, r, :], start=False, stop=False,
                  skip_group_check=True).then_inc(self.used, 1)

    at = 0

    def pe_clear(self, pe):
        for out in (self.s.slot_a, self.s.slot_b):
            pe.matmul(out, self.k.zero_h[:, :], self.k.iota_h[:, 0:out.shape[1]], start=True, stop=False,
                      skip_group_check=True)

    def pe_close(self, pe):
        for out in (self.s.slot_a, self.s.slot_b):
            pe.matmul(out, self.k.zero_h[:, :], self.k.iota_h[:, 0:out.shape[1]], start=False, stop=True,
                      skip_group_check=True)


def sort_whole(k, s, batch, other=None, degree=None, spare=None):
    nc = k.nc
    ctx, sem, sb = phase(k, s.name + "_sort")
    with ctx:
        s.signals(sem)
        chain, placed = sem("chain"), sem("placed")
        hot_ready, chunks_ready, a_ready, b_ready, used = (
            sem(n) for n in ("hot_ready", "chunks_ready", "a_ready", "b_ready", "used"))
        lane_hot, chunks = sb("lane_hot", [P, 2, batch, P], F16), sb("chunks", [P, 2, batch, s.c], F16)
        both = sb("both", [P, 2, 2, batch, P], F16) if spare is None else (
            spare.bitcast(F16)[:, 0:4 * batch * P].rearrange("p (j h b n) -> p j h b n", j=2, h=2, b=batch))
        lane_a, lane_b = both[:, 0], both[:, 1]
        outs = [s.slot_a, s.slot_b]
        if other is not None:
            other.signals(lambda n: sem("other_" + n))
            hist_l = sb("hist_l", [P, 2, batch, P], F16)
            hist_w = k.hist_w[0:s.np_, :].rearrange("p (m w) -> p m w", w=TILES)
            hist = k.ps[:, 2, 0:TILES]
            outs.append(hist)
        q = slice(0, s.np_)
        turns = s.m // (2 * batch)
        assert s.m % (2 * batch) == 0
        block = ctx.enter_context(nc.Block())

        @block.vector
        def _(dve):
            link = Chain(dve, chain)
            s.dve_keys(dve, link)
            if other is not None:
                other.dve_keys(dve, link)
                wide = [s.np_, s.m, TILES]
                link(dve.tensor_scalar(other.local1[:, 0:s.m], other.local1[:, 0:s.m], -1.0, None, ALU.add))
                link(dve.tensor_tensor(hist_w, k.iota_h[q, 0:TILES].unsqueeze(1).to_broadcast(wide),
                                       other.bucket[:, 0:s.m].unsqueeze(2).to_broadcast(wide), ALU.is_equal))
            s.dve_ranks(dve, link)
            s.dve_places(dve, link)
            wide = [s.np_, batch, P]
            number = k.iota_h[q, 0:P].unsqueeze(1).to_broadcast(wide)
            with dve.Fori(0, turns) as i:
                for h in range(2):
                    cols = bass.ds(i * (2 * batch) + h * batch, batch)
                    dve.wait_ge(used, i * 2 + (h + 1))
                    dve.tensor_tensor(lane_hot[q, h], number, s.lane[:, cols].unsqueeze(2).to_broadcast(wide),
                                      ALU.is_equal).then_inc(hot_ready, 1)
                    if other is not None:
                        dve.tensor_tensor(hist_l[q, h], number, other.local1[:, cols].unsqueeze(2).to_broadcast(wide),
                                          ALU.is_equal)
                    for r in range(batch):
                        dve.tensor_scalar(chunks[q, h, r, :], k.iota_h[q, 0:s.c],
                                          s.chunk[:, bass.ds(i * (2 * batch) + (h * batch + r), 1)], None,
                                          ALU.is_equal).then_inc(chunks_ready, 1)
            dve.wait_ge(placed, 1)
            if other is not None:
                link(dve.tensor_scalar(degree, hist, 1.0, None, ALU.max))
            s.dve_slots(dve, link)

        @block.gpsimd
        def _(pool):
            wide = [s.np_, batch, P]
            with pool.Fori(0, turns) as i:
                for h in range(2):
                    part = s.part_b[:, bass.ds(i * (2 * batch) + h * batch, batch)]
                    pool.wait_ge(hot_ready, i * 2 + (h + 1))
                    pool.tensor_tensor(lane_b[q, h], lane_hot[q, h], part.unsqueeze(2).to_broadcast(wide),
                                       ALU.mult).then_inc(b_ready, 1)

        @block.scalar
        def _(act):
            with act.Fori(0, turns) as i:
                for h in range(2):
                    act.wait_ge(hot_ready, i * 2 + (h + 1))
                    for r in range(batch):
                        act.activation(lane_a[q, h, r, :], lane_hot[q, h, r, :], ACT.Copy,
                                       scale=s.part_a[:, bass.ds(i * (2 * batch) + (h * batch + r), 1)]).then_inc(a_ready, 1)

        @block.tensor
        def _(pe):
            pe.sem_inc(used, 2)
            s.pe_keys(pe)
            if other is not None:
                other.pe_keys(pe)
            for out in outs:
                pe.matmul(out, k.zero_h[:, :], k.iota_h[:, 0:out.shape[1]], start=True, stop=False, skip_group_check=True)
            with pe.Fori(0, turns) as i:
                for h in range(2):
                    pe.wait_ge(b_ready, i * 2 + (h + 1))
                    for r in range(batch):
                        n = i * (2 * batch) + (h * batch + r)
                        pe.wait_ge(chunks_ready, n + 1)
                        if other is not None:
                            pe.matmul(hist, hist_l[q, h, r, :], hist_w[:, bass.ds(n, 1), :], start=False, stop=False,
                                      skip_group_check=True)
                        pe.matmul(s.slot_b, lane_b[q, h, r, :], chunks[q, h, r, :], start=False, stop=False, skip_group_check=True)
                        pe.wait_ge(a_ready, n + 1)
                        last = pe.matmul(s.slot_a, lane_a[q, h, r, :], chunks[q, h, r, :], start=False, stop=False,
                                         skip_group_check=True)
                    last.then_inc(used, 1)
            for out in outs:
                last = pe.matmul(out, k.zero_h[:, :], k.iota_h[:, 0:out.shape[1]], start=False, stop=True,
                                 skip_group_check=True)
            last.then_inc(placed, 1)


def finish_sort(k, s):
    ctx, sem, sb = phase(k, s.name + "_finish")
    with ctx:
        chain = sem("chain")
        block = ctx.enter_context(k.nc.Block())

        @block.vector
        def _(dve):
            s.dve_slots(dve, Chain(dve, chain))


def root_degree(k, name, degree, counts=None, places=None):
    nc = k.nc
    ctx, sem, sb = phase(k, name)
    with ctx:
        chain, rooted, ready = sem("chain"), sem("rooted"), sem("ready")
        block = ctx.enter_context(nc.Block())

        @block.vector
        def _(dve):
            link = Chain(dve, chain)
            if counts is not None:
                link(dve.tensor_scalar(degree, counts, 1.0, None, ALU.max))
            dve.sem_inc(ready, 1)
            if places is not None:
                places.dve_places(dve, link)
            dve.wait_ge(rooted, 1)
            link(dve.reciprocal(degree, degree))

        @block.scalar
        def _(act):
            act.wait_ge(ready, 1)
            act.activation(degree, degree, ACT.Sqrt).then_inc(rooted, 1)


def add_row(k, block, sem, row, loaded, loads=16):
    added = sem("row_added")

    @block.gpsimd
    def _(pool):
        pool.wait_ge(loaded, loads)
        pool.tensor_tensor(k.x[:], k.x[:], row[:].unsqueeze(1).to_broadcast([P, TILES, D]), ALU.add).then_inc(added, 1)
        pool.wait_ge(added, 1)


def moments(k, name, src, loaded=None, row=None):
    nc = k.nc
    ctx, sem, sb = phase(k, name)
    with ctx:
        stats, mv, var = sb("stats", [P, TILES, 6]), sb("mv", [P, TILES, 2]), sb("var", [P, TILES])
        chain, rooted = sem("chain"), sem("rooted")
        block = ctx.enter_context(nc.Block())
        if row is not None:
            add_row(k, block, sem, *row)

        @block.vector
        def _(dve):
            link = Chain(dve, chain)
            if loaded is not None:
                dve.wait_ge(loaded, 32)
            for t in range(TILES):
                dve.bn_stats(stats[:, t, :], src[:, t, :]).then_inc(chain, 1)
            dve.wait_ge(chain, TILES)
            link.n = TILES
            for t in range(TILES):
                dve.bn_aggr(mv[:, t, :], stats[:, t, :]).then_inc(chain, 1)
            link.n += TILES
            dve.wait_ge(chain, link.n)
            link(dve.tensor_copy(k.mean[:], mv[:, :, 0]))
            link(dve.tensor_scalar(var[:], mv[:, :, 1], EPS_LN, None, ALU.add))
            dve.wait_ge(rooted, 1)
            link(dve.reciprocal(k.rstd[:], var[:]))

        @block.scalar
        def _(act):
            act.wait_ge(chain, 2 * TILES + 2)
            act.activation(var[:], var[:], ACT.Sqrt).then_inc(rooted, 1)


def conv_dense(k, n, table, w, loaded, bias=None, last=None):
    nc, ps = k.nc, k.ps
    ctx, sem, sb = phase(k, f"dense{n}")
    with ctx:
        act_in, act_out, turned = sb("act_in", [P, RING, D]), sb("act_out", [P, RING, D]), sb("turned", [P, RING, D])
        stored = sem("stored")
        in_ready, scaled, flipped, turned_back, multiplied, row_ready, cleared = (
            sem(x) for x in ("in_ready", "scaled", "flipped", "turned_back", "multiplied", "row_ready", "cleared"))
        flips, prods = [ps[:, bank(r), 0:D] for r in range(RING)], [ps[:, 3 + bank(r), 0:D] for r in range(RING)]
        block = ctx.enter_context(nc.Block())
        loads = 16 * (1 + (bias is not None) + (last is not None))
        if last is not None:
            add_row(k, block, sem, last, loaded, loads)

        @block.sync
        def _(sp):
            with sp.Fori(0, TILES) as t:
                sp.wait_ge(row_ready, t + (1 + RING))
                sp.dma_start(table[bass.ds(t * P, P), :], k.rows[:, bass.ds(t, 1), :]).then_inc(stored, 16)
            sp.wait_ge(stored, 16 * TILES)

        @block.vector
        def _(dve):
            dve.sem_inc(turned_back, RING)
            dve.wait_ge(loaded, loads)

            def make_in(i, r):
                t = bass.ds(i * RING + r, 1)
                dve.wait_ge(scaled, i * RING + (r + 1))
                if n == 0:
                    dve.tensor_scalar(act_in[:, r % RING, :], k.x[:, t, :], k.mean[:, t], k.rstd[:, t],
                                      ALU.subtract, ALU.mult).then_inc(in_ready, 1)
                else:
                    dve.scalar_tensor_tensor(act_in[:, r % RING, :], k.h[:, t, 0:D], k.deg_in[:, t], bias[:],
                                             ALU.mult, ALU.add).then_inc(in_ready, 1)

            def turn(i, r):
                dve.wait_ge(flipped, i * RING + (r + 1 + RING))
                dve.wait_ge(multiplied, i * RING + (r + 1))
                dve.tensor_copy(turned[:, r % RING, :], flips[r % RING]).then_inc(turned_back, 1)

            def body(i, r, left):
                if left > 4:
                    make_in(i, r + 4)
                if left > 1:
                    turn(i, r + 1)

            for r in range(4):
                make_in(0, r)
            turn(0, 0)
            run(dve, TILES // RING, RING, body)
            dve.wait_ge(in_ready, TILES)
            dve.memset(k.h, 0.0).then_inc(cleared, 1)

        @block.scalar
        def _(act):
            act.sem_inc(scaled, RING)
            act.sem_inc(row_ready, RING)

            def scale(i, r):
                act.wait_ge(in_ready, i * RING + (r + 1))
                act.wait_ge(flipped, i * RING + (r + 1))
                act.activation(act_out[:, r % RING, :], act_in[:, r % RING, :], ACT.Relu if n else ACT.Copy,
                               scale=k.deg_out[:, bass.ds(i * RING + r, 1)]).then_inc(scaled, 1)

            def body(i, r, left):
                if left > 3:
                    scale(i, r + 3)
                act.wait_ge(multiplied, i * RING + (r + 1 + RING))
                act.copy(k.rows[:, bass.ds(i * RING + r, 1), :], prods[r]).then_inc(row_ready, 1)

            for r in range(3):
                scale(0, r)
            run(act, TILES // RING, RING, body)

        @block.tensor
        def _(pe):
            pe.sem_inc(flipped, RING)
            pe.sem_inc(multiplied, RING)

            def flip(i, r):
                pe.wait_ge(scaled, i * RING + (r + 1 + RING))
                pe.wait_ge(turned_back, i * RING + bank_free(r))
                for half in range(2):
                    last = pe.transpose(flips[r % RING][:, half * P:(half + 1) * P],
                                        act_out[:, r % RING, half * P:(half + 1) * P], k.ident[:])
                last.then_inc(flipped, 1)

            def body(i, r, left):
                pe.wait_ge(turned_back, i * RING + (r + 1 + RING))
                pe.wait_ge(row_ready, i * RING + bank_free(r))
                for half in range(2):
                    last = pe.matmul(prods[r], turned[:, r, half * P:(half + 1) * P], w[:, half, :],
                                     start=(half == 0), stop=(half == 1))
                last.then_inc(multiplied, 1)
                if left > 2:
                    flip(i, r + 2)

            for r in range(2):
                flip(0, r)
            pe.wait_ge(loaded, loads)
            run(pe, TILES // RING, RING, body)


def conv_sum(k, n, table, side):
    nc, ps = k.nc, k.ps
    ctx, sem, sb = phase(k, f"sum{n}")
    with ctx:
        G, HALF, BANKS = 16, 8, 4
        W = D + 1
        msg = k.rows_room[:, 0:G * W].rearrange("p (g w) -> p g w", w=W)
        hot = k.rows_room[:, G * W:G * (W + P)].rearrange("p (g w) -> p g w", w=P)
        idx = sb("idx", [P, G], I32)
        idx_ready, hot_ready, summed, added, issued, ones_ready = (
            sem(x) for x in ("idx_ready", "hot_ready", "summed", "added", "issued", "ones_ready"))
        gathered = [sem(f"gathered{r}") for r in range(G)]
        sums = [ps[:, r % BANKS, 0:W] for r in range(G)]
        turns = EC // G
        assert side.width == HALF * 2 * turns + HALF // 2 and TILES <= turns
        columns = None
        if n:
            columns = Columns(k, side, sem, sb, HALF)
            columns.at = (n - 1) * HALF * turns
        chain = sem("chain")
        block = ctx.enter_context(nc.Block())

        @block.scalar
        def _(act):
            with act.Fori(0, turns) as i:
                for r in range(G):
                    act.wait_ge(summed, i * G + (r + 1))
                    act.copy(idx[:, r:r + 1], k.src_slot[:, bass.ds(i * G + r, 1)]).then_inc(idx_ready, 1)
                    if n and r % 2:
                        columns.act(act, i, r // 2)

        @block.gpsimd
        def _(pool):
            with pool.Fori(0, turns) as i:
                for r in range(G):
                    pool.wait_ge(idx_ready, i * G + (r + 1))
                    pool.sem_inc(issued, 1)
                    pool.indirect_dma_start(out=msg[:, r, 0:D], out_offset=None, in_=table[:, :],
                                            in_offset=bass.IndirectOffsetOnAxis(ap=idx[:, r:r + 1], axis=0)
                                            ).then_inc(gathered[r], 16)

        @block.vector
        def _(dve):
            def make_hot(i, r, more=0):
                dve.wait_ge(summed, i * G + (r + more + 1))
                dve.tensor_scalar(hot[:, r, :], k.iota1[:], k.src_local[:, bass.ds(i * G + (r + more), 1)], None,
                                  ALU.is_equal).then_inc(hot_ready, 1)

            def add(i, r, window):
                here = k.h[:, bass.ds(window, 1), :]
                dve.wait_ge(summed, i * G + (r + 1 + G))
                dve.wait_ge(added, i * G + (r + BANKS))
                dve.tensor_tensor(here, here, sums[r], ALU.add).then_inc(added, 1)

            dve.sem_inc(added, BANKS)
            dve.memset(msg[:, :, D:W], 1.0).then_inc(ones_ready, 1)
            link = Chain(dve, chain)
            for r in range(HALF):
                dve.wait_ge(summed, r + 1)
                dve.tensor_scalar(hot[:, r, :], k.iota1[:], k.src_local[:, r:r + 1], None, ALU.is_equal).then_inc(hot_ready, 1)
                if n and r % 2:
                    columns.dve(dve, 0, r // 2)
            for i in link.loop(turns, 0 if n else side.RANK_LINKS):
                windows = owners(k, dve, k.win_dst, i * G, G, TILES - 1)
                for r in range(HALF):
                    make_hot(i, r + HALF)
                    if n and r % 2:
                        columns.dve(dve, i, (HALF + r) // 2)
                    add(i, r, windows[r])
                if not n:
                    side.dve_rank(dve, link, i)
                for r in range(HALF):
                    make_hot(i, r, G)
                    if n and r % 2:
                        columns.dve(dve, i, r // 2, HALF)
                    add(i, r + HALF, windows[r + HALF])

        @block.tensor
        def _(pe):
            pe.sem_inc(summed, G)
            if n:
                pe.sem_inc(columns.used, HALF)
            if n == 1:
                columns.pe_clear(pe)
            pe.wait_ge(ones_ready, 1)
            with pe.Fori(0, turns) as i:
                for r in range(G):
                    pe.wait_ge(hot_ready, i * G + (r + 1))
                    pe.wait_ge(added, i * G + (r + 1))
                    pe.wait_ge(gathered[r], i * 16 + 16)
                    pe.matmul(sums[r], hot[:, r, :], msg[:, r, :], start=True, stop=True).then_inc(summed, 1)
                    if n and r % 2:
                        columns.pe(pe, i, r // 2)
            if n == 2:
                columns.pe_close(pe)


def conv_finish(k):
    ctx, sem, sb = phase(k, "finish")
    with ctx:
        chain = sem("chain")
        block = ctx.enter_context(k.nc.Block())

        @block.vector
        def _(dve):
            with dve.Fori(0, TILES // RING) as i:
                for r in range(RING):
                    t = bass.ds(i * RING + r, 1)
                    dve.scalar_tensor_tensor(k.x[:, t, :], k.h[:, t, 0:D], k.deg_in[:, t], k.x[:, t, :],
                                             ALU.mult, ALU.add).then_inc(chain, 1)
            dve.wait_ge(chain, TILES)


def norm_dense(k, name, weight, width, result, table=None, xn_table=None, clear=None):
    nc, ps = k.nc, k.ps
    ctx, sem, sb = phase(k, name)
    with ctx:
        xn, turned = sb("xn", [P, RING, D]), sb("turned", [P, RING, D])
        xn_ready, kept, flipped, turned_back, multiplied, row_ready, stored, cleared = (
            sem(x) for x in ("xn_ready", "kept", "flipped", "turned_back", "multiplied", "row_ready", "stored", "cleared"))
        xn_stored = [sem(f"xn_stored{r}") for r in range(RING)]
        flips, prods = [ps[:, bank(r), 0:D] for r in range(RING)], [ps[:, 3 + bank(r), 0:width] for r in range(RING)]
        block = ctx.enter_context(nc.Block())

        if xn_table is not None:
            @block.sync
            def _(sp):
                sp.sem_inc(kept, RING)
                with sp.Fori(0, TILES // RING) as i:
                    for r in range(RING):
                        sp.wait_ge(xn_ready, i * RING + (r + 1))
                        sp.dma_start(xn_table[bass.ds((i * RING + r) * P, P), :], xn[:, r, :]).then_inc(xn_stored[r], 16)
                    for r in range(RING):
                        sp.wait_ge(xn_stored[r], i * 16 + 16)
                        sp.sem_inc(kept, 1)

        if table is not None:
            @block.sync
            def _(sp):
                with sp.Fori(0, TILES) as t:
                    sp.wait_ge(row_ready, t + (1 + RING))
                    sp.dma_start(table[bass.ds(t * P, P), :], result[:, bass.ds(t, 1), :]).then_inc(stored, 16)
                sp.wait_ge(stored, 16 * TILES)

        @block.vector
        def _(dve):
            def normalize(i, r):
                t, place = bass.ds(i * RING + r, 1), r % RING
                dve.wait_ge(flipped, i * RING + (r + 1))
                if xn_table is not None:
                    dve.wait_ge(kept, i * RING + (r + 1))
                dve.tensor_scalar(xn[:, place, :], k.x[:, t, :], k.mean[:, t], k.rstd[:, t],
                                  ALU.subtract, ALU.mult).then_inc(xn_ready, 1)

            with dve.Fori(0, TILES // RING) as i:
                for r in range(RING):
                    normalize(i, r)
            if clear is not None:
                dve.memset(clear, 0.0).then_inc(cleared, 1)

        @block.scalar
        def _(act):
            act.sem_inc(turned_back, RING)
            act.sem_inc(row_ready, RING)

            def turn(i, r):
                act.wait_ge(flipped, i * RING + (r + 1 + RING))
                act.wait_ge(multiplied, i * RING + (r + 1))
                act.copy(turned[:, r % RING, :], flips[r % RING]).then_inc(turned_back, 1)

            def body(i, r, left):
                if left > 1:
                    turn(i, r + 1)
                act.wait_ge(multiplied, i * RING + (r + 1 + RING))
                act.copy(result[:, bass.ds(i * RING + r, 1), :], prods[r]).then_inc(row_ready, 1)

            turn(0, 0)
            run(act, TILES // RING, RING, body)

        @block.tensor
        def _(pe):
            pe.sem_inc(flipped, RING)
            pe.sem_inc(multiplied, RING)

            def flip(i, r):
                pe.wait_ge(xn_ready, i * RING + (r + 1))
                pe.wait_ge(turned_back, i * RING + bank_free(r))
                for half in range(2):
                    last = pe.transpose(flips[r % RING][:, half * P:(half + 1) * P],
                                        xn[:, r % RING, half * P:(half + 1) * P], k.ident[:])
                last.then_inc(flipped, 1)

            def body(i, r, left):
                pe.wait_ge(turned_back, i * RING + (r + 1 + RING))
                pe.wait_ge(row_ready, i * RING + bank_free(r))
                for half in range(2):
                    last = pe.matmul(prods[r], turned[:, r, half * P:(half + 1) * P], weight[:, half, :],
                                     start=(half == 0), stop=(half == 1))
                last.then_inc(multiplied, 1)
                if left > 2:
                    flip(i, r + 2)

            for r in range(2):
                flip(0, r)
            run(pe, TILES // RING, RING, body)


class Moe:

    def __init__(self, k, ctx, name, experts, chunks, gate_w, gate_b, w1, b1, w2, b2):
        sb = lambda n, s, d=F32: ctx.enter_context(k.nc.sbuf_tensor(f"{name}_{n}", s, d))
        self.name, self.e, self.c = name, experts, chunks
        self.gate_w, self.gate_b, self.w1, self.b1, self.w2, self.b2 = gate_w, gate_b, w1, b1, w2, b2
        self.gate = sb("gate", [P, 2, experts])
        self.gate_bias = sb("gate_bias", [P, experts])
        self.score = sb("score", [P, TILES, experts])
        self.b1_t = sb("b1_t", [P, experts, FF // P])
        self.b2_sb = sb("b2_sb", [experts, D])
        self.weight = sb("weight", [P, TILES, 2])
        self.combine = sb("combine", [P, TILES, experts])
        self.slot = sb("slot", [P, chunks + 8], I32)
        self.pos = sb("pos", [P, TILES, 2], I32)
        self.owner = sb("owner", [1, chunks + 8], I32)
        self.small = ctx.enter_context(k.nc.semaphore(f"{name}_small"))
        self.loads = 0
        self.big = ctx.enter_context(k.nc.semaphore(f"{name}_big"))


def load_experts(k, eng, moe, which, first, last):
    dram, n = ((moe.w1, FF), (moe.w2, D))[which]
    for e in range(first, last, 4):
        end = min(e + 4, last)
        here = k.big[:, (which * moe.e + e) * 1024:(which * moe.e + end) * 1024]
        eng.dma_start(here.rearrange("p (m n) -> p m n", n=n),
                      dram[e:end, :, :].rearrange("e (k p) n -> p (e k) n", p=P)).then_inc(moe.big, 16)
        moe.loads += 16


def load_row(eng, row, dram, loaded):
    eng.dma_start(row[:, :], dram.partition_broadcast(P)).then_inc(loaded, 16)


def load_small(k, eng, moe):
    with k.nc.allow_non_contiguous_dma(reason="the bias of a hidden unit goes to the unit's partition"):
        eng.dma_start(moe.gate[:], moe.gate_w.rearrange("(k p) e -> p k e", p=P)).then_inc(moe.small, 16)
        eng.dma_start(moe.gate_bias[:], moe.gate_b.partition_broadcast(P)).then_inc(moe.small, 16)
        eng.dma_start(moe.b1_t[:].rearrange("p e f -> p (e f)"),
                      moe.b1.rearrange("e (f p) -> p (e f)", p=P)).then_inc(moe.small, 16)
        eng.dma_start(moe.b2_sb[:], moe.b2[:, :]).then_inc(moe.small, 16)


SMALL_LOADS = 64


def prefetch(k, name, jobs):
    ctx, sem, sb = phase(k, name)
    with ctx:
        block = ctx.enter_context(k.nc.Block())

        @block.sync
        def _(sp):
            for job in jobs:
                job(sp)


def choose(k, moe, softmax_first, key, node, valid):
    nc = k.nc
    e = moe.e
    ctx, sem, sb = phase(k, moe.name + "_choose")
    with ctx:
        top, which = sb("top", [P, TILES, 8]), sb("which", [P, TILES, 8], U32)
        ids, tmp, peak, node_f = sb("ids", [P, TILES, 2]), sb("tmp", [P, TILES, e]), sb("peak", [P, TILES]), sb("node_f", [P, TILES, 2])
        chain, numbered, ready, powered = sem("chain"), sem("numbered"), sem("ready"), sem("powered")
        block = ctx.enter_context(nc.Block())
        wide = [P, TILES, e]

        @block.gpsimd
        def _(pool):
            pool.iota(node, pattern=[[P, TILES], [0, 2]], base=0, channel_multiplier=1).then_inc(numbered, 1)

        @block.scalar
        def _(act):
            act.wait_ge(ready, 1)
            if softmax_first:
                act.activation(moe.score[:], moe.score[:], ACT.Exp).then_inc(powered, 1)
            else:
                act.activation(moe.weight[:, :, 1], moe.weight[:, :, 1], ACT.Exp).then_inc(powered, 1)

        @block.vector
        def _(dve):
            link = Chain(dve, chain)
            score = moe.score[:]
            link(dve.memset(moe.slot[:, moe.c:], 0))
            link(dve.memset(moe.owner[:, moe.c:], 0))
            dve.wait_ge(moe.small, SMALL_LOADS)
            link(dve.tensor_tensor(score, score, moe.gate_bias[:].unsqueeze(1).to_broadcast(wide), ALU.add))
            if softmax_first:
                link(dve.tensor_reduce(peak[:], score, AX.X, ALU.max))
                dve.tensor_tensor(score, score, peak[:].unsqueeze(2).to_broadcast(wide), ALU.subtract).then_inc(ready, 1)
                dve.wait_ge(powered, 1)
                link(dve.tensor_reduce(peak[:], score, AX.X, ALU.add))
                link(dve.reciprocal(peak[:], peak[:]))
                link(dve.tensor_tensor(score, score, peak[:].unsqueeze(2).to_broadcast(wide), ALU.mult))
            for t in range(TILES):
                dve.max(top[:, t, :], moe.score[:, t, :]).then_inc(chain, 1)
            link.n += TILES
            dve.wait_ge(chain, link.n)
            for t in range(TILES):
                dve.max_index(which[:, t, :], top[:, t, :], moe.score[:, t, :]).then_inc(chain, 1)
            link.n += TILES
            dve.wait_ge(chain, link.n)
            link(dve.tensor_copy(ids[:], which[:, :, 0:2]))
            if softmax_first:
                link(dve.tensor_copy(moe.weight[:], top[:, :, 0:2]))
            else:
                dve.tensor_tensor(moe.weight[:, :, 1], top[:, :, 1], top[:, :, 0], ALU.subtract).then_inc(ready, 1)
                dve.wait_ge(powered, 1)
                link(dve.tensor_scalar(peak[:], moe.weight[:, :, 1], 1.0, None, ALU.add))
                link(dve.reciprocal(moe.weight[:, :, 0], peak[:]))
                link(dve.tensor_tensor(moe.weight[:, :, 1], moe.weight[:, :, 1], moe.weight[:, :, 0], ALU.mult))
            number = k.iota_f[:, 0:e].unsqueeze(1).to_broadcast(wide)
            for j in range(2):
                out = moe.combine[:] if j == 0 else tmp[:]
                link(dve.tensor_tensor(out, number, ids[:, :, j:j + 1].to_broadcast(wide), ALU.is_equal))
                link(dve.tensor_tensor(out, out, moe.weight[:, :, j:j + 1].to_broadcast(wide), ALU.mult))
            link(dve.tensor_tensor(moe.combine[:], moe.combine[:], tmp[:], ALU.add))
            link(dve.tensor_scalar(key, ids[:], 128.0, None, ALU.mult))
            dve.wait_ge(numbered, 1)
            link(dve.tensor_copy(node_f[:], node))
            link(dve.tensor_scalar(valid, node_f[:], float(NODES), None, ALU.is_lt))


def experts(k, moe, xn_table, y_table, func):
    nc, ps = k.nc, k.ps
    ctx, sem, sb = phase(k, moe.name + "_experts")
    with ctx:
        U, Y = 8, 4
        KD, KF = D // P, FF // P
        rows, idx = sb("rows", [P, U, D]), sb("idx", [P, U], I32)
        x_t, hid_t, y = sb("x_t", [P, 2, D]), sb("hid_t", [P, 2, FF]), sb("y", [P, Y, D])
        w1 = sb("w1", [P, 2, KD * FF])
        idx_ready, issued, flip_x, x_back, w1_ready, up, acted, down, y_ready, kept = (
            sem(n) for n in ("idx_ready", "issued", "flip_x", "x_back", "w1_ready", "up", "acted", "down", "y_ready", "kept"))
        gathered, stored = [sem(f"gathered{r}") for r in range(U)], [sem(f"stored{r}") for r in range(U)]
        all_w1, all_w2 = (k.big[:, j * moe.e * 1024:(j + 1) * moe.e * 1024].rearrange("p (e w) -> p e w", w=1024)
                          for j in range(2))
        turns = moe.c // U
        assert moe.c % U == 0
        block = ctx.enter_context(nc.Block())

        @block.sync
        def _(sp):
            sp.sem_inc(kept, Y)
            with sp.Fori(0, turns) as i:
                for r in range(U):
                    sp.wait_ge(y_ready, i * U + (r + 1 + 2))
                    sp.dma_start(y_table[bass.ds((i * U + r) * P, P), :], y[:, r % Y, :]).then_inc(stored[r], 16)
                    if r >= 2:
                        sp.wait_ge(stored[r - 2], i * 16 + 16)
                        sp.sem_inc(kept, 1)
                for r in range(U - 2, U):
                    sp.wait_ge(stored[r], i * 16 + 16)
                    sp.sem_inc(kept, 1)

        @block.gpsimd
        def _(pool):
            with pool.Fori(0, turns) as i:
                for r in range(U):
                    pool.wait_ge(idx_ready, i * U + (r + 1))
                    pool.sem_inc(issued, 1)
                    pool.indirect_dma_start(out=rows[:, r, :], out_offset=None, in_=xn_table[:, :],
                                            in_offset=bass.IndirectOffsetOnAxis(ap=idx[:, r:r + 1], axis=0)
                                            ).then_inc(gathered[r], 16)
            for r in range(2):
                pool.wait_ge(idx_ready, moe.c + (r + 1))
                pool.sem_inc(issued, 1)
                pool.indirect_dma_start(out=rows[:, r, :], out_offset=None, in_=xn_table[:, :],
                                        in_offset=bass.IndirectOffsetOnAxis(ap=idx[:, r:r + 1], axis=0)
                                        ).then_inc(gathered[r], 16)

        @block.scalar
        def _(act):
            act.sem_inc(acted, 2)
            act.wait_ge(moe.small, SMALL_LOADS)
            act.copy(idx[:], moe.slot[:, 0:U]).then_inc(idx_ready, U)
            with act.Fori(0, turns) as i:
                mine = owners(k, act, moe.owner, i * U, U, moe.e - 1)
                for r in range(U):
                    act.wait_ge(up, i * U + (r + 1 + 2))
                    act.wait_ge(down, i * U + (r + 1))
                    for f in range(KF):
                        last = act.activation(hid_t[:, r % 2, f * P:(f + 1) * P], ps[:, 4 + r % 2, f * P:(f + 1) * P], func,
                                              bias=moe.b1_t[:, bass.ds(mine[r], 1), f])
                    last.then_inc(acted, 1)
                    act.wait_ge(flip_x, i * U + (r + 1 + U))
                    act.copy(idx[:, r:r + 1], moe.slot[:, bass.ds(i * U + (r + U), 1)]).then_inc(idx_ready, 1)

        @block.vector
        def _(dve):
            dve.sem_inc(x_back, 2)
            dve.sem_inc(w1_ready, 2)
            dve.sem_inc(y_ready, 2)
            dve.wait_ge(moe.big, moe.loads)

            def keep_x(i, r):
                dve.wait_ge(flip_x, i * U + (r + 1 + U))
                dve.wait_ge(up, i * U + (r + 1))
                dve.tensor_copy(x_t[:, r % 2, :], ps[:, r % 2, 0:D]).then_inc(x_back, 1)

            def keep_w1(i, r, e):
                dve.wait_ge(up, i * U + (r + 1))
                dve.tensor_copy(w1[:, r % 2, :], all_w1[:, bass.ds(e, 1), :]).then_inc(w1_ready, 1)

            first = owners(k, dve, moe.owner, 0, 2, moe.e - 1)
            for r in range(2):
                keep_x(0, r)
                keep_w1(0, r, first[r])
            with dve.Fori(0, turns) as i:
                mine = owners(k, dve, moe.owner, i * U + 2, U, moe.e - 1)
                for pair in range(0, U, 2):
                    for r in (pair, pair + 1):
                        keep_w1(i, r + 2, mine[r])
                    for r in (pair, pair + 1):
                        keep_x(i, r + 2)
                    for r in (pair, pair + 1):
                        dve.wait_ge(down, i * U + (r + 1 + 2))
                        dve.wait_ge(kept, i * U + (r + 1))
                        dve.tensor_copy(y[:, r % Y, :], ps[:, 6 + r % 2, 0:D]).then_inc(y_ready, 1)

        @block.tensor
        def _(pe):
            pe.sem_inc(flip_x, U)
            pe.sem_inc(up, 2)
            pe.sem_inc(down, 2)

            def transpose_x(i, r):
                pe.wait_ge(x_back, i * U + (r + 1))
                pe.wait_ge(gathered[r % U], i * 16 + (16 + r // U * 16))
                for h in range(KD):
                    last = pe.transpose(ps[:, r % 2, h * P:(h + 1) * P], rows[:, r % U, h * P:(h + 1) * P], k.ident[:])
                last.then_inc(flip_x, 1)

            transpose_x(0, 0)
            transpose_x(0, 1)
            pe.wait_ge(moe.big, moe.loads)
            with pe.Fori(0, turns) as i:
                mine = owners(k, pe, moe.owner, i * U, U, moe.e - 1)
                for pair in range(0, U, 2):
                    for r in (pair, pair + 1):
                        pe.wait_ge(x_back, i * U + (r + 1 + 2))
                        pe.wait_ge(w1_ready, i * U + (r + 1 + 2))
                        pe.wait_ge(acted, i * U + (r + 1))
                        for f in range(KF):
                            for h in range(KD):
                                last = pe.matmul(ps[:, 4 + r % 2, f * P:(f + 1) * P],
                                                 w1[:, r % 2, h * FF + f * P:h * FF + (f + 1) * P],
                                                 x_t[:, r % 2, h * P:(h + 1) * P], start=(h == 0), stop=(h == KD - 1))
                        last.then_inc(up, 1)
                    for r in (pair, pair + 1):
                        transpose_x(i, r + 2)
                    for r in (pair, pair + 1):
                        w2 = all_w2[:, bass.ds(mine[r], 1), :]
                        pe.wait_ge(acted, i * U + (r + 1 + 2))
                        pe.wait_ge(y_ready, i * U + (r + 1))
                        for f in range(KF):
                            last = pe.matmul(ps[:, 6 + r % 2, 0:D], hid_t[:, r % 2, f * P:(f + 1) * P],
                                             w2[:, :, f * D:(f + 1) * D],
                                             start=(f == 0), stop=(f == KF - 1))
                        last.then_inc(down, 1)


def combine(k, moe, y_table, result, add_norm, out=None):
    nc, ps = k.nc, k.ps
    e = moe.e
    ctx, sem, sb = phase(k, moe.name + "_combine")
    with ctx:
        got, idx = sb("got", [P, RING, 2, D]), sb("idx", [P, RING, 2], I32)
        cw, cw_t, part = sb("cw", [P, RING, e]), sb("cw_t", [e, RING, P]), sb("part", [P, RING, D])
        idx_ready, issued, cw_ready, flipped, cw_back, biased, summed, chain = (
            sem(n) for n in ("idx_ready", "issued", "cw_ready", "flipped", "cw_back", "biased", "summed", "chain"))
        gathered = [sem(f"gathered{r}") for r in range(RING)]
        if add_norm:
            xn, shift, shift_ready, xn_ready = sb("xn", [P, RING, D]), sb("shift", [P, TILES]), sem("shift_ready"), sem("xn_ready")
        block = ctx.enter_context(nc.Block())
        if out is not None:
            written = sem("written")

            @block.sync
            def _(sp):
                with sp.Fori(0, TILES // RING - 1) as i:
                    sp.wait_ge(summed, i * RING + 2 * RING)
                    sp.dma_start(out[bass.ds(i * (RING * P), RING * P), :].rearrange("(t p) d -> p t d", p=P),
                                 result[:, bass.ds(i * RING, RING), :]).then_inc(written, 16)
                sp.wait_ge(summed, TILES + RING)
                sp.dma_start(out[(TILES - RING) * P:(TILES - 1) * P, :].rearrange("(t p) d -> p t d", p=P),
                             result[:, TILES - RING:TILES - 1, :]).then_inc(written, 16)
                sp.dma_start(out[(TILES - 1) * P:NODES, :], result[0:LAST, TILES - 1, :]).then_inc(written, 16)
                sp.wait_ge(written, 16 * (TILES // RING + 1))

        pos, weight = moe.pos[:], moe.weight[:].rearrange("p t j -> p (t j)")

        @block.scalar
        def _(act):
            act.sem_inc(cw_back, RING)
            if add_norm:
                act.wait_ge(shift_ready, 2)
            with act.Fori(0, TILES // RING) as i:
                for r in range(RING):
                    t = bass.ds(i * RING + r, 1)
                    act.wait_ge(summed, i * RING + (r + 1))
                    act.copy(idx[:, r, :], pos[:, t, :]).then_inc(idx_ready, 1)
                    act.wait_ge(flipped, i * RING + (r + 1))
                    act.copy(cw[:, r, :], moe.combine[:, t, :]).then_inc(cw_ready, 1)
                    if add_norm:
                        act.activation(xn[:, r, :], k.x[:, t, :], ACT.Identity, bias=shift[:, t],
                                       scale=k.rstd[:, t]).then_inc(xn_ready, 1)
                for r in range(RING):
                    act.wait_ge(flipped, i * RING + (r + 1 + RING))
                    act.wait_ge(biased, i * RING + (r + 1))
                    act.copy(cw_t[:, r, :], ps[0:e, bank(r), 0:P]).then_inc(cw_back, 1)

        @block.gpsimd
        def _(pool):
            with pool.Fori(0, TILES // RING) as i:
                for r in range(RING):
                    pool.wait_ge(idx_ready, i * RING + (r + 1))
                    pool.sem_inc(issued, 1)
                    for j in range(2):
                        pool.indirect_dma_start(out=got[:, r, j, :], out_offset=None, in_=y_table[:, :],
                                                in_offset=bass.IndirectOffsetOnAxis(ap=idx[:, r, j:j + 1], axis=0)
                                                ).then_inc(gathered[r], 16)

        @block.tensor
        def _(pe):
            pe.sem_inc(flipped, RING)
            pe.sem_inc(biased, RING)
            with pe.Fori(0, TILES // RING) as i:
                for r in range(RING):
                    pe.wait_ge(cw_ready, i * RING + (r + 1))
                    pe.wait_ge(cw_back, i * RING + bank_free(r))
                    pe.transpose(ps[0:e, bank(r), 0:P], cw[:, r, :], k.ident[:]).then_inc(flipped, 1)
                for r in range(RING):
                    pe.wait_ge(cw_back, i * RING + (r + 1 + RING))
                    pe.wait_ge(summed, i * RING + bank_free(r))
                    pe.matmul(ps[:, 3 + bank(r), 0:D], cw_t[:, r, :], moe.b2_sb[:], start=True, stop=True).then_inc(biased, 1)

        @block.vector
        def _(dve):
            dve.sem_inc(summed, RING)
            link = Chain(dve, chain)
            if add_norm:
                dve.tensor_tensor(shift[:], k.mean[:], k.rstd[:], ALU.mult).then_inc(shift_ready, 1)
                dve.wait_ge(shift_ready, 1)
                dve.tensor_scalar(shift[:], shift[:], -1.0, None, ALU.mult).then_inc(shift_ready, 1)
            for i in link.loop(TILES // RING, RING * 2):
                for r in range(RING):
                    t = bass.ds(i * RING + r, 1)
                    base = xn[:, r, :] if add_norm else k.x[:, t, :]
                    if add_norm:
                        dve.wait_ge(xn_ready, i * RING + (r + 1))
                    dve.wait_ge(biased, i * RING + (r + 1 + RING))
                    link(dve.tensor_tensor(part[:, r, :], base, ps[:, 3 + bank(r), 0:D], ALU.add))
                    dve.wait_ge(gathered[r], i * 32 + 32)
                    w = [weight[:, bass.ds((i * RING + r) * 2 + j, 1)] for j in range(2)]
                    link(dve.scalar_tensor_tensor(part[:, r, :], got[:, r, 0, :], w[0], part[:, r, :], ALU.mult, ALU.add))
                    dve.scalar_tensor_tensor(result[:, t, :], got[:, r, 1, :], w[1], part[:, r, :],
                                             ALU.mult, ALU.add).then_inc(summed, 1)


def add_scaled_norm(k, y):
    nc = k.nc
    ctx, sem, sb = phase(k, "scaled_norm")
    with ctx:
        chain = sem("chain")
        block = ctx.enter_context(nc.Block())

        @block.vector
        def _(dve):
            dve.wait_ge(k.gamma_loaded, 16)
            link = Chain(dve, chain)
            gamma_row = k.gamma[:].unsqueeze(1)
            for i in link.loop(TILES // RING, 2 * RING):
                tiles = [bass.ds(i * RING + r, 1) for r in range(RING)]
                for t in tiles:
                    link.loose(dve.scalar_tensor_tensor(y[:, t, :], y[:, t, :], k.mean[:, t], gamma_row,
                                                        ALU.subtract, ALU.mult))
                for t in tiles:
                    link.loose(dve.scalar_tensor_tensor(k.x[:, t, :], y[:, t, :], k.rstd[:, t], k.x[:, t, :],
                                                        ALU.mult, ALU.add))
            link.settle()


def gat_weights(k, weight, left, right, w_all):
    nc, ps = k.nc, k.ps
    ctx, sem, sb = phase(k, "gat_weights")
    with ctx:
        lr, lr_t, w_t = sb("lr", [2 * HEADS, HD]), sb("lr_t", [HD, 2 * HEADS]), sb("w_t", [HD, 2, P])
        loaded, flipped, back, multiplied, done = (sem(n) for n in ("loaded", "flipped", "back", "multiplied", "done"))
        block = ctx.enter_context(nc.Block())

        @block.sync
        def _(sp):
            sp.dma_start(w_all[:, :, 0:HD], weight.rearrange("(k p) n -> p k n", p=P)).then_inc(loaded, 16)
            sp.dma_start(lr[0:HEADS, :], right[:, :]).then_inc(loaded, 16)
            sp.dma_start(lr[HEADS:2 * HEADS, :], left[:, :]).then_inc(loaded, 16)

        @block.tensor
        def _(pe):
            pe.wait_ge(loaded, 48)
            pe.transpose(ps[0:HD, 0, 0:2 * HEADS], lr[:, :], k.ident[0:2 * HEADS, 0:2 * HEADS])
            for half in range(2):
                last = pe.transpose(ps[0:HD, 1, half * P:(half + 1) * P], w_all[:, half, 0:HD], k.ident[:])
            last.then_inc(flipped, 1)
            pe.wait_ge(back, 2)
            for half in range(2):
                last = pe.matmul(ps[:, 2, half * 8:half * 8 + 8], w_t[:, half, :], lr_t[:], start=True, stop=True)
            last.then_inc(multiplied, 1)

        @block.vector
        def _(dve):
            dve.wait_ge(flipped, 1)
            dve.tensor_copy(lr_t[:], ps[0:HD, 0, 0:2 * HEADS]).then_inc(back, 1)
            dve.tensor_copy(w_t[:].rearrange("p k n -> p (k n)"), ps[0:HD, 1, 0:2 * P]).then_inc(back, 1)
            dve.wait_ge(multiplied, 1)
            for half in range(2):
                dve.tensor_copy(w_all[:, half, HD:HD + 8], ps[:, 2, half * 8:half * 8 + 8]).then_inc(done, 1)


def gat_sum(k, table, rows, acc, room):
    nc, ps = k.nc, k.ps
    ctx, sem, sb = phase(k, "gat_sum")
    with ctx:
        G, Q, W = 8, 4, HEADS * HD + HEADS
        idx, msg = sb("idx", [P, Q, G], I32), sb("msg", [P, Q, G, GW])
        hot = sb("hot", [P, Q, G, P])
        logit, e = sb("logit", [P, 2, G, HEADS]), sb("e", [P, 2, G, HEADS])
        val = room[:, 0:2 * G * W].rearrange("p (h c n) -> p h c n", h=2, c=G)
        hot_t = room[:, 2 * G * W:2 * G * (W + P)].rearrange("p (h c n) -> p h c n", h=2, c=G)
        idx_ready, issued, hot_ready, flipped, hot_back, scored, z_ready, l_ready, e_ready, val_ready, summed, added = (
            sem(n) for n in ("idx_ready", "issued", "hot_ready", "flipped", "hot_back", "scored", "z_ready", "l_ready",
                             "e_ready", "val_ready", "summed", "added"))
        gathered = [sem(f"gathered{h}") for h in range(Q)]
        turns = EC // (Q * G)
        assert EC % (Q * G) == 0
        block = ctx.enter_context(nc.Block())
        left = ps[:, 2, 0:G * HEADS]
        sums = [ps[:, 3 + c % 4, 0:W] for c in range(G)]

        @block.scalar
        def _(act):
            act.sem_inc(hot_back, 2)

            def keep_indices(i, g):
                act.wait_ge(val_ready, i * Q + (g + 1))
                act.copy(idx[:, g % Q, :], k.dst_slot[:, bass.ds((i * Q + g) * G, G)]).then_inc(idx_ready, 1)

            def keep_flipped(i, g):
                act.wait_ge(scored, i * Q + (g + 1))
                for b in range(2):
                    act.wait_ge(flipped, i * (2 * Q) + (g * 2 + b + 1))
                    act.copy(hot_t[:, g % 2, b * 4:b * 4 + 4, :].rearrange("p c n -> p (c n)"), ps[:, b, :]).then_inc(hot_back, 1)

            def exponent(i, g):
                act.wait_ge(l_ready, i * Q + (g + 1))
                act.activation(e[:, g % 2], logit[:, g % 2], ACT.Exp).then_inc(e_ready, 1)

            for g in range(Q):
                keep_indices(0, g)
            keep_flipped(0, 0)
            exponent(0, 0)
            keep_flipped(0, 1)
            exponent(0, 1)
            keep_flipped(0, 2)
            keep_flipped(0, 3)

            def body(i, g, left):
                if left > Q:
                    keep_indices(i, g + Q)
                if left > 2:
                    exponent(i, g + 2)
                if left > 4:
                    keep_flipped(i, g + 4)

            run(act, turns, Q, body)

        @block.gpsimd
        def _(pool):
            with pool.Fori(0, turns) as i:
                for g in range(Q):
                    pool.wait_ge(idx_ready, i * Q + (g + 1))
                    pool.sem_inc(issued, 1)
                    for c in range(G):
                        pool.indirect_dma_start(out=msg[:, g, c, :], out_offset=None, in_=table[:, :],
                                                in_offset=bass.IndirectOffsetOnAxis(ap=idx[:, g, c:c + 1], axis=0)
                                                ).then_inc(gathered[g], 16)

        @block.tensor
        def _(pe):
            pe.sem_inc(scored, 2)
            pe.sem_inc(summed, 2 * G)

            def flip(i, g):
                for b in range(2):
                    pe.wait_ge(hot_ready, i * (2 * Q) + (g * 2 + b + 1))
                    pe.wait_ge(hot_back, i * (2 * Q) + (g * 2 + b + 1))
                    for c in range(4):
                        last = pe.transpose(ps[:, b, c * P:(c + 1) * P], hot[:, g % Q, b * 4 + c, :], k.ident[:])
                    last.then_inc(flipped, 1)

            def score(i, g, windows):
                pe.wait_ge(z_ready, i * Q + (g + 1))
                for c in range(G):
                    if c % 4 == 0:
                        pe.wait_ge(hot_back, i * (2 * Q) + (g * 2 + c // 4 + 1 + 2))
                    last = pe.matmul(left[:, c * HEADS:(c + 1) * HEADS], hot_t[:, g % 2, c, :],
                                     rows[:, bass.ds(windows[c], 1), HD + HEADS:GW], start=True, stop=True)
                last.then_inc(scored, 1)

            def body(i, g, left):
                pe.wait_ge(val_ready, i * Q + (g + 1 + Q))
                for c in range(G):
                    pe.wait_ge(added, (i * Q + g) * G + (c + 1))
                    pe.matmul(sums[c], hot[:, g, c, :], val[:, g % 2, c, :], start=True, stop=True).then_inc(summed, 1)
                if left > 3:
                    if g % 2 == 0:
                        ahead[:] = owners(k, pe, k.win_src, (i * Q + g + 3) * G, (2 if left > 4 else 1) * G, TILES - 1)
                    score(i, g + 3, ahead[g % 2 * G:(g % 2 + 1) * G])
                if left > 4:
                    flip(i, g + 4)

            ahead = list(owners(k, pe, k.win_src, 0, 2 * G, TILES - 1))
            for g in range(2):
                flip(0, g)
                score(0, g, ahead[g * G:(g + 1) * G])
            flip(0, 2)
            score(0, 2, owners(k, pe, k.win_src, 2 * G, G, TILES - 1))
            flip(0, 3)
            run(pe, turns, Q, body)

        @block.vector
        def _(dve):
            dve.sem_inc(z_ready, 1)
            dve.sem_inc(val_ready, Q)
            dve.sem_inc(added, 4)

            def make_hot(i, g, c):
                made = dve.tensor_scalar(hot[:, g % Q, c, :], k.iota1[:], k.dst_local[:, bass.ds((i * Q + g) * G + c, 1)],
                                         None, ALU.is_equal)
                if c % 4 == 3:
                    made.then_inc(hot_ready, 1)

            def make_logit(i, g):
                h = g % 2
                dve.wait_ge(scored, i * Q + (g + 1 + 2))
                dve.wait_ge(gathered[g % Q], i * (16 * G) + 16 * G * (1 + g // Q))
                dve.tensor_tensor(logit[:, h], left.rearrange("p (c n) -> p c n", n=HEADS),
                                  msg[:, g % Q, :, HD:HD + HEADS], ALU.add).then_inc(z_ready, 1)
                dve.wait_ge(z_ready, i * Q + (g + 1 + 1))
                dve.scalar_tensor_tensor(logit[:, h], logit[:, h], 0.2, logit[:, h], ALU.mult, ALU.max).then_inc(l_ready, 1)

            def make_values(i, g):
                h, wide = g % 2, [P, G, HEADS, HD]
                dve.wait_ge(e_ready, i * Q + (g + 1))
                dve.tensor_copy(val[:, h, :, HEADS * HD:W], e[:, h])
                dve.tensor_tensor(val[:, h, :, 0:HEADS * HD].rearrange("p c (n d) -> p c n d", d=HD),
                                  msg[:, g % Q, :, 0:HD].unsqueeze(2).to_broadcast(wide),
                                  e[:, h].unsqueeze(3).to_broadcast(wide), ALU.mult).then_inc(val_ready, 1)

            def body(i, g, left):
                if left > 2:
                    make_logit(i, g + 2)
                if g % 2 == 0:
                    mine[:] = owners(k, dve, k.win_src, (i * Q + g) * G, 2 * G, TILES - 1)
                for c in range(G):
                    here = acc[:, bass.ds(mine[g % 2 * G + c], 1), :]
                    dve.wait_ge(summed, (i * Q + g) * G + (c + 1 + 2 * G))
                    dve.wait_ge(added, (i * Q + g) * G + (c + 4))
                    dve.tensor_tensor(here, here, sums[c], ALU.add).then_inc(added, 1)
                    if left > 4:
                        make_hot(i, g + 4, c)
                if left > 2:
                    make_values(i, g + 2)

            mine = []
            for g in range(Q):
                for c in range(G):
                    make_hot(0, g, c)
            for g in range(2):
                make_logit(0, g)
                make_values(0, g)
            run(dve, turns, Q, body)


def gat_finish(k, acc, tmp, bias):
    nc = k.nc
    ctx, sem, sb = phase(k, "gat_finish")
    with ctx:
        b, inv = sb("b", [P, HD]), sb("inv", [P, TILES, HEADS])
        loaded, chain, biased, powered, lowered = (sem(n) for n in ("loaded", "chain", "biased", "powered", "lowered"))
        block = ctx.enter_context(nc.Block())
        part = TILES // RING
        pieces = [slice(j * part, (j + 1) * part) for j in range(RING)]
        wide = [P, part, HEADS, HD]

        @block.sync
        def _(sp):
            sp.dma_start(b[:], bias.partition_broadcast(P)).then_inc(loaded, 16)

        @block.gpsimd
        def _(pool):
            for piece in pieces:
                pool.tensor_scalar(k.x[:, piece, :], k.x[:, piece, :], -1.0, None, ALU.add).then_inc(lowered, 1)

        @block.scalar
        def _(act):
            for j, piece in enumerate(pieces):
                act.wait_ge(biased, j + 1)
                act.activation(tmp[:, piece, :], acc[:, piece, 0:D], ACT.Exp).then_inc(powered, 1)

        @block.vector
        def _(dve):
            link = Chain(dve, chain)
            link(dve.tensor_scalar(inv[:], acc[:, :, D:D + HEADS], ROWSUM_EPS, None, ALU.max))
            link(dve.reciprocal(inv[:], inv[:]))
            dve.wait_ge(loaded, 16)
            for piece in pieces:
                v4 = acc[:, piece, 0:D].rearrange("p t (n d) -> p t n d", d=HD)
                link(dve.tensor_tensor(v4, v4, inv[:, piece, :].unsqueeze(3).to_broadcast(wide), ALU.mult))
                dve.tensor_tensor(v4, v4, b[:].unsqueeze(1).unsqueeze(1).to_broadcast(wide), ALU.add).then_inc(biased, 1)
            dve.wait_ge(biased, RING)
            for j, piece in enumerate(pieces):
                x = k.x[:, piece, :]
                dve.wait_ge(lowered, j + 1)
                link(dve.scalar_tensor_tensor(x, acc[:, piece, 0:D], 0.0, x, ALU.max, ALU.add))
                dve.wait_ge(powered, j + 1)
                link(dve.scalar_tensor_tensor(x, tmp[:, piece, :], 1.0, x, ALU.min, ALU.add))


SORT_BUFFERS = 12
SIDE_WIDTH = EC + 4
H_SIZE, ROWS_SIZE, SIDE_SIZE = TILES * (D + 1), TILES * D, SORT_BUFFERS * SIDE_WIDTH
EARLY = min(E0, (E0 * 2048 - H_SIZE - ROWS_SIZE - SIDE_SIZE) // 1024)


def mixture(k, moe, xn_table, y_table, func, softmax_first, result, add_norm, loads, out=None):
    nc = k.nc
    moments(k, moe.name + "_ln", k.x)
    norm_dense(k, moe.name + "_gate", moe.gate, moe.e, moe.score[:], xn_table=xn_table)
    prefetch(k, moe.name + "_rest", loads)
    with ExitStack() as ctx:
        key = ctx.enter_context(nc.sbuf_tensor(moe.name + "_key", [P, TILES, 2], I32))
        node = ctx.enter_context(nc.sbuf_tensor(moe.name + "_node", [P, TILES, 2], I32))
        valid = ctx.enter_context(nc.sbuf_tensor(moe.name + "_valid", [P, TILES, 2], F32))
        local = ctx.enter_context(nc.sbuf_tensor(moe.name + "_local", [P, moe.c], F32))
        choose(k, moe, softmax_first, key[:], node[:], valid[:])
        flat = lambda a: a.rearrange("p t j -> p (t j)")
        with ExitStack() as sort_ctx:
            s = Sort(k, sort_ctx, moe.name, P, PM, moe.e, moe.c, flat(key[:]), flat(node[:]), moe.slot[:, 0:moe.c],
                     local[:], moe.owner[:, 0:moe.c], pos=flat(moe.pos[:]), valid=flat(valid[:]))
            sort_whole(k, s, 5)
    experts(k, moe, xn_table, y_table, func)
    combine(k, moe, y_table, result, add_norm, out)


def build(nc, t, out):
    with ExitStack() as ctx:
        k = allocate(nc, ctx)
        table = nc.dram_tensor("conv_table", (TILES * P, D), F32, kind="Internal").ap()
        end = E0 * 2048
        k.h = k.big[:, end - H_SIZE:end].rearrange("p (t d) -> p t d", d=D + 1)
        k.rows_room = k.big[:, end - H_SIZE - ROWS_SIZE:end - H_SIZE]
        k.rows = k.rows_room.rearrange("p (t d) -> p t d", d=D)
        side_room = k.big[:, end - H_SIZE - ROWS_SIZE - SIDE_SIZE:end - H_SIZE - ROWS_SIZE]
        xn_table = nc.dram_tensor("xn_table", (TILES * P, D), F32, kind="Internal").ap()
        y_table = nc.dram_tensor("y_table", (C0 * P, D), F32, kind="Internal").ap()
        gat_table = nc.dram_tensor("gat_table", (TILES * P, GW), F32, kind="Internal").ap()
        moe0, moe1 = (Moe(k, ctx, f"moe{n}", e, c, *(t[f"L{n}_ffn_{w}"] for w in ("gate_w", "gate_b", *names)))
                      for n, e, c, names in ((0, E0, C0, ("w1", "b1", "w2", "b2")), (1, E1, C1, ("W1", "b1", "W2", "b2"))))
        at = E1 * 2048
        y_all = k.big[:, at:at + TILES * D].rearrange("p (t d) -> p t d", d=D)
        at += TILES * D
        acc = k.big[:, at:at + TILES * (D + HEADS)].rearrange("p (t d) -> p t d", d=D + HEADS)
        at += TILES * (D + HEADS)
        gat_rows = k.big[:, at:at + TILES * GW].rearrange("p (t d) -> p t d", d=GW)
        at += TILES * GW
        w_all = k.big[:, at:at + 2 * GW].rearrange("p (h d) -> p h d", d=GW)
        k.gamma, k.gamma_loaded = k.sb("gamma", [P, D]), ctx.enter_context(nc.semaphore("gamma_loaded"))
        k.beta, k.beta_loaded = k.sb("beta", [P, D]), ctx.enter_context(nc.semaphore("beta_loaded"))
        k.x_loaded = ctx.enter_context(nc.semaphore("x_loaded"))
        jobs = [lambda sp: load_row(sp, k.gamma, t["L0_ffn_gamma"], k.gamma_loaded),
                lambda sp: load_row(sp, k.beta, t["L0_ffn_beta"], k.beta_loaded),
                lambda sp: load_small(k, sp, moe0), lambda sp: load_small(k, sp, moe1),
                lambda sp: load_experts(k, sp, moe0, 0, 0, EARLY)]
        with ExitStack() as side_ctx:
            edge_rooms = [side_ctx.enter_context(nc.sbuf_tensor(n, [P, EM], I32)) for n in ("edge_src", "edge_dst")]
            k.edge_src, k.edge_dst = (a[0:EP, :] for a in edge_rooms)
            side = Sort(k, side_ctx, "src", EP, EM, TILES, EC, k.edge_src[:], k.edge_dst[:], k.dst_slot[:, 0:EC], k.dst_local[:, 0:EC],
                        k.win_src[:], room=side_room, width=SIDE_WIDTH)
            with ExitStack() as main_ctx:
                room = k.big[:, end - H_SIZE - ROWS_SIZE:end]
                k.hist_w = room[:, SORT_BUFFERS * EM:].bitcast(F16)[:, 0:EM * TILES]
                main = Sort(k, main_ctx, "dst", EP, EM, TILES, EC, k.edge_dst[:], k.edge_src[:], k.src_slot[:],
                            k.src_local[:, 0:EC], k.win_dst[:], room=room)
                setup(k, t["x"], t["src"], t["dst"], k.edge_src, k.edge_dst, jobs)
                sort_whole(k, main, 8, other=side, degree=k.deg_out[:], spare=room[:, SORT_BUFFERS * EM + EM * TILES // 2:])
            new = lambda name, shape: side_ctx.enter_context(nc.sbuf_tensor(name, shape, F32))
            conv_w = [new(f"conv_w{n}", [P, 2, D]) for n in range(3)]
            conv_b = [new("conv_b0", [P, D])] + [a[:].bitcast(F32)[:, 0:D] for a in edge_rooms]
            conv_rows = [[], conv_b[0:1], conv_b[1:3]]
            conv_loaded = [ctx.enter_context(nc.semaphore(f"conv_loaded{n}")) for n in range(3)]
            jobs = [lambda sp, n=n: sp.dma_start(conv_w[n][:], t[f"L0_gnn_W{n}"].rearrange("(k p) n -> p k n", p=P)
                                                 ).then_inc(conv_loaded[n], 16) for n in range(3)]
            jobs += [lambda sp, n=n: load_row(sp, conv_b[n], t[f"L0_gnn_b{n}"], conv_loaded[min(n + 1, 2)]) for n in range(3)]
            prefetch(k, "conv_weights", jobs)
            root_degree(k, "root_out", k.deg_out[:])
            moments(k, "ln0", k.x, loaded=k.x_loaded)
            for n in range(3):
                conv_dense(k, n, table, conv_w[n], conv_loaded[n], *conv_rows[n])
                conv_sum(k, n, table, side)
                if n == 0:
                    root_degree(k, "root_in", k.deg_in[:], counts=k.h[:, :, D], places=side)
            finish_sort(k, side)
        conv_finish(k)
        recycle(k)
        mixture(k, moe0, xn_table, y_table, ACT.Relu, False, y_all, True,
                [lambda sp: load_experts(k, sp, moe0, 0, EARLY, E0), lambda sp: load_experts(k, sp, moe0, 1, 0, E0)])
        recycle(k)
        moments(k, "ln_y", y_all, row=(k.beta, k.beta_loaded))
        add_scaled_norm(k, y_all)
        moments(k, "ln2", k.x)
        gat_weights(k, t["L1_gnn_W"], t["L1_gnn_Wl"], t["L1_gnn_Wr"], w_all)
        norm_dense(k, "gat_dense", w_all, GW, gat_rows, table=gat_table, clear=acc)
        gat_sum(k, gat_table, gat_rows, acc, k.big[:, E1 * 2048:E1 * 2048 + TILES * D])
        gat_finish(k, acc, y_all, t["L1_gnn_b"])
        recycle(k)
        mixture(k, moe1, xn_table, y_table, ACT.Gelu, True, k.x[:], False,
                [lambda sp, w=w: load_experts(k, sp, moe1, w, 0, E1) for w in range(2)], out)


def kernel(**inputs):
    import numpy as np
    import concourse.bacc as bacc
    from concourse.bass_utils import run_bass_kernel_spmd

    nc = bacc.Bacc("TRN2", target_bir_lowering=False, num_devices=1)
    arrays, aps = {}, {}
    for name, a in inputs.items():
        a = np.ascontiguousarray(a)
        arrays[f"in_{name}"] = a
        aps[name] = nc.dram_tensor(f"in_{name}", a.shape, mybir.dt.from_np(a.dtype), kind="ExternalInput").ap()
    out = nc.dram_tensor("out_x", (NODES, D), F32, kind="ExternalOutput").ap()
    build(nc, aps, out)
    result = run_bass_kernel_spmd(nc, [arrays], core_ids=[0])
    return result.results[0]["out_x"]
```
